# Optimizing a Trainium2 kernel written in Bass

```python
import numpy as np
import jax
import jax.numpy as jnp

def _softmax(x, axis=-1):
    return jax.nn.softmax(x, axis=axis)

def _gelu(x):
    return jax.nn.gelu(x, approximate=True)

def _silu(x):
    return jax.nn.silu(x)

def _sigmoid(x):
    return jax.nn.sigmoid(x)

def _layernorm(x, axis=-1, eps=1e-05):
    m = jnp.mean(x, axis=axis, keepdims=True)
    v = jnp.var(x, axis=axis, keepdims=True)
    return (x - m) / jnp.sqrt(v + eps)

def _scatter_add(tgt, idx, src, axis=0):
    return tgt.at[idx].add(src)

def _segment_sum(src, seg, n):
    return jax.ops.segment_sum(src, seg, n)
kernel_name = 'mk_seq_postln_d2_jaxref_r8_f10104'

def setup_inputs(seed: int=0):
    np.random.seed(seed)
    _w = jnp.asarray

    def _L0_attn_setup():
        import jax, jax.numpy as jnp
        import numpy as np
        import math
        H = 16
        KV = 8
        D = 128
        HID = 256
        LAYER_IDX = 1
        LAMBDA_INIT = 0.8 - 0.6 * math.exp(-0.3 * LAYER_IDX)
        EPS = 1e-05
        key = jax.random.key(seed)
        ks = jax.random.split(key, 8)
        B, S = (2, 256)
        op_size = H * D + 2 * KV * D
        return {'hidden_states': jax.random.normal(ks[0], (B, S, HID), jnp.float32), 'Wqkv_w': jax.random.normal(ks[1], (op_size, HID), jnp.float32) * 0.02, 'Wqkv_b': jnp.zeros((op_size,), jnp.float32), 'lambda_q1': jax.random.normal(ks[2], (D,), jnp.float32) * 0.1, 'lambda_k1': jax.random.normal(ks[3], (D,), jnp.float32) * 0.1, 'lambda_q2': jax.random.normal(ks[4], (D,), jnp.float32) * 0.1, 'lambda_k2': jax.random.normal(ks[5], (D,), jnp.float32) * 0.1, 'subln_w': jnp.ones((2 * D,), jnp.float32), 'out_w': jax.random.normal(ks[6], (HID, H * D), jnp.float32) * 0.02, 'out_b': jnp.zeros((HID,), jnp.float32)}
    _L0_attn_in = _L0_attn_setup()

    def _L0_ffn_setup():
        import jax, jax.numpy as jnp
        import numpy as np
        B, S, D, H = (4, 256, 256, 1024)

        def fwht(x):
            orig_shape = x.shape
            n = orig_shape[-1]
            x = x.reshape(-1, n)
            h = 1
            while h < n:
                xb = x.reshape(-1, n // (2 * h), 2, h)
                a = xb[:, :, 0, :]
                b = xb[:, :, 1, :]
                x = jnp.stack([a + b, a - b], axis=2).reshape(-1, n)
                h *= 2
            scale = jnp.asarray(1.0 / np.sqrt(n), dtype=x.dtype)
            return (x * scale).reshape(orig_shape)
        key = jax.random.key(seed)
        kx, k1, k2, k3 = jax.random.split(key, 4)
        x = jax.random.normal(kx, (B, S, D), dtype=jnp.float32)
        W1 = jax.random.normal(k1, (H, D), dtype=jnp.float32) * (1.0 / np.sqrt(D))
        W2 = jax.random.normal(k2, (D, H), dtype=jnp.float32) * (1.0 / np.sqrt(H))
        W3 = jax.random.normal(k3, (H, D), dtype=jnp.float32) * (1.0 / np.sqrt(D))
        return {'x': x, 'W1': W1, 'W2': W2, 'W3': W3}
    _L0_ffn_in = _L0_ffn_setup()

    def _L1_attn_setup():
        import math
        import jax, jax.numpy as jnp
        import numpy as np
        NUM_HEAD = 16
        EMB = 256
        HEAD_DIM = EMB // NUM_HEAD
        B, T = (2, 256)

        def get_slopes(n):
            start = 2 ** (-2 ** (-(math.log2(n) - 3)))
            return np.array([start * start ** i for i in range(n)], dtype=np.float32)
        key = jax.random.key(seed)
        ks = jax.random.split(key, 5)
        x = jax.random.normal(ks[0], (B, T, EMB), jnp.float32)

        def w(k, scale=0.02):
            return jax.random.normal(k, (EMB, EMB), jnp.float32) * scale
        return {'x': x, 'Wq': w(ks[1]), 'bq': jnp.zeros((EMB,), jnp.float32), 'Wk': w(ks[2]), 'bk': jnp.zeros((EMB,), jnp.float32), 'Wv': w(ks[3]), 'bv': jnp.zeros((EMB,), jnp.float32), 'Wo': w(ks[4], scale=0.02 / math.sqrt(24)), 'bo': jnp.zeros((EMB,), jnp.float32)}
    _L1_attn_in = _L1_attn_setup()

    def _L1_ffn_setup():
        import jax, jax.numpy as jnp
        import numpy as np
        B, S, D = (2, 256, 256)
        E = 8
        TOPK = 2
        H_SHARED = 1024
        H_ROUTED = 128
        STD = 0.02
        key = jax.random.key(seed)
        ks = jax.random.split(key, 7)
        return {'x': jax.random.normal(ks[0], (B, S, D), jnp.float32), 'w12': jax.random.normal(ks[1], (E, 2 * H_ROUTED, D), jnp.float32) * STD, 'w3': jax.random.normal(ks[2], (E, D, H_ROUTED), jnp.float32) * STD, 'router_w': jax.random.normal(ks[3], (E, D), jnp.float32) * STD, 'expert_bias': jnp.zeros((E,), jnp.float32), 'sw1': jax.random.normal(ks[4], (H_SHARED, D), jnp.float32) * STD, 'sw2': jax.random.normal(ks[5], (H_SHARED, D), jnp.float32) * STD, 'sw3': jax.random.normal(ks[6], (D, H_SHARED), jnp.float32) * STD}
    _L1_ffn_in = _L1_ffn_setup()
    _d = {'L0_attn_hidden_states': _L0_attn_in['hidden_states'], 'L0_attn_Wqkv_w': _L0_attn_in['Wqkv_w'], 'L0_attn_Wqkv_b': _L0_attn_in['Wqkv_b'], 'L0_attn_lambda_q1': _L0_attn_in['lambda_q1'], 'L0_attn_lambda_k1': _L0_attn_in['lambda_k1'], 'L0_attn_lambda_q2': _L0_attn_in['lambda_q2'], 'L0_attn_lambda_k2': _L0_attn_in['lambda_k2'], 'L0_attn_subln_w': _L0_attn_in['subln_w'], 'L0_attn_out_w': _L0_attn_in['out_w'], 'L0_attn_out_b': _L0_attn_in['out_b'], 'L0_ffn_W1': _L0_ffn_in['W1'], 'L0_ffn_W2': _L0_ffn_in['W2'], 'L0_ffn_W3': _L0_ffn_in['W3'], 'L1_attn_Wq': _L1_attn_in['Wq'], 'L1_attn_bq': _L1_attn_in['bq'], 'L1_attn_Wk': _L1_attn_in['Wk'], 'L1_attn_bk': _L1_attn_in['bk'], 'L1_attn_Wv': _L1_attn_in['Wv'], 'L1_attn_bv': _L1_attn_in['bv'], 'L1_attn_Wo': _L1_attn_in['Wo'], 'L1_attn_bo': _L1_attn_in['bo'], 'L1_ffn_w12': _L1_ffn_in['w12'], 'L1_ffn_w3': _L1_ffn_in['w3'], 'L1_ffn_router_w': _L1_ffn_in['router_w'], 'L1_ffn_expert_bias': _L1_ffn_in['expert_bias'], 'L1_ffn_sw1': _L1_ffn_in['sw1'], 'L1_ffn_sw2': _L1_ffn_in['sw2'], 'L1_ffn_sw3': _L1_ffn_in['sw3']}
    _x0 = _d['L0_attn_hidden_states']
    _d['L0_attn_hidden_states'] = jax.random.normal(jax.random.fold_in(jax.random.key(seed), 1), (2, 1024, 256), dtype=_x0.dtype)
    del _x0
    return _d

def reference(L0_attn_hidden_states, L0_attn_Wqkv_w, L0_attn_Wqkv_b, L0_attn_lambda_q1, L0_attn_lambda_k1, L0_attn_lambda_q2, L0_attn_lambda_k2, L0_attn_subln_w, L0_attn_out_w, L0_attn_out_b, L0_ffn_W1, L0_ffn_W2, L0_ffn_W3, L1_attn_Wq, L1_attn_bq, L1_attn_Wk, L1_attn_bk, L1_attn_Wv, L1_attn_bv, L1_attn_Wo, L1_attn_bo, L1_ffn_w12, L1_ffn_w3, L1_ffn_router_w, L1_ffn_expert_bias, L1_ffn_sw1, L1_ffn_sw2, L1_ffn_sw3):

    def _L0_attn_ref(hidden_states, Wqkv_w, Wqkv_b, lambda_q1, lambda_k1, lambda_q2, lambda_k2, subln_w, out_w, out_b):
        import jax, jax.numpy as jnp
        import numpy as np
        import math
        H = 16
        KV = 8
        D = 128
        HID = 256
        LAYER_IDX = 1
        LAMBDA_INIT = 0.8 - 0.6 * math.exp(-0.3 * LAYER_IDX)
        EPS = 1e-05
        B, S, _ = hidden_states.shape
        qkv = hidden_states @ Wqkv_w.T + Wqkv_b
        q, k, v = jnp.split(qkv, [H * D, H * D + KV * D], axis=-1)
        q = q.reshape(B, S, H // 2, 2, D)
        k = k.reshape(B, S, KV // 2, 2, D)
        v = v.reshape(B, S, KV // 2, 2 * D)
        rep = H // KV
        k = jnp.repeat(k, rep, axis=2)
        v = jnp.repeat(v, rep, axis=2)
        scale = D ** (-0.5)
        causal = jnp.tril(jnp.ones((S, S), bool))
        neg = jnp.finfo(jnp.float32).min

        def attn_map(qi, ki):
            s = jnp.einsum('bqhd,bkhd->bhqk', qi, ki) * scale
            s = jnp.where(causal, s, neg)
            return jax.nn.softmax(s, axis=-1)
        p1 = attn_map(q[:, :, :, 0], k[:, :, :, 0])
        p2 = attn_map(q[:, :, :, 1], k[:, :, :, 1])
        lam1 = jnp.exp(jnp.sum(lambda_q1 * lambda_k1))
        lam2 = jnp.exp(jnp.sum(lambda_q2 * lambda_k2))
        lam = lam1 - lam2 + LAMBDA_INIT
        p = p1 - lam * p2
        o = jnp.einsum('bhqk,bkhe->bqhe', p, v)
        rms = jax.lax.rsqrt(jnp.mean(o * o, axis=-1, keepdims=True) + EPS)
        o = o * rms * subln_w
        o = o * (1.0 - LAMBDA_INIT)
        o = o.reshape(B, S, H * D)
        return o @ out_w.T + out_b

    def _L0_ffn_ref(x, W1, W2, W3):
        import jax, jax.numpy as jnp
        import numpy as np
        B, S, D, H = (4, 256, 256, 1024)

        def fwht(x):
            orig_shape = x.shape
            n = orig_shape[-1]
            x = x.reshape(-1, n)
            h = 1
            while h < n:
                xb = x.reshape(-1, n // (2 * h), 2, h)
                a = xb[:, :, 0, :]
                b = xb[:, :, 1, :]
                x = jnp.stack([a + b, a - b], axis=2).reshape(-1, n)
                h *= 2
            scale = jnp.asarray(1.0 / np.sqrt(n), dtype=x.dtype)
            return (x * scale).reshape(orig_shape)
        up_gate = jnp.einsum('bsd,hd->bsh', x, W1)
        up_lin = jnp.einsum('bsd,hd->bsh', x, W3)
        hidden = jax.nn.silu(up_gate) * up_lin
        hidden = fwht(hidden)
        out = jnp.einsum('bsh,dh->bsd', hidden, W2)
        return out

    def _L1_attn_ref(x, Wq, bq, Wk, bk, Wv, bv, Wo, bo):
        import math
        import jax, jax.numpy as jnp
        import numpy as np
        NUM_HEAD = 16
        EMB = 256
        HEAD_DIM = EMB // NUM_HEAD
        B, T = (2, 256)

        def get_slopes(n):
            start = 2 ** (-2 ** (-(math.log2(n) - 3)))
            return np.array([start * start ** i for i in range(n)], dtype=np.float32)
        Bx, Tx, C = x.shape
        slopes = jnp.asarray(get_slopes(NUM_HEAD))

        def split_heads(y):
            return y.reshape(Bx, Tx, NUM_HEAD, HEAD_DIM).transpose(0, 2, 1, 3)
        q = split_heads(x @ Wq + bq)
        k = split_heads(x @ Wk + bk)
        v = split_heads(x @ Wv + bv)
        attn = jnp.einsum('bhqd,bhkd->bhqk', q, k) / jnp.sqrt(jnp.float32(HEAD_DIM))
        alibi = -slopes[:, None, None] * (Tx - 1 - jnp.arange(Tx, dtype=jnp.float32))[None, None, :]
        attn = attn + alibi
        causal = jnp.tril(jnp.ones((Tx, Tx), dtype=bool))[None, None]
        attn = jnp.where(causal, attn, jnp.finfo(jnp.float32).min)
        p = jax.nn.softmax(attn, axis=-1)
        out = jnp.einsum('bhqk,bhkd->bhqd', p, v).transpose(0, 2, 1, 3).reshape(Bx, Tx, C)
        return out @ Wo + bo

    def _L1_ffn_ref(x, w12, w3, router_w, expert_bias, sw1, sw2, sw3):
        import jax, jax.numpy as jnp
        import numpy as np
        B, S, D = (2, 256, 256)
        E = 8
        TOPK = 2
        H_SHARED = 1024
        H_ROUTED = 128
        STD = 0.02
        b, s, d = x.shape
        g = x @ sw1.T
        u = x @ sw2.T
        shared_out = jax.nn.silu(g) * u @ sw3.T
        scores = jax.nn.sigmoid(x @ router_w.T)
        selection_scores = scores + expert_bias
        _, top_idx = jax.lax.top_k(selection_scores, TOPK)
        top_scores = jnp.take_along_axis(scores, top_idx, axis=-1)
        top_scores = top_scores / (top_scores.sum(-1, keepdims=True) + 1e-09)
        flat_x = x.reshape(-1, d)
        T = flat_x.shape[0]
        flat_idx = top_idx.reshape(T, TOPK)
        flat_sc = top_scores.reshape(T, TOPK)
        combine = jnp.zeros((T, E), x.dtype).at[jnp.arange(T)[:, None], flat_idx].add(flat_sc)
        h12 = jnp.einsum('td,ehd->teh', flat_x, w12)
        h1, h2 = jnp.split(h12, 2, axis=-1)
        h = jax.nn.silu(h1) * h2
        out_e = jnp.einsum('teh,edh->ted', h, w3)
        routed_out = jnp.einsum('ted,te->td', out_e, combine).reshape(b, s, d)
        return shared_out + routed_out
    x = L0_attn_hidden_states
    x = _layernorm(x + _L0_attn_ref(x, L0_attn_Wqkv_w, L0_attn_Wqkv_b, L0_attn_lambda_q1, L0_attn_lambda_k1, L0_attn_lambda_q2, L0_attn_lambda_k2, L0_attn_subln_w, L0_attn_out_w, L0_attn_out_b), axis=-1)
    x = _layernorm(x + _L0_ffn_ref(x, L0_ffn_W1, L0_ffn_W2, L0_ffn_W3), axis=-1)
    x = _layernorm(x + _L1_attn_ref(x, L1_attn_Wq, L1_attn_bq, L1_attn_Wk, L1_attn_bk, L1_attn_Wv, L1_attn_bv, L1_attn_Wo, L1_attn_bo), axis=-1)
    x = _layernorm(x + _L1_ffn_ref(x, L1_ffn_w12, L1_ffn_w3, L1_ffn_router_w, L1_ffn_expert_bias, L1_ffn_sw1, L1_ffn_sw2, L1_ffn_sw3), axis=-1)
    return x

_drawn_inputs = setup_inputs


def setup_inputs(seed=0):
    import zlib

    import numpy as np

    out = dict(_drawn_inputs(seed))
    spreads = {'L0_attn_Wqkv_b': (0.0, 0.1),
     'L0_attn_subln_w': (1.0, 0.2),
     'L0_attn_out_b': (0.0, 0.1),
     'L1_attn_bq': (0.0, 0.8),
     'L1_attn_bk': (0.0, 2.0),
     'L1_attn_bv': (0.0, 0.8),
     'L1_attn_bo': (0.0, 0.1),
     'L1_ffn_expert_bias': (0.0, 0.8)}
    factors = {'L0_attn_lambda_q1': 4.586,
     'L0_attn_lambda_k1': 8.0,
     'L0_attn_lambda_q2': 200.0,
     'L0_attn_lambda_k2': 3.009,
     'L1_attn_Wq': 8.0,
     'L1_attn_Wk': 8.0,
     'L1_attn_Wv': 5.286,
     'L1_attn_Wo': 4.31,
     'L1_ffn_w12': 6.304,
     'L1_ffn_w3': 5.985,
     'L1_ffn_router_w': 8.0,
     'L1_ffn_sw1': 5.053,
     'L1_ffn_sw2': 4.94,
     'L1_ffn_sw3': 4.939}
    for name, (base, spread) in spreads.items():
        noise = np.random.default_rng([zlib.crc32(name.encode()), seed]).standard_normal(out[name].shape)
        drawn = base * np.exp(spread * noise) if base else spread * noise
        out[name] = jnp.asarray(drawn.astype(out[name].dtype))
    for name, factor in factors.items():
        out[name] = (out[name] * factor).astype(out[name].dtype)
    return out
```

```python
from contextlib import ExitStack

import numpy as np

import concourse.bass as bass
from concourse import mybir

F32 = mybir.dt.float32
F32R = mybir.dt.float32r
BF16 = mybir.dt.bfloat16
ACT = mybir.ActivationFunctionType
ALU = mybir.AluOpType
AX = mybir.AxisListType

P = 128
B, T, HID = 2, 1024, 256
NT = T // P
KC = HID // P
HALF = 512
EPS = 1e-5

D0 = 128
GROUPS0 = 4
HEADS0 = 8
E0 = 2 * D0
LAMBDA_INIT = float(0.8 - 0.6 * np.exp(-0.3 * 1))
SCALE0 = float(D0 ** -0.5)
PROJ0 = 2 * D0 + 2 * 2 * D0 + E0
UNITS0 = 12
V_STEPS = 4
STEPS0 = 2 * NT

HEADS1, D1 = 16, 16
GROUPS1 = 4
SLOT1 = 64
STEPS1 = NT * 4
SCALE1 = float(D1 ** -0.5)

CH_F0, CH_SHARED, CH_ROUTED = 8, 8, 8
EXPERTS = 8
CHUNKS = CH_F0 + CH_SHARED + CH_ROUTED
QUAD = 4
FFN_COLS = 2 * KC * P + HID


def build(nc, d):
    with ExitStack() as ctx:
        program(nc, d, ctx)


def program(nc, d, ctx):
    def sem(name):
        return ctx.enter_context(nc.semaphore(name))

    def sb(name, shape, dt=F32, scope=ctx):
        return scope.enter_context(nc.sbuf_tensor(name, shape, dt))

    ps = [ctx.enter_context(nc.psum_tensor(f"ps{i}", [P, 2 * HALF], F32)) for i in range(4)]
    ring = [ps[0][:, 0:HALF], ps[0][:, HALF:], ps[1][:, 0:HALF], ps[1][:, HALF:]]
    xt_bank = [ps[2][:, 0:HALF], ps[2][:, HALF:], ps[3][:, 0:HALF], ps[3][:, HALF:]]

    X = sb("X", [P, NT, HID])
    XT_h = sb("XT_h", [P, KC, T], F32R)
    XT_l = sb("XT_l", [P, KC, T], F32R)
    ident = sb("ident", [P, P])
    ident_bf = sb("ident_bf", [P, P], BF16)
    mask_bf = sb("mask_bf", [P, P], BF16)
    rows_bc = sb("rows_bc", [P, 3, HID])
    subln = sb("subln", [P, KC])
    eps_col = sb("eps_col", [P, 1])
    bsel = sb("bsel", [P, 2])
    rbias = sb("rbias", [P, EXPERTS])
    first = sb("first", [P, EXPERTS])
    neglam = sb("neglam", [P, 1])
    Wa_raw = sb("Wa_raw", [P, KC, PROJ0])
    Wa_h = sb("Wa_h", [P, KC, PROJ0], F32R)
    Wa_l = sb("Wa_l", [P, KC, PROJ0], F32R)
    ba = sb("ba", [P, 6])
    bva = sb("bva", [P, E0])
    st = sb("st", [P, NT, 6])
    mv = sb("mv", [P, NT, 2])
    sd = sb("sd", [P, NT])
    rstd = sb("rstd", [P, NT])

    with ExitStack() as s:
        mask_raw = sb("mask_raw", [P, P], F32, s)
        lam_in = sb("lam_in", [P, 4, D0], F32, s)
        lam_prod = sb("lam_prod", [P, 2, D0], F32, s)
        lam_sum = sb("lam_sum", [P, 2], F32, s)
        lam_exp = sb("lam_exp", [P, 2], F32, s)
        hada_raw = sb("hada_raw", [P, P], F32, s)
        hada = sb("hada", [P, P], F32R, s)
        w2a = sb("w2a", [P, CH_F0, HID], F32, s)
        w2b = sb("w2b", [P, CH_F0, HID], F32, s)
        w2_h = sb("w2_h", [P, CH_F0, HID], F32R, s)
        w2_l = sb("w2_l", [P, CH_F0, HID], F32R, s)

    with ExitStack() as s:
        O = sb("O", [P, NT, HEADS0, E0], F32, s)
        ssq = sb("ssq", [P, HEADS0 * NT], F32, s)
        orstd = sb("orstd", [P, HEADS0 * NT], F32, s)
        with ExitStack() as s2:
            V_h = sb("V_h", [P, NT, E0], F32R, s2)
            V_l = sb("V_l", [P, NT, E0], F32R, s2)
            K_h = sb("K_h", [P, 2, T], F32R, s2)
            K_l = sb("K_l", [P, 2, T], F32R, s2)
            Q_h = sb("Q_h", [P, 2, 2, T], F32R, s2)
            Q_l = sb("Q_l", [P, 2, 2, T], F32R, s2)
            E1 = [sb(f"E1_{i}", [P, T], F32, s2) for i in range(2)]
            E2 = [sb(f"E2_{i}", [P, T], F32, s2) for i in range(2)]
            PT_h = sb("PT_h", [P, T], F32R, s2)
            PT_l = sb("PT_l", [P, T], F32R, s2)
            sq_junk = ps[3][:, HALF:HALF + E0]
            nmax = sb("nmax", [P, 4, 2], F32, s2)
            lsum = sb("lsum", [P, 4, 2], F32, s2)
            rsum = sb("rsum", [P, 8, 2], F32, s2)
            mixc = sb("mixc", [P, 4], F32, s2)
        with ExitStack() as s2:
            Wo_raw = sb("Wo_raw", [P, 2 * HEADS0, HID], F32, s2)
            Wo_h = sb("Wo_h", [P, 2 * HEADS0, HID], F32R, s2)
            Wo_l = sb("Wo_l", [P, 2 * HEADS0, HID], F32R, s2)
            On = sb("On", [P, HEADS0, E0], F32, s2)
            OT_h = [sb(f"OT_h{i}", [P, 2 * HEADS0, P], F32R, s2) for i in range(2)]
            OT_l = [sb(f"OT_l{i}", [P, 2 * HEADS0, P], F32R, s2) for i in range(2)]

    s = ctx
    Fw_raw = [sb(f"Fw_raw{i}", [P, FFN_COLS], F32, s) for i in range(2)]
    Fw_h = [sb(f"Fw_h{i}", [P, FFN_COLS], F32R, s) for i in range(2)]
    Fw_l = [sb(f"Fw_l{i}", [P, FFN_COLS], F32R, s) for i in range(2)]
    with ExitStack() as s:
        silu_g = [sb(f"silu_g{i}", [P, HALF], F32, s) for i in range(2)]
        comb_bc = [sb(f"comb_bc{i}", [P, NT, P], F32, s) for i in range(2)]
        Hf = [sb(f"Hf{i}", [P, T], F32, s) for i in range(2)]
        H_h = [sb(f"H_h{i}", [P, T], F32R, s) for i in range(2)]
        H_l = [sb(f"H_l{i}", [P, T], F32R, s) for i in range(2)]
        Rw_raw = sb("Rw_raw", [P, KC, P], F32, s)
        Rw_h = sb("Rw_h", [P, KC, P], F32R, s)
        Rw_l = sb("Rw_l", [P, KC, P], F32R, s)
        LG = sb("LG", [P, T], F32, s)
        sc = sb("sc", [P, NT, EXPERTS], F32, s)
        sel = sb("sel", [P, NT, EXPERTS], F32, s)
        ta = sb("ta", [P, NT, EXPERTS], F32, s)
        tb = sb("tb", [P, NT, EXPERTS], F32, s)
        comb_oh = sb("comb_oh", [P, 2, NT, EXPERTS], F32, s)
        comb, oh = comb_oh[:, 0], comb_oh[:, 1]
        tm = sb("tm", [P, NT], F32, s)
        combT = sb("combT", [NT * EXPERTS, P], F32, s)
    with ExitStack() as s:
        Wb_raw = sb("Wb_raw", [P, KC, 4 * P], F32, s)
        Wb_h = sb("Wb_h", [P, KC, 4 * P], F32R, s)
        Wb_l = sb("Wb_l", [P, KC, 4 * P], F32R, s)
        bb = sb("bb", [P, 4], F32, s)
        bbq = sb("bbq", [P, 2], F32, s)
        alibi = sb("alibi", [P, 2, T], F32, s)
        Wv_raw = sb("Wv_raw", [P, 2, KC, HID], F32, s)
        Wv_h = sb("Wv_h", [P, 2, KC, HID], F32R, s)
        Wv_l = sb("Wv_l", [P, 2, KC, HID], F32R, s)
        V1 = sb("V1", [P, NT, HID], F32, s)
        Vs = sb("Vs", [P, NT, 4, 32], F32, s)
        stf = [sb(f"stf{i}", [P, HALF], F32, s) for i in range(2)]
        stz = [sb(f"stz{i}", [P, HALF], F32R, s) for i in range(2)]
        QS = sb("QS", [P, 4, T], F32R, s)
        KS = sb("KS", [P, 2, T], F32R, s)
        E3 = [sb(f"E3_{i}", [P, T], F32, s) for i in range(3)]
        PT1 = [sb(f"PT1_{i}", [P, 4, T], F32, s) for i in range(2)]
        nmax1 = sb("nmax1", [P, 4], F32, s)
        lsum1 = sb("lsum1", [P, STEPS1], F32, s)
        rsum1 = sb("rsum1", [P, STEPS1], F32, s)
        OTs = sb("OTs", [P, T], F32, s)
        O1 = sb("O1", [P, NT, HID], F32, s)
        O1T_h, O1T_l = QS[:, 0:KC], QS[:, KC:2 * KC]

    const_in = sem("const_in")
    x_in = sem("x_in")
    out_done = sem("out_done")
    wa_in = sem("wa_in")
    wo_in = sem("wo_in")
    w2_out = sem("w2_out")
    fw_in = [sem("fw_in0"), sem("fw_in1")]
    wb_in = sem("wb_in")
    wv_in = sem("wv_in")
    rw_in = sem("rw_in")
    combt_out = sem("combt_out")
    comb_in = [sem("comb_in0"), sem("comb_in1")]
    pre_dve = sem("pre_dve")
    pre_act = sem("pre_act")
    pre_pe = sem("pre_pe")
    pre_hi = sem("pre_hi")
    w2_ready = sem("w2_ready")
    z_done = sem("z_done")
    ln_st = sem("ln_st")
    ln_ag = sem("ln_ag")
    ln_sd = sem("ln_sd")
    ln_rs = sem("ln_rs")
    ln_done = sem("ln_done")
    xt_ps = sem("xt_ps")
    xt_hi = sem("xt_hi")
    xt_lo = sem("xt_lo")
    xb_done = sem("xb_done")
    wa_scaled = sem("wa_scaled")
    wa_hi = sem("wa_hi")
    wa_lo = sem("wa_lo")
    pj_mm = sem("pj_mm")
    pj_hi = sem("pj_hi")
    pj_dve = sem("pj_dve")
    v_hi = sem("v_hi")
    v_lo = sem("v_lo")
    s_ready = [sem("s_ready0"), sem("s_ready1")]
    nmax_ready = [sem("nmax_ready0"), sem("nmax_ready1")]
    exp_done = [sem("exp_done0"), sem("exp_done1")]
    rsum_ready = sem("rsum_ready")
    mix_ready = sem("mix_ready")
    mix_scaled = sem("mix_scaled")
    p_ready = sem("p_ready")
    pt_ps = sem("pt_ps")
    pt_hi = sem("pt_hi")
    pt_lo = sem("pt_lo")
    pv_done = sem("pv_done")
    o_done = sem("o_done")
    sq_done = sem("sq_done")
    wo_scaled = sem("wo_scaled")
    wo_hi = sem("wo_hi")
    wo_lo = sem("wo_lo")
    or_dve = sem("or_dve")
    or_act = sem("or_act")
    on_done = sem("on_done")
    ot_ps = sem("ot_ps")
    ot_hi = sem("ot_hi")
    ot_lo = sem("ot_lo")
    y_mm = sem("y_mm")
    y_zero = sem("y_zero")
    fw_hi = sem("fw_hi")
    fw_lo = sem("fw_lo")
    gate_mm = sem("gate_mm")
    up_mm = sem("up_mm")
    silu_done = sem("silu_done")
    gu_used = sem("gu_used")
    hm_done = sem("hm_done")
    h_hi = sem("h_hi")
    h_lo = sem("h_lo")
    down_mm = sem("down_mm")
    rw_hi = sem("rw_hi")
    rw_lo = sem("rw_lo")
    lg_mm = sem("lg_mm")
    lg_copy = sem("lg_copy")
    lg_t = sem("lg_t")
    sig_exp = sem("sig_exp")
    rt_dve = sem("rt_dve")
    ct_ps = sem("ct_ps")
    ct_copy = sem("ct_copy")
    qs_zero = sem("qs_zero")
    wv_hi = sem("wv_hi")
    wv_lo = sem("wv_lo")
    v1_mm = sem("v1_mm")
    v1_done = sem("v1_done")
    vs_done = sem("vs_done")
    wb_hi = sem("wb_hi")
    wb_lo = sem("wb_lo")
    bq_scaled = sem("bq_scaled")
    u_mm = sem("u_mm")
    uk_full = sem("uk_full")
    uq_full = sem("uq_full")
    u_z = sem("u_z")
    u_done = sem("u_done")
    s1_ready = sem("s1_ready")
    nmax1_ready = sem("nmax1_ready")
    exp1_done = sem("exp1_done")
    pt1_ps = sem("pt1_ps")
    pt1_act = sem("pt1_act")
    pt1_dve = sem("pt1_dve")
    pv1_done = sem("pv1_done")
    ots_done = sem("ots_done")
    otb_ps = sem("otb_ps")
    rs1_done = sem("rs1_done")
    o1_done = sem("o1_done")
    o1t_ps = sem("o1t_ps")
    o1t_hi = sem("o1t_hi")
    o1t_lo = sem("o1t_lo")
    y1_mm = sem("y1_mm")

    def pass3(pe, out, a_h, a_l, b_h, b_l, start, stop, **kw):
        nc.tensor.matmul(out, a_h, b_h, start=start, stop=False, **kw)
        nc.tensor.matmul(out, a_h, b_l, start=False, stop=False, **kw)
        return nc.tensor.matmul(out, a_l, b_h, start=False, stop=stop, **kw)

    def tile(i, n=P):
        return slice(i * n, (i + 1) * n)

    def key_span(i):
        w = (i + 1) * P
        return [(a, min(max(w, a + 2 * P), a + HALF)) for a in range(0, w, HALF)]

    def tail0(last):
        u = [("u", i) for i in range(0 if last else UNITS0)]
        return [("t", STEPS0 - 2), *u[0:2], ("v", STEPS0 - 2), *u[2:4], ("t", STEPS0 - 1), *u[4:8],
                ("v", STEPS0 - 1), *u[8:]]

    LN_B = 4 * NT
    UNITS_IT = UNITS0 + NT
    R_B = 20

    block = ctx.enter_context(nc.Block())

    @block.sync
    def _(sp):
        for t, src in ((ident, "ident"), (mask_raw, "mask"), (hada_raw, "hada"), (bsel, "bsel"),
                       (subln, "subln"), (w2a, "w2")):
            sp.dma_start(t[:], d[src]).then_inc(const_in, 16)
        for t, src in ((rows_bc, "rows"), (lam_in, "lam"), (rbias, "rbias"), (first, "first")):
            sp.dma_start(t[:], d[src].partition_broadcast(P)).then_inc(const_in, 16)

        def load_wa(g):
            sp.dma_start(Wa_raw[:], d["wa"][g]).then_inc(wa_in, 16)
            sp.dma_start(ba[:], d["ba"][g]).then_inc(wa_in, 16)
            sp.dma_start(bva[:], d["bva"][g].partition_broadcast(P)).then_inc(wa_in, 16)

        def load_wb(g):
            sp.dma_start(Wb_raw[:], d["wb"][g]).then_inc(wb_in, 16)
            sp.dma_start(bb[:], d["bb"][g]).then_inc(wb_in, 16)
            sp.dma_start(alibi[:], d["alibi"][g]).then_inc(wb_in, 16)

        def load_chunk(b, c, j, down):
            cc = b * CHUNKS + c
            sp.wait_ge(fw_lo, cc + 1)
            sp.dma_start(Fw_raw[j % 2][:, 0:2 * KC * P], d["fa"][c]).then_inc(fw_in[j % 2], 16)
            sp.dma_start(Fw_raw[j % 2][:, 2 * KC * P:], down).then_inc(fw_in[j % 2], 16)

        load_wa(0)
        sp.wait_ge(w2_ready, 4)
        sp.dma_start(d["w2s"].rearrange("c p n -> p c n"), w2b[:]).then_inc(w2_out, 16)
        sp.wait_ge(w2_out, 16)
        with sp.Fori(0, B) as b:
            sp.wait_ge(out_done, 16 * b + 1)
            sp.dma_start(X[:], d["x"][b].rearrange("(t p) n -> p t n", p=P)).then_inc(x_in, 16)
            with sp.Fori(0, GROUPS0) as g:
                it = b * GROUPS0 + g
                sp.wait_ge(wa_lo, it + 1)
                sp.wait_ge(pj_dve, it * UNITS_IT + UNITS_IT)
                load_wa(g + 1)
            sp.wait_ge(sq_done, STEPS0 * GROUPS0 * b + STEPS0 * GROUPS0 + 1)
            for q in range(4):
                sp.dma_start(Wo_raw[:, tile(q, 4), :], d["wo0"][:, tile(q, 4), :]).then_inc(wo_in, 16)
            with sp.Fori(0, CH_F0 // QUAD) as q:
                sp.wait_ge(z_done, LN_B * b + NT)
                for j in range(QUAD):
                    load_chunk(b, q * QUAD + j, j, d["w2s"][q * QUAD + j])
            sp.wait_ge(z_done, LN_B * b + 2 * NT)
            sp.dma_start(Wv_raw[:], d["wvo"]).then_inc(wv_in, 16)
            load_wb(0)
            with sp.Fori(0, GROUPS1) as g:
                sp.wait_ge(wb_lo, b * (GROUPS1 + 1) + g + 1)
                sp.wait_ge(u_done, (b * GROUPS1 + g) * 8 + 8)
                load_wb(g + 1)
            sp.wait_ge(z_done, LN_B * b + 3 * NT)
            sp.dma_start(Rw_raw[:], d["rw"]).then_inc(rw_in, 16)
            with sp.Fori(0, CH_SHARED // QUAD) as q:
                for j in range(QUAD):
                    load_chunk(b, CH_F0 + q * QUAD + j, j, d["fb"][q * QUAD + j])
            sp.wait_ge(ct_copy, b + 1)
            sp.dma_start(d["combs"], combT[:]).then_inc(combt_out, 16)
            with sp.Fori(0, CH_ROUTED // QUAD) as q:
                sp.wait_ge(combt_out, 16 * b + 16)
                for j in range(QUAD):
                    e = q * QUAD + j
                    sp.wait_ge(hm_done, b * EXPERTS + e + 1)
                    src = d["combs"].rearrange("(t e) p -> e t p", e=EXPERTS)[e]
                    sp.dma_start(comb_bc[j % 2][:], src.partition_broadcast(P)).then_inc(comb_in[j % 2], 16)
                    load_chunk(b, CH_F0 + CH_SHARED + e, j, d["fb"][CH_SHARED + e])
            sp.wait_ge(ln_done, LN_B * b + LN_B)
            sp.dma_start(d["out"][b].rearrange("(t p) n -> p t n", p=P), X[:]).then_inc(out_done, 16)
        sp.wait_ge(out_done, 16 * B + 1)

    @block.tensor
    def _(pe):
        def transpose_x(b, k):
            for j in range(NT // 2):
                if k == 0:
                    pe.wait_ge(x_in, 16 * b + 16)
                else:
                    pe.wait_ge(ln_done, LN_B * b + NT * (k - 1) + 2 * j + 2)
                for c in range(KC):
                    for r in range(2):
                        mm = nc.tensor.transpose(xt_bank[j][:, c * 2 * P + r * P:c * 2 * P + (r + 1) * P],
                                                 X[:, 2 * j + r, tile(c)], ident[:])
                mm.then_inc(xt_ps, 1)

        def wait_xt(b, k):
            pe.wait_ge(xt_lo, LN_B // 2 * b + 4 * k + 4)

        def project0(it, u):
            if u == 0:
                pe.wait_ge(wa_lo, it + 1)
            if u < UNITS0:
                if u >= 4:
                    pe.wait_ge(pj_dve, UNITS_IT * it + u - 3)
                w, n = tile(u // 2), tile(u % 2, HALF)
                for c in range(KC):
                    mm = pass3(pe, ring[u % 4], Wa_h[:, c, w], Wa_l[:, c, w], XT_h[:, c, n], XT_l[:, c, n],
                               c == 0, c == KC - 1)
            else:
                t, w = u - UNITS0, slice(UNITS0 // 2 * P, PROJ0)
                if t >= 2:
                    pe.wait_ge(pj_dve, UNITS_IT * it + u - 1)
                for c in range(KC):
                    mm = pass3(pe, ring[u % 2 * 2 + 1][:, 0:E0], XT_h[:, c, tile(t)], XT_l[:, c, tile(t)],
                               Wa_h[:, c, w], Wa_l[:, c, w], c == 0, c == KC - 1)
            mm.then_inc(pj_mm, 1)

        def attn0_group(b, g, last):
            it = b * GROUPS0 + g

            def scores(n):
                h, i = n // NT, n % NT
                if n == 0:
                    pe.wait_ge(pj_dve, UNITS_IT * it + UNITS0)
                if n == V_STEPS:
                    pe.wait_ge(pj_dve, UNITS_IT * it + UNITS_IT)
                for m in range(2):
                    if n >= 1:
                        pe.wait_ge(exp_done[m], STEPS0 * it + n)
                    for a, z in key_span(i):
                        mm = pass3(pe, ps[m][:, a:z], Q_h[:, h, m, tile(i)], Q_l[:, h, m, tile(i)],
                                   K_h[:, m, a:z], K_l[:, m, a:z], True, True)
                    mm = nc.tensor.matmul(ps[m][:, tile(i)], ident_bf[:], mask_bf[:],
                                          start=False, stop=True, skip_group_check=True)
                    mm.then_inc(s_ready[m], 1)

            def weigh_values(n):
                i = n % NT
                if n < NT:
                    pe.wait_ge(v_lo, NT * it + n + 1)
                pe.wait_ge(pt_lo, STEPS0 * it + n + 1)
                if n >= 1:
                    pe.wait_ge(o_done, STEPS0 * it + n)
                for kb in range(i + 1):
                    mm = pass3(pe, ps[3][:, 0:E0], PT_h[:, tile(kb)], PT_l[:, tile(kb)], V_h[:, kb, :], V_l[:, kb, :],
                               kb == 0, kb == i)
                mm.then_inc(pv_done, 1)

            def transpose_p(n):
                pe.wait_ge(p_ready, STEPS0 * it + n + 1)
                if n >= 1:
                    pe.wait_ge(pt_lo, STEPS0 * it + n)
                for kb in range(n % NT + 1):
                    mm = nc.tensor.transpose(ps[2][:, tile(kb)], E1[n % 2][:, tile(kb)], ident[:])
                mm.then_inc(pt_ps, 1)

            for s in range(STEPS0):
                if s >= 2:
                    transpose_p(s - 2)
                scores(s)
                if s < V_STEPS:
                    project0(it, UNITS0 + 2 * s)
                    project0(it, UNITS0 + 2 * s + 1)
                if s >= 2:
                    weigh_values(s - 2)
            for kind, n in tail0(last):
                if kind == "u":
                    if n % 2 == 0 and n < 4:
                        pe.wait_ge(exp_done[n // 2], STEPS0 * it + STEPS0)
                    project0(it + 1, n)
                elif kind == "t":
                    transpose_p(n)
                else:
                    weigh_values(n)

        def attn0_out(b):
            for i in range(NT + 1):
                if i < NT:
                    pe.wait_ge(on_done, NT * b + i + 1)
                    for q in range(4):
                        if i >= 1:
                            pe.wait_ge(ot_lo, 4 * NT * b + 4 * (i - 1) + q + 1)
                        for r in range(4):
                            ch = 4 * q + r
                            mm = nc.tensor.transpose(ring[q][:, tile(r)], On[:, ch // 2, tile(ch % 2)], ident[:])
                        mm.then_inc(ot_ps, 1)
                if i >= 1:
                    t = i - 1
                    pe.wait_ge(ot_lo, 4 * NT * b + 4 * t + 4)
                    if t == 0:
                        pe.wait_ge(wo_lo, 4 * b + 4)
                    if t >= 2:
                        pe.wait_ge(z_done, LN_B * b + t - 1)
                    y = ps[3][:, t % 2 * HALF:t % 2 * HALF + HID]
                    for ch in range(2 * HEADS0):
                        mm = pass3(pe, y, OT_h[t % 2][:, ch, :], OT_l[t % 2][:, ch, :], Wo_h[:, ch, :], Wo_l[:, ch, :],
                                   ch == 0, ch == 2 * HEADS0 - 1)
                    mm.then_inc(y_mm, 1)

        def gate_up(b, c, j):
            cc = b * CHUNKS + c
            pe.wait_ge(fw_lo, cc + 3)
            for h in range(2):
                pe.wait_ge(gu_used, 2 * cc + h + 1)
                for k, ready in ((0, gate_mm), (1, up_mm)):
                    for kc in range(KC):
                        w, n = tile(k * KC + kc), tile(h, HALF)
                        mm = pass3(pe, ps[2 + h][:, tile(k, HALF)], Fw_h[j % 2][:, w], Fw_l[j % 2][:, w],
                                   XT_h[:, kc, n], XT_l[:, kc, n], kc == 0, kc == KC - 1)
                    mm.then_inc(ready, 1)

        def down(b, c, j):
            cc = b * CHUNKS + c
            pe.wait_ge(h_lo, cc + 3)
            w = slice(2 * KC * P, FFN_COLS)
            for t in range(NT):
                mm = pass3(pe, ring[t // 2][:, tile(t % 2, HID)], H_h[j % 2][:, tile(t)], H_l[j % 2][:, tile(t)],
                           Fw_h[j % 2][:, w], Fw_l[j % 2][:, w], False, True, skip_group_check=True)
            mm.then_inc(down_mm, 1)

        def ffn(b, layer, c0, chunks):
            with pe.Fori(0, chunks // QUAD) as q:
                wait_xt(b, 2 * layer + 1)
                for j in range(QUAD + 1):
                    if j < QUAD:
                        gate_up(b, q * QUAD + (c0 + j), j)
                    if j == 1:
                        pe.wait_ge(y_zero, 2 * b + layer + 1)
                    if j >= 1:
                        down(b, q * QUAD + (c0 + j - 1), j - 1)

        def attn1_values(b):
            pe.wait_ge(wv_lo, b + 1)
            wait_xt(b, 2)
            for t in range(NT):
                if t >= 4:
                    pe.wait_ge(v1_done, NT * b + t - 3)
                for c in range(KC):
                    mm = pass3(pe, ring[t % 4][:, 0:HID], XT_h[:, c, tile(t)], XT_l[:, c, tile(t)], Wv_h[:, 0, c, :],
                               Wv_l[:, 0, c, :], c == 0, c == KC - 1)
                mm.then_inc(v1_mm, 1)

        def attn1_group(b, g):
            it = b * GROUPS1 + g
            pe.wait_ge(wb_lo, b * (GROUPS1 + 1) + g + 1)
            pe.wait_ge(v1_done, NT * b + NT)
            for u in range(8):
                if u >= 4:
                    pe.wait_ge(uq_full, 4 * it + u - 3)
                w, n = tile(u // 2), tile(u % 2, HALF)
                for c in range(KC):
                    mm = pass3(pe, ring[u % 4], Wb_h[:, c, w], Wb_l[:, c, w], XT_h[:, c, n], XT_l[:, c, n],
                               c == 0, c == KC - 1)
                mm.then_inc(u_mm, 1)

            def scores(m):
                i, j = m // 4, m % 4
                if m < 2:
                    pe.wait_ge(u_done, 8 * it + 8)
                else:
                    pe.wait_ge(exp1_done, STEPS1 * it + m - 1)
                for a, z in key_span(i):
                    diag = a <= i * P < z
                    mm = nc.tensor.matmul(ps[m % 2][:, a:z], QS[:, j, tile(i)], KS[:, j // 2, a:z],
                                          start=True, stop=True)
                    if diag:
                        mm = nc.tensor.matmul(ps[m % 2][:, tile(i)], ident_bf[:], mask_bf[:], start=False, stop=True,
                                              skip_group_check=True)
                mm.then_inc(s1_ready, 1)

            def taken(m):
                if m % 2 == 0:
                    pe.wait_ge(pt1_act, STEPS1 // 2 * it + m // 2 + 1)
                else:
                    pe.wait_ge(pt1_dve, STEPS1 // 2 * it + m // 2 + 1)

            def transpose_p(m):
                pe.wait_ge(exp1_done, STEPS1 * it + m + 1)
                if m >= 1:
                    taken(m - 1)
                for kb in range(m // 4 + 1):
                    mm = nc.tensor.transpose(ps[2][:, tile(kb)], E3[m % 3][:, tile(kb)], ident[:])
                mm.then_inc(pt1_ps, 1)

            def weigh_values(i):
                taken(4 * i + 2)
                taken(4 * i + 3)
                if i == 0:
                    pe.wait_ge(vs_done, it + 1)
                for kb in range(i + 1):
                    for j in range(4):
                        mm = nc.tensor.matmul(ps[3][32 * j:32 * j + 32, tile(i)], Vs[:, kb, j, :],
                                              PT1[i % 2][:, j, tile(kb)], start=kb == 0, stop=kb == i,
                                              tile_position=(0, 32 * j))
                mm.then_inc(pv1_done, 1)

            for s in range(STEPS1 + 3):
                if s < STEPS1:
                    scores(s)
                if s >= 6 and s % 4 == 2:
                    weigh_values((s - 6) // 4)
                if 0 <= s - 2 < STEPS1:
                    transpose_p(s - 2)
            for r in range(2):
                pe.wait_ge(ots_done, 2 * it + r + 1)
                for t in range(4 * r, 4 * r + 4):
                    mm = nc.tensor.transpose(ps[2][:, tile(t)], OTs[:, tile(t)], ident[:])
                mm.then_inc(otb_ps, 1)

        def attn1_out(b):
            pe.wait_ge(o1_done, NT * GROUPS1 * b + NT * GROUPS1)
            for j in range(NT // 2):
                for c in range(KC):
                    for r in range(2):
                        mm = nc.tensor.transpose(xt_bank[j][:, c * 2 * P + r * P:c * 2 * P + (r + 1) * P],
                                                 O1[:, 2 * j + r, tile(c)], ident[:])
                mm.then_inc(o1t_ps, 1)
            for t in range(NT):
                pe.wait_ge(o1t_lo, 4 * b + t // 2 + 1)
                for c in range(KC):
                    mm = pass3(pe, ring[t // 2][:, tile(t % 2, HID)], O1T_h[:, c, tile(t)], O1T_l[:, c, tile(t)],
                               Wv_h[:, 1, c, :], Wv_l[:, 1, c, :], c == 0, c == KC - 1)
                mm.then_inc(y1_mm, 1)

        def router(b):
            pe.wait_ge(rw_lo, b + 1)
            wait_xt(b, 3)
            for h in range(2):
                for c in range(KC):
                    n = tile(h, HALF)
                    mm = pass3(pe, ps[0][:, n], Rw_h[:, c, :], Rw_l[:, c, :], XT_h[:, c, n], XT_l[:, c, n],
                               c == 0, c == KC - 1)
                mm.then_inc(lg_mm, 1)
            for t in range(NT):
                if t % 4 == 0:
                    pe.wait_ge(lg_copy, 2 * b + t // 4 + 1)
                mm = nc.tensor.transpose(ps[1][:, tile(t)], LG[:, tile(t)], ident[:])
            mm.then_inc(lg_t, 1)
            pe.wait_ge(rt_dve, R_B * b + R_B)
            nc.tensor.transpose(ps[0][:, 0:P], comb_oh[:].rearrange("p a t e -> p (a t e)"),
                                ident[:]).then_inc(ct_ps, 1)

        pe.wait_ge(pre_dve, 13)
        for q in range(4):
            n = tile(q, 2)
            nc.tensor.matmul(ring[q], hada[:], w2_h[:, n, :], start=True, stop=False)
            nc.tensor.matmul(ring[q], hada[:], w2_l[:, n, :], start=False, stop=True).then_inc(pre_pe, 1)
        pe.wait_ge(w2_ready, 4)
        with pe.Fori(0, B) as b:
            transpose_x(b, 0)
            wait_xt(b, 0)
            for u in range(UNITS0):
                project0(b * GROUPS0, u)
            with pe.Fori(0, GROUPS0 - 1) as g:
                attn0_group(b, g, False)
            attn0_group(b, GROUPS0 - 1, True)
            attn0_out(b)
            transpose_x(b, 1)
            ffn(b, 0, 0, CH_F0)
            transpose_x(b, 2)
            attn1_values(b)
            with pe.Fori(0, GROUPS1) as g:
                attn1_group(b, g)
            attn1_out(b)
            transpose_x(b, 3)
            router(b)
            ffn(b, 1, CH_F0, CH_SHARED + CH_ROUTED)

    @block.scalar
    def _(act):
        def x_parts(b, k):
            for j in range(NT // 2):
                act.wait_ge(xt_ps, LN_B // 2 * b + 4 * k + j + 1)
                nc.scalar.activation(XT_h[:, :, tile(j, 2 * P)], xt_bank[j].rearrange("p (c n) -> p c n", c=KC),
                                     ACT.Copy).then_inc(xt_hi, 1)

        def ln_sqrt(b, k):
            act.wait_ge(ln_ag, LN_B * b + NT * k + NT)
            nc.scalar.activation(sd[:], mv[:, :, 1], ACT.Sqrt, bias=eps_col[:]).then_inc(ln_sd, 1)

        def split_wa(it):
            act.wait_ge(wa_in, 48 * it + 48)
            q = slice(2 * D0, UNITS0 // 2 * D0)
            nc.scalar.mul(ba[:, 2:6], ba[:, 2:6], SCALE0)
            nc.scalar.mul(Wa_raw[:, :, q], Wa_raw[:, :, q], SCALE0).then_inc(wa_scaled, 1)
            act.wait_ge(wa_scaled, it + 1)
            nc.scalar.copy(Wa_h[:], Wa_raw[:]).then_inc(wa_hi, 1)

        def take0(it, u):
            if u < UNITS0:
                act.wait_ge(pj_mm, UNITS_IT * it + u + 1)
                dst = K_h[:, u // 2, tile(u % 2, HALF)] if u < 4 else \
                    Q_h[:, (u - 4) // 4, (u - 4) // 2 % 2, tile(u % 2, HALF)]
                nc.scalar.activation(dst, ring[u % 4], ACT.Identity, bias=ba[:, u // 2:u // 2 + 1]).then_inc(pj_hi, 1)

        def attn0_group(b, g, last):
            it = b * GROUPS0 + g

            def high(n):
                w = (n % NT + 1) * P
                act.wait_ge(pt_ps, STEPS0 * it + n + 1)
                nc.scalar.copy(PT_h[:, 0:w], ps[2][:, 0:w]).then_inc(pt_hi, 1)

            def squares(n):
                act.wait_ge(o_done, STEPS0 * it + n + 1)
                act.wait_ge(sq_done, STEPS0 * it + n + 1)
                nc.scalar.activation(sq_junk, O[:, n % NT, bass.ds(g * 2 + n // NT, 1), :], ACT.Square,
                                     accum_out=ssq[:, bass.ds(g * STEPS0 + n, 1)]).then_inc(sq_done, 1)

            for s in range(STEPS0):
                if s >= 2:
                    high(s - 2)
                w = (s % NT + 1) * P
                for m, e in ((0, E1[s % 2]), (1, E2[s % 2])):
                    act.wait_ge(nmax_ready[m], STEPS0 * it + s + 1)
                    nc.scalar.activation(e[:, 0:w], ps[m][:, 0:w], ACT.Exp, bias=nmax[:, s % 4, m:m + 1],
                                         accum_out=lsum[:, s % 4, m:m + 1]).then_inc(exp_done[m], 1)
                if s < V_STEPS:
                    for t in (2 * s, 2 * s + 1):
                        act.wait_ge(pj_dve, UNITS_IT * it + UNITS0 + t + 1)
                        nc.scalar.copy(V_h[:, t, :], O[:, t, bass.ds(g * 2 + 1, 1), :]).then_inc(v_hi, 1)
                if s >= 3:
                    squares(s - 3)
                if s == NT:
                    split_wa(it + 1)
            squares(STEPS0 - 3)
            for kind, n in tail0(last):
                if kind == "u":
                    take0(it + 1, n)
                    if n == 3:
                        squares(STEPS0 - 2)
                elif kind == "t":
                    high(n)
            if last:
                squares(STEPS0 - 2)
            squares(STEPS0 - 1)

        def attn0_out(b):
            act.wait_ge(or_dve, 2 * b + 1)
            nc.scalar.activation(ssq[:], orstd[:], ACT.Sqrt).then_inc(or_act, 1)
            for q in range(4):
                act.wait_ge(wo_scaled, 8 * b + 2 * q + 2)
                nc.scalar.copy(Wo_h[:, tile(q, 4), :], Wo_raw[:, tile(q, 4), :]).then_inc(wo_hi, 1)
            for i in range(NT):
                for q in range(4):
                    act.wait_ge(ot_ps, 4 * NT * b + 4 * i + q + 1)
                    nc.scalar.copy(OT_h[i % 2][:, tile(q, 4), :],
                                   ring[q].rearrange("p (c n) -> p c n", c=4)).then_inc(ot_hi, 1)

        def ffn_split(b, c, j):
            cc = b * CHUNKS + c
            act.wait_ge(fw_in[j % 2], b * (CHUNKS * 16) + (c + (2 - j % 2)) * 16)
            act.wait_ge(down_mm, cc + 1)
            nc.scalar.copy(Fw_h[j % 2][:], Fw_raw[j % 2][:]).then_inc(fw_hi, 1)

        def ffn(b, c0, chunks, routed):
            with act.Fori(0, chunks // QUAD) as q:
                ffn_split(b, q * QUAD + c0, 0)
                for j in range(QUAD):
                    c = q * QUAD + (c0 + j)
                    cc = b * CHUNKS + c
                    if j + 1 < QUAD:
                        ffn_split(b, c + 1, j + 1)
                    for h in range(2):
                        act.wait_ge(gate_mm, 2 * cc + h + 1)
                        act.wait_ge(gu_used, 2 * cc + h + 1)
                        nc.scalar.activation(silu_g[h][:], ps[2 + h][:, 0:HALF], ACT.Silu).then_inc(silu_done, 1)
                    if routed:
                        act.wait_ge(hm_done, b * EXPERTS + (c - (CH_F0 + CH_SHARED)) + 3)
                    else:
                        act.wait_ge(gu_used, 2 * cc + 4)
                    nc.scalar.copy(H_h[j % 2][:], Hf[j % 2][:]).then_inc(h_hi, 1)

        def split_wb(b, s):
            act.wait_ge(wb_in, 48 * ((GROUPS1 + 1) * b + s) + 48)
            nc.scalar.mul(bbq[:], bb[:, 0:2], SCALE1).then_inc(bq_scaled, 1)
            nc.scalar.copy(Wb_h[:], Wb_raw[:]).then_inc(wb_hi, 1)

        def attn1_group(b, g):
            it = b * GROUPS1 + g
            act.wait_ge(bq_scaled, b * (GROUPS1 + 1) + g + 1)
            for u in range(8):
                if u < 4:
                    act.wait_ge(u_mm, 8 * it + u + 1)
                    if u >= 2:
                        act.wait_ge(u_done, 8 * it + u - 1)
                    nc.scalar.activation(stf[u % 2][:], ring[u % 4], ACT.Identity, bias=bbq[:, u // 2:u // 2 + 1],
                                         scale=SCALE1).then_inc(uq_full, 1)
                    act.wait_ge(uq_full, 4 * it + u + 1)
                else:
                    act.wait_ge(uk_full, 4 * it + u - 3)
                nc.scalar.copy(stz[u % 2][:], stf[u % 2][:]).then_inc(u_z, 1)

            def take_o(r):
                act.wait_ge(pv1_done, NT * it + 4 * r + 4)
                nc.scalar.copy(OTs[:, tile(r, HALF)], ps[3][:, tile(r, HALF)]).then_inc(ots_done, 1)

            for s in range(STEPS1 + 3):
                m = s - 3
                if 0 <= m and m % 2 == 0:
                    i, w = m // 4, (m // 4 + 1) * P
                    act.wait_ge(pt1_ps, STEPS1 * it + m + 1)
                    if i >= 2:
                        act.wait_ge(pv1_done, NT * it + i - 1)
                    nc.scalar.copy(PT1[i % 2][:, m % 4, 0:w], ps[2][:, 0:w]).then_inc(pt1_act, 1)
                if s < STEPS1:
                    w = (s // 4 + 1) * P
                    act.wait_ge(nmax1_ready, STEPS1 * it + s + 1)
                    if s >= 3:
                        act.wait_ge(pt1_ps, STEPS1 * it + s - 2)
                    nc.scalar.activation(E3[s % 3][:, 0:w], ps[s % 2][:, 0:w], ACT.Exp, bias=nmax1[:, s % 4:s % 4 + 1],
                                         accum_out=lsum1[:, s:s + 1]).then_inc(exp1_done, 1)
                if s == 20:
                    take_o(0)
                if s == 12:
                    split_wb(b, g + 1)
            take_o(1)

        def attn1_out(b):
            for j in range(NT // 2):
                act.wait_ge(o1t_ps, 4 * b + j + 1)
                nc.scalar.copy(O1T_h[:, :, tile(j, 2 * P)],
                               xt_bank[j].rearrange("p (c n) -> p c n", c=KC)).then_inc(o1t_hi, 1)

        def router(b):
            act.wait_ge(rw_in, 16 * b + 16)
            nc.scalar.copy(Rw_h[:], Rw_raw[:]).then_inc(rw_hi, 1)
            act.wait_ge(lg_t, b + 1)
            nc.scalar.activation(ta[:], ps[1][:].rearrange("p (t n) -> p t n", t=NT)[:, :, 0:EXPERTS], ACT.Exp,
                                 scale=-1.0).then_inc(sig_exp, 1)

        act.wait_ge(pre_dve, 6)
        nc.scalar.activation(lam_exp[:], lam_sum[:], ACT.Exp).then_inc(pre_act, 1)
        for q in range(4):
            act.wait_ge(pre_pe, q + 1)
            nc.scalar.mul(w2b[:, tile(q, 2), :], ring[q].rearrange("p (c n) -> p c n", c=2),
                          float((CH_F0 * P) ** -0.5)).then_inc(w2_ready, 1)
        split_wa(0)
        with act.Fori(0, B) as b:
            x_parts(b, 0)
            for u in range(UNITS0):
                take0(b * GROUPS0, u)
            with act.Fori(0, GROUPS0 - 1) as g:
                attn0_group(b, g, False)
            attn0_group(b, GROUPS0 - 1, True)
            attn0_out(b)
            ln_sqrt(b, 0)
            x_parts(b, 1)
            ffn(b, 0, CH_F0, False)
            ln_sqrt(b, 1)
            x_parts(b, 2)
            act.wait_ge(wv_in, 16 * b + 16)
            nc.scalar.copy(Wv_h[:], Wv_raw[:]).then_inc(wv_hi, 1)
            split_wb(b, 0)
            with act.Fori(0, GROUPS1) as g:
                attn1_group(b, g)
            attn1_out(b)
            ln_sqrt(b, 2)
            x_parts(b, 3)
            router(b)
            ffn(b, CH_F0, CH_SHARED, False)
            ffn(b, CH_F0 + CH_SHARED, CH_ROUTED, True)
            ln_sqrt(b, 3)

    @block.vector
    def _(dve):
        def x_parts(b, k):
            for j in range(NT // 2):
                dve.wait_ge(xt_hi, LN_B // 2 * b + 4 * k + j + 1)
                n = tile(j, 2 * P)
                nc.vector.tensor_tensor(XT_l[:, :, n], xt_bank[j].rearrange("p (c n) -> p c n", c=KC),
                                        XT_h[:, :, n].bitcast(F32), ALU.subtract).then_inc(xt_lo, 1)

        def residual(b, k, t, y):
            nc.vector.tensor_tensor(X[:, t, :], y, X[:, t, :], ALU.add).then_inc(z_done, 1)

        def stats(b, k, t):
            dve.wait_ge(z_done, LN_B * b + NT * k + t + 1)
            nc.vector.bn_stats(st[:, t, :], X[:, t, :]).then_inc(ln_st, 1)

        def layernorm(b, k):
            dve.wait_ge(ln_st, LN_B * b + NT * k + NT)
            dve.nop(nofuse=True)
            for t in range(NT):
                nc.vector.bn_aggr(mv[:, t, :], st[:, t, :]).then_inc(ln_ag, 1)
            dve.wait_ge(ln_sd, 4 * b + k + 1)
            nc.vector.reciprocal(rstd[:], sd[:]).then_inc(ln_rs, 1)
            dve.wait_ge(ln_rs, 4 * b + k + 1)
            for t in range(NT):
                nc.vector.tensor_scalar(X[:, t, :], X[:, t, :], mv[:, t, 0:1], rstd[:, t:t + 1], ALU.subtract,
                                        ALU.mult).then_inc(ln_done, 1)

        def take0(it, u):
            h, l = (K_h, K_l) if u < 4 else (Q_h, Q_l)
            at = (slice(None), u // 2) if u < 4 else (slice(None), (u - 4) // 4, (u - 4) // 2 % 2)
            at += (tile(u % 2, HALF),)
            dve.wait_ge(pj_hi, UNITS0 * it + u + 1)
            nc.vector.scalar_tensor_tensor(out=l[at], in0=ring[u % 4], scalar=ba[:, u // 2:u // 2 + 1],
                                           in1=h[at].bitcast(F32), op0=ALU.add,
                                           op1=ALU.subtract).then_inc(pj_dve, 1)

        def attn0_group(b, g, last):
            it = b * GROUPS0 + g

            def mix(n):
                dve.wait_ge(exp_done[1], STEPS0 * it + n + 1)
                nc.vector.reciprocal(rsum[:, n % 8, :], lsum[:, n % 4, :]).then_inc(rsum_ready, 1)
                dve.wait_ge(rsum_ready, STEPS0 * it + n + 1)
                nc.vector.scalar_tensor_tensor(out=mixc[:, n % 4:n % 4 + 1], in0=rsum[:, n % 8, 1:2],
                                               scalar=lsum[:, n % 4, 0:1], in1=neglam[:], op0=ALU.mult,
                                               op1=ALU.mult).then_inc(mix_ready, 1)

            def low(n):
                w = (n % NT + 1) * P
                dve.wait_ge(pt_hi, STEPS0 * it + n + 1)
                nc.vector.tensor_tensor(PT_l[:, 0:w], ps[2][:, 0:w], PT_h[:, 0:w].bitcast(F32),
                                        ALU.subtract).then_inc(pt_lo, 1)

            def output(n):
                dve.wait_ge(pv_done, STEPS0 * it + n + 1)
                nc.vector.tensor_scalar(O[:, n % NT, bass.ds(g * 2 + n // NT, 1), :],
                                        ps[3][:, 0:E0].unsqueeze(1), rsum[:, n % 8, 0:1], None,
                                        ALU.mult).then_inc(o_done, 1)

            for s in range(STEPS0):
                if s >= 1:
                    mix(s - 1)
                if s >= 2:
                    low(s - 2)
                for m in range(2):
                    dve.wait_ge(s_ready[m], STEPS0 * it + s + 1)
                    nc.vector.tensor_reduce(nmax[:, s % 4, m:m + 1], ps[m][:, 0:(s % NT + 1) * P], AX.X, ALU.max,
                                            negate=True).then_inc(nmax_ready[m], 1)
                if s < V_STEPS:
                    for t in (2 * s, 2 * s + 1):
                        dve.wait_ge(pj_mm, UNITS_IT * it + UNITS0 + t + 1)
                        nc.vector.tensor_tensor(O[:, t, bass.ds(g * 2 + 1, 1), :],
                                                ring[t % 2 * 2 + 1][:, 0:E0].unsqueeze(1), bva[:].unsqueeze(1),
                                                ALU.add).then_inc(pj_dve, 1)
                if s >= 2:
                    output(s - 2)
            mix(STEPS0 - 1)
            for kind, n in tail0(last):
                if kind == "u":
                    take0(it + 1, n)
                elif kind == "t":
                    low(n)
                else:
                    output(n)

        def attn0_out(b):
            dve.wait_ge(sq_done, STEPS0 * GROUPS0 * b + STEPS0 * GROUPS0 + 1)
            nc.vector.tensor_scalar(orstd[:], ssq[:], 1.0 / E0, EPS, ALU.mult, ALU.add).then_inc(or_dve, 1)
            dve.wait_ge(or_act, b + 1)
            nc.vector.reciprocal(orstd[:], ssq[:]).then_inc(or_dve, 1)
            dve.wait_ge(or_dve, 2 * b + 2)

            def normalise(i):
                if i >= 1:
                    dve.wait_ge(ot_ps, 4 * NT * b + 4 * i)
                for h in range(HEADS0):
                    ins = nc.vector.tensor_scalar(On[:, h, :], O[:, i, h, :], orstd[:, h * NT + i:h * NT + i + 1], None,
                                                  ALU.mult)
                ins.then_inc(on_done, 1)

            normalise(0)
            for q in range(4):
                dve.wait_ge(wo_hi, 4 * b + q + 1)
                n = tile(q, 4)
                nc.vector.tensor_tensor(Wo_l[:, n, :], Wo_raw[:, n, :], Wo_h[:, n, :].bitcast(F32),
                                        ALU.subtract).then_inc(wo_lo, 1)
            dve.wait_ge(xb_done, 2 * b + 1)
            for i in range(NT + 1):
                if i < NT:
                    for q in range(4):
                        dve.wait_ge(ot_hi, 4 * NT * b + 4 * i + q + 1)
                        n = tile(q, 4)
                        nc.vector.tensor_tensor(OT_l[i % 2][:, n, :], ring[q].rearrange("p (c n) -> p c n", c=4),
                                                OT_h[i % 2][:, n, :].bitcast(F32), ALU.subtract).then_inc(ot_lo, 1)
                if i + 1 < NT:
                    normalise(i + 1)
                if i >= 1:
                    t = i - 1
                    dve.wait_ge(y_mm, NT * b + t + 1)
                    residual(b, 0, t, ps[3][:, t % 2 * HALF:t % 2 * HALF + HID])
                    if t >= 1:
                        stats(b, 0, t - 1)
            stats(b, 0, NT - 1)

        def ffn(b, layer, c0, chunks, routed):
            if not routed:
                if layer == 1:
                    dve.wait_ge(ct_copy, b + 1)
                for p in ps[0:2]:
                    last = nc.vector.memset(p[:], 0.0)
                last.then_inc(y_zero, 1)
            with dve.Fori(0, chunks // QUAD) as q:
                for j in range(QUAD):
                    c = q * QUAD + (c0 + j)
                    cc = b * CHUNKS + c
                    dve.wait_ge(h_lo, cc + 1)
                    for h in range(2):
                        dve.wait_ge(silu_done, 2 * cc + h + 1)
                        dve.wait_ge(up_mm, 2 * cc + h + 1)
                        nc.vector.tensor_tensor(Hf[j % 2][:, tile(h, HALF)], ps[2 + h][:, HALF:], silu_g[h][:],
                                                ALU.mult).then_inc(gu_used, 1)
                    if routed:
                        dve.wait_ge(gu_used, 2 * cc + 4)
                        dve.wait_ge(comb_in[j % 2],
                                    b * (EXPERTS // 2 * 16) + q * (QUAD // 2 * 16) + (j // 2 * 16 + 16))
                        nc.vector.tensor_tensor(Hf[j % 2][:], Hf[j % 2][:], comb_bc[j % 2][:].rearrange("p t n -> p (t n)"),
                                                ALU.mult).then_inc(hm_done, 1)

        def ffn_out(b, k, c_end):
            dve.wait_ge(down_mm, b * CHUNKS + c_end + 2)
            for t in range(NT):
                residual(b, k, t, ring[t // 2][:, tile(t % 2, HID)])
                if t >= 1:
                    stats(b, k, t - 1)
            stats(b, k, NT - 1)

        def attn1_group(b, g):
            it = b * GROUPS1 + g
            for u in range(8):
                if u == 0:
                    dve.wait_ge(qs_zero, 2 * b + 2)
                if u >= 4:
                    dve.wait_ge(u_done, 8 * it + u - 1)
                    dve.wait_ge(u_mm, 8 * it + u + 1)
                    p = (u - 4) // 2
                    nc.vector.scalar_tensor_tensor(out=stf[u % 2][:], in0=ring[u % 4], scalar=bb[:, u // 2:u // 2 + 1],
                                                   in1=alibi[:, p, tile(u % 2, HALF)], op0=ALU.add,
                                                   op1=ALU.add).then_inc(uk_full, 1)
                dve.wait_ge(u_z, 8 * it + u + 1)

                def stack(dst, rows, k):
                    return nc.vector.scalar_tensor_tensor(out=dst, in0=stz[u % 2][rows, :].bitcast(F32),
                                                          scalar=bsel[rows, k:k + 1], in1=stf[u % 2][rows, :],
                                                          op0=ALU.mult, op1=ALU.add)

                n = tile(u % 2, HALF)
                if u < 4:
                    for r in range(2):
                        rows = tile(r, SLOT1)
                        ins = stack(QS[rows, u // 2 * 2 + r, n], rows, 0)
                else:
                    ins = stack(KS[:, (u - 4) // 2, n], slice(0, P), 1)
                ins.then_inc(u_done, 1)
            for s in range(STEPS1 + 3):
                m = s - 3
                if 0 <= m and m % 2 == 1:
                    i, w = m // 4, (m // 4 + 1) * P
                    dve.wait_ge(pt1_ps, STEPS1 * it + m + 1)
                    if i >= 2:
                        dve.wait_ge(pv1_done, NT * it + i - 1)
                    nc.vector.tensor_copy(PT1[i % 2][:, m % 4, 0:w], ps[2][:, 0:w]).then_inc(pt1_dve, 1)
                if s < STEPS1:
                    dve.wait_ge(s1_ready, STEPS1 * it + s + 1)
                    nc.vector.tensor_reduce(nmax1[:, s % 4:s % 4 + 1], ps[s % 2][:, 0:(s // 4 + 1) * P], AX.X, ALU.max,
                                            negate=True).then_inc(nmax1_ready, 1)
            dve.wait_ge(exp1_done, STEPS1 * it + STEPS1)
            nc.vector.reciprocal(rsum1[:], lsum1[:]).then_inc(rs1_done, 1)
            dve.wait_ge(rs1_done, it + 1)
            for t in range(NT):
                if t % 4 == 0:
                    dve.wait_ge(otb_ps, 2 * it + t // 4 + 1)
                src = ps[2][:, tile(t)].rearrange("p (j e) -> p j e", j=4)[:, :, 0:D1]
                dst = O1[:, t, bass.ds(g * 4 * D1, 4 * D1)].rearrange("p (j e) -> p j e", j=4)
                nc.vector.tensor_tensor(dst, src, rsum1[:, tile(t, 4)].unsqueeze(2).to_broadcast([P, 4, D1]),
                                        ALU.mult).then_inc(o1_done, 1)

        def attn1_out(b):
            for j in range(NT // 2):
                dve.wait_ge(o1t_hi, 4 * b + j + 1)
                n = tile(j, 2 * P)
                nc.vector.tensor_tensor(O1T_l[:, :, n], xt_bank[j].rearrange("p (c n) -> p c n", c=KC),
                                        O1T_h[:, :, n].bitcast(F32), ALU.subtract).then_inc(o1t_lo, 1)
            dve.wait_ge(xb_done, 2 * b + 2)
            for t in range(NT):
                dve.wait_ge(y1_mm, NT * b + t // 2 * 2 + 2)
                residual(b, 2, t, ring[t // 2][:, tile(t % 2, HID)])
                if t >= 1:
                    stats(b, 2, t - 1)
            stats(b, 2, NT - 1)

        def router(b):
            for h in range(2):
                dve.wait_ge(lg_mm, 2 * b + h + 1)
                nc.vector.tensor_copy(LG[:, tile(h, HALF)], ps[0][:, tile(h, HALF)]).then_inc(lg_copy, 1)
            dve.wait_ge(sig_exp, b + 1)
            done = [0]

            def then(ins):
                done[0] += 1
                ins.then_inc(rt_dve, 1)
                dve.wait_ge(rt_dve, R_B * b + done[0])

            def over_e(a):
                return a[:].unsqueeze(2).to_broadcast([P, NT, EXPERTS])

            def over_t(a):
                return a[:].unsqueeze(1).to_broadcast([P, NT, EXPERTS])

            def pick_first_best(vals, tmp, dst):
                then(nc.vector.tensor_reduce(tm[:], vals, AX.X, ALU.max))
                then(nc.vector.tensor_tensor(tmp, vals, over_e(tm), ALU.is_equal))
                then(nc.vector.tensor_tensor(tmp, tmp, over_t(first), ALU.mult))
                then(nc.vector.tensor_reduce(tm[:], tmp, AX.X, ALU.max))
                then(nc.vector.tensor_tensor(dst, tmp, over_e(tm), ALU.is_equal))

            then(nc.vector.tensor_scalar(ta[:], ta[:], 1.0, None, ALU.add))
            then(nc.vector.reciprocal(sc[:], ta[:]))
            then(nc.vector.tensor_tensor(sel[:], sc[:], over_t(rbias), ALU.add))
            pick_first_best(sel[:], ta[:], oh)
            then(nc.vector.scalar_tensor_tensor(out=sel[:], in0=oh, scalar=-1e30, in1=sel[:], op0=ALU.mult,
                                                op1=ALU.add))
            pick_first_best(sel[:], ta[:], tb[:])
            then(nc.vector.tensor_tensor(oh, oh, tb[:], ALU.add))
            then(nc.vector.tensor_tensor(sc[:], sc[:], oh, ALU.mult))
            then(nc.vector.tensor_reduce(tm[:], sc[:], AX.X, ALU.add))
            then(nc.vector.tensor_scalar(tm[:], tm[:], 1e-9, None, ALU.add))
            then(nc.vector.reciprocal(tm[:], tm[:]))
            then(nc.vector.tensor_tensor(comb, sc[:], over_e(tm), ALU.mult))
            assert done[0] == R_B
            dve.wait_ge(ct_ps, b + 1)
            nc.vector.tensor_copy(combT[:], ps[0][0:NT * EXPERTS, 0:P]).then_inc(ct_copy, 1)

        dve.wait_ge(const_in, 160)
        nc.vector.memset(eps_col[:], EPS).then_inc(pre_dve, 1)
        nc.vector.tensor_copy(ident_bf[:], ident[:]).then_inc(pre_dve, 1)
        nc.vector.tensor_copy(mask_bf[:], mask_raw[:]).then_inc(pre_dve, 1)
        nc.vector.tensor_copy(hada[:], hada_raw[:]).then_inc(pre_dve, 1)
        for k in range(2):
            nc.vector.tensor_tensor_reduce(out=lam_prod[:, k, :], in0=lam_in[:, 2 * k, :], in1=lam_in[:, 2 * k + 1, :],
                                           scale=1.0, scalar=0.0, op0=ALU.mult, op1=ALU.add,
                                           accum_out=lam_sum[:, k:k + 1]).then_inc(pre_dve, 1)
        nc.vector.tensor_scalar(subln[:], subln[:], 1.0 - LAMBDA_INIT, None, ALU.mult)
        src, dst = w2a, w2b
        for n, h in enumerate((1, 2, 4)):
            v, o = (a[:].rearrange("p (g r h) n -> p g r (h n)", r=2, h=h) for a in (src, dst))
            nc.vector.tensor_tensor(o[:, :, 0], v[:, :, 0], v[:, :, 1], ALU.add).then_inc(pre_dve, 1)
            nc.vector.tensor_tensor(o[:, :, 1], v[:, :, 0], v[:, :, 1], ALU.subtract).then_inc(pre_dve, 1)
            dve.wait_ge(pre_dve, 8 + 2 * n)
            src, dst = dst, src
        nc.vector.tensor_copy(w2_h[:], src[:]).then_inc(pre_hi, 1)
        dve.wait_ge(pre_hi, 1)
        nc.vector.tensor_tensor(w2_l[:], src[:], w2_h[:].bitcast(F32), ALU.subtract).then_inc(pre_dve, 1)
        dve.wait_ge(pre_act, 1)
        nc.vector.scalar_tensor_tensor(out=neglam[:], in0=lam_exp[:, 1:2], scalar=-LAMBDA_INIT, in1=lam_exp[:, 0:1],
                                       op0=ALU.add, op1=ALU.subtract).then_inc(pre_dve, 1)
        dve.wait_ge(pre_dve, 14)
        with dve.Fori(0, B) as b:
            x_parts(b, 0)
            for u in range(UNITS0):
                take0(b * GROUPS0, u)
            with dve.Fori(0, GROUPS0 - 1) as g:
                attn0_group(b, g, False)
            attn0_group(b, GROUPS0 - 1, True)
            attn0_out(b)
            layernorm(b, 0)
            x_parts(b, 1)
            ffn(b, 0, 0, CH_F0, False)
            ffn_out(b, 1, CH_F0)
            layernorm(b, 1)
            x_parts(b, 2)
            for t in range(NT):
                dve.wait_ge(v1_mm, NT * b + t + 1)
                nc.vector.tensor_tensor(V1[:, t, :], ring[t % 4][:, 0:HID], rows_bc[:, 2, :], ALU.add).then_inc(v1_done, 1)
            with dve.Fori(0, GROUPS1) as g:
                attn1_group(b, g)
            attn1_out(b)
            layernorm(b, 2)
            x_parts(b, 3)
            router(b)
            ffn(b, 1, CH_F0, CH_SHARED, False)
            ffn(b, 1, CH_F0 + CH_SHARED, CH_ROUTED, True)
            ffn_out(b, 3, CHUNKS)
            layernorm(b, 3)

    @block.gpsimd
    def _(pool):
        def low(dst, full, high):
            return nc.gpsimd.tensor_tensor(dst, full, high.bitcast(F32), ALU.subtract)

        def split_wa(it):
            pool.wait_ge(wa_hi, it + 1)
            low(Wa_l[:], Wa_raw[:], Wa_h[:]).then_inc(wa_lo, 1)

        def attn0_group(b, g):
            it = b * GROUPS0 + g
            for n in range(STEPS0):
                if n < V_STEPS:
                    for t in (2 * n, 2 * n + 1):
                        pool.wait_ge(v_hi, NT * it + t + 1)
                        low(V_l[:, t, :].unsqueeze(1), O[:, t, bass.ds(g * 2 + 1, 1), :],
                            V_h[:, t, :].unsqueeze(1)).then_inc(v_lo, 1)
                w = (n % NT + 1) * P
                e1, e2 = E1[n % 2][:, 0:w], E2[n % 2][:, 0:w]
                pool.wait_ge(mix_ready, STEPS0 * it + n + 1)
                pool.nop(nofuse=True)
                nc.gpsimd.tensor_scalar(e2, e2, mixc[:, n % 4:n % 4 + 1], 1.0, ALU.mult,
                                        ALU.mult).then_inc(mix_scaled, 1)
                pool.wait_ge(mix_scaled, STEPS0 * it + n + 1)
                nc.gpsimd.tensor_tensor(e1, e1, e2, ALU.add).then_inc(p_ready, 1)
                if n == NT:
                    split_wa(it + 1)

        def add_bias(b, k, row):
            pool.wait_ge(xt_ps, LN_B // 2 * b + 4 * k + 4)
            nc.gpsimd.tensor_tensor(X[:], X[:], rows_bc[:, row, :].unsqueeze(1).to_broadcast([P, NT, HID]),
                                    ALU.add).then_inc(xb_done, 1)

        def attn0_out(b):
            pool.wait_ge(wo_in, 64 * b + 64)
            pool.nop(nofuse=True)
            for q in range(4):
                for c in range(KC):
                    w = Wo_raw[:, tile(q, 4), :].rearrange("p (h c) n -> p c h n", c=KC)[:, c]
                    nc.gpsimd.tensor_scalar(w, w, subln[:, c:c + 1], 1.0, ALU.mult, ALU.mult).then_inc(wo_scaled, 1)

        def ffn(b, c0, chunks):
            with pool.Fori(0, chunks // QUAD) as q:
                def split(j):
                    pool.wait_ge(fw_hi, b * CHUNKS + q * QUAD + (c0 + j + 1))
                    low(Fw_l[j % 2][:], Fw_raw[j % 2][:], Fw_h[j % 2][:]).then_inc(fw_lo, 1)

                split(0)
                for j in range(QUAD):
                    if j + 1 < QUAD:
                        split(j + 1)
                    pool.wait_ge(h_hi, b * CHUNKS + q * QUAD + (c0 + j + 1))
                    low(H_l[j % 2][:], Hf[j % 2][:], H_h[j % 2][:]).then_inc(h_lo, 1)

        def split_wb(b, s):
            pool.wait_ge(wb_hi, b * (GROUPS1 + 1) + s + 1)
            low(Wb_l[:], Wb_raw[:], Wb_h[:]).then_inc(wb_lo, 1)

        pool.sem_inc(fw_lo, 2)
        pool.sem_inc(h_lo, 2)
        pool.sem_inc(gu_used, 2)
        pool.sem_inc(down_mm, 2)
        pool.sem_inc(hm_done, 2)
        pool.sem_inc(out_done, 1)
        pool.sem_inc(sq_done, 1)
        split_wa(0)
        with pool.Fori(0, B) as b:
            add_bias(b, 0, 0)
            with pool.Fori(0, GROUPS0) as g:
                attn0_group(b, g)
            attn0_out(b)
            ffn(b, 0, CH_F0)
            add_bias(b, 2, 1)
            nc.gpsimd.memset(QS[:].bitcast(F32), 0.0).then_inc(qs_zero, 1)
            nc.gpsimd.memset(Vs[:], 0.0).then_inc(qs_zero, 1)
            pool.wait_ge(wv_hi, b + 1)
            low(Wv_l[:], Wv_raw[:], Wv_h[:]).then_inc(wv_lo, 1)
            split_wb(b, 0)
            with pool.Fori(0, GROUPS1) as g:
                pool.wait_ge(qs_zero, 2 * b + 2)
                pool.wait_ge(v1_done, NT * b + NT)
                it = b * GROUPS1 + g
                pool.wait_ge(uq_full, 4 * it + 1)
                nc.gpsimd.tensor_copy(Vs[:, :, :, 0:D1], V1[:, :, bass.ds(g * 4 * D1, 4 * D1)]
                                      .rearrange("p t (j e) -> p t j e", j=4)).then_inc(vs_done, 1)
                split_wb(b, g + 1)
            pool.wait_ge(rw_in, 16 * b + 16)
            pool.wait_ge(rw_hi, b + 1)
            low(Rw_l[:], Rw_raw[:], Rw_h[:]).then_inc(rw_lo, 1)
            ffn(b, CH_F0, CH_SHARED)
            ffn(b, CH_F0 + CH_SHARED, CH_ROUTED)


def kernel(**inputs):
    import concourse.bacc as bacc
    from concourse.bass_utils import run_bass_kernel_spmd

    f32 = np.float32
    a = {k: np.asarray(v) for k, v in inputs.items()}

    def rows(w):
        return w.T.reshape(-1, P, w.shape[0]).transpose(1, 0, 2)

    w, bias = a["L0_attn_Wqkv_w"], a["L0_attn_Wqkv_b"]
    nq, nk = 2 * HEADS0 * D0, 2 * GROUPS0 * D0
    wa, ba, bva = [], [], []
    for g in [*range(GROUPS0), 0]:
        k, v = slice(nq + g * E0, nq + (g + 1) * E0), slice(nq + nk + g * E0, nq + nk + (g + 1) * E0)
        q = slice(g * 2 * E0, (g + 1) * 2 * E0)
        wa.append(rows(np.concatenate([w[k], w[q], w[v]])))
        ba.append(np.concatenate([bias[k], bias[q]]).reshape(6, P).T)
        bva.append(bias[v])

    wb, bb = [], []
    lo_q, lo_k, ones = slice(D1, 2 * D1), slice(2 * D1, 3 * D1), slice(3 * D1, 3 * D1 + 2)
    for g in [*range(GROUPS1), 0]:
        cols, bcols = np.zeros((HID, 4 * P), f32), np.zeros((4 * P,), f32)
        for s, (wn, bn) in enumerate((("L1_attn_Wq", "L1_attn_bq"), ("L1_attn_Wk", "L1_attn_bk"))):
            for j in range(4):
                src = slice((4 * g + j) * D1, (4 * g + j + 1) * D1)
                at = s * 2 * P + j * SLOT1
                for r in range(3):
                    cols[:, at + r * D1:at + (r + 1) * D1] = a[wn][:, src]
                    bcols[at + r * D1:at + (r + 1) * D1] = a[bn][src]
                if s == 0:
                    bcols[at + ones.start:at + ones.stop] = 1.0 / SCALE1
        wb.append(cols.reshape(KC, P, 4 * P).transpose(1, 0, 2))
        bb.append(bcols.reshape(4, P).T)
    bsel = np.zeros((P, 2), f32)
    slopes_start = 2.0 ** (-2.0 ** -(np.log2(HEADS1) - 3))
    slopes = np.array([slopes_start * slopes_start ** i for i in range(HEADS1)], f32)
    ramp = -slopes[:, None] * (T - 1 - np.arange(T, dtype=f32))[None, :]
    alibi = np.zeros((GROUPS1 + 1, P, 2, T), f32)
    for j in range(2):
        at = j * SLOT1
        bsel[at + lo_q.start:at + lo_q.stop, 0] = -1.0
        bsel[at + lo_k.start:at + lo_k.stop, 1] = -1.0
        bsel[at + ones.start + 1, 1] = -1.0
        for g in range(GROUPS1 + 1):
            for p in range(2):
                alibi[g, at + ones.start:at + ones.stop, p, :] = ramp[(4 * g + 2 * p + j) % HEADS1]

    def chunks(gate, up):
        return [np.concatenate([rows(g).reshape(P, -1), rows(u).reshape(P, -1)], axis=1)
                for g, u in zip(gate.reshape(-1, P, HID), up.reshape(-1, P, HID))]

    w12 = a["L1_ffn_w12"]
    fa = chunks(a["L0_ffn_W1"], a["L0_ffn_W3"]) + chunks(a["L1_ffn_sw1"], a["L1_ffn_sw2"]) \
        + chunks(w12[:, :P].reshape(-1, HID), w12[:, P:].reshape(-1, HID))
    fb = np.concatenate([a["L1_ffn_sw3"].T.reshape(-1, P, HID), a["L1_ffn_w3"].transpose(0, 2, 1)])
    rw = np.zeros((P, KC, P), f32)
    rw[:, :, 0:EXPERTS] = rows(a["L1_ffn_router_w"])
    hada = np.ones((1, 1), f32)
    while hada.shape[0] < P:
        hada = np.block([[hada, hada], [hada, -hada]])

    arrays = {
        "x": a["L0_attn_hidden_states"],
        "wa": np.stack(wa), "ba": np.stack(ba), "bva": np.stack(bva),
        "lam": np.stack([a[f"L0_attn_lambda_{n}"] for n in ("q1", "k1", "q2", "k2")]),
        "subln": a["L0_attn_subln_w"].reshape(KC, P).T,
        "wo0": rows(a["L0_attn_out_w"]),
        "rows": np.stack([a["L0_attn_out_b"], a["L1_attn_bo"], a["L1_attn_bv"]]),
        "w2": rows(a["L0_ffn_W2"]),
        "fa": np.stack(fa), "fb": fb, "rw": rw, "rbias": a["L1_ffn_expert_bias"],
        "wb": np.stack(wb), "bb": np.stack(bb), "bsel": bsel, "alibi": alibi,
        "wvo": np.stack([a[n].reshape(KC, P, HID).transpose(1, 0, 2) for n in ("L1_attn_Wv", "L1_attn_Wo")], axis=1),
        "ident": np.eye(P, dtype=f32),
        "mask": np.triu(np.full((P, P), -1e30, f32), 1),
        "hada": hada.astype(f32),
        "first": np.arange(EXPERTS, 0, -1).astype(f32),
    }
    arrays = {f"in_{k}": np.ascontiguousarray(v) for k, v in arrays.items()}
    nc = bacc.Bacc("TRN2", target_bir_lowering=False, num_devices=1)
    d = {k[3:]: nc.dram_tensor(k, v.shape, F32, kind="ExternalInput").ap() for k, v in arrays.items()}
    d["out"] = nc.dram_tensor("out", (B, T, HID), F32, kind="ExternalOutput").ap()
    d["w2s"] = nc.dram_tensor("w2s", (CH_F0, P, HID), F32, kind="Internal").ap()
    d["combs"] = nc.dram_tensor("combs", (NT * EXPERTS, P), F32, kind="Internal").ap()
    build(nc, d)
    r = run_bass_kernel_spmd(nc, [arrays], core_ids=[0])
    return r.results[0]["out"]
```

```python
from contextlib import ExitStack

import numpy as np

import concourse.bass as bass
from concourse import mybir

F32 = mybir.dt.float32
F32R = mybir.dt.float32r
BF16 = mybir.dt.bfloat16
ACT = mybir.ActivationFunctionType
ALU = mybir.AluOpType
AX = mybir.AxisListType

P = 128
B, T, HID = 2, 1024, 256
NT = T // P
KC = HID // P
HALF = 512
EPS = 1e-5

D0 = 128
GROUPS0 = 4
HEADS0 = 8
E0 = 2 * D0
LAMBDA_INIT = float(0.8 - 0.6 * np.exp(-0.3 * 1))
SCALE0 = float(D0 ** -0.5)
PROJ0 = 2 * D0 + 2 * 2 * D0 + E0
UNITS0 = 12
V_STEPS = 4
STEPS0 = 2 * NT

HEADS1, D1 = 16, 16
GROUPS1 = 4
SLOT1 = 64
PIECES1 = 12
MAX_ROW = 32
SCALE1 = float(D1 ** -0.5)

CH_F0, CH_SHARED, CH_ROUTED = 8, 8, 8
EXPERTS = 8
CHUNKS = CH_F0 + CH_SHARED + CH_ROUTED
QUAD = 4
FFN_COLS = 2 * KC * P + HID


def build(nc, d):
    with ExitStack() as ctx:
        program(nc, d, ctx)


def program(nc, d, ctx):
    def sem(name):
        return ctx.enter_context(nc.semaphore(name))

    def sb(name, shape, dt=F32, scope=ctx):
        return scope.enter_context(nc.sbuf_tensor(name, shape, dt))

    ps = [ctx.enter_context(nc.psum_tensor(f"ps{i}", [P, 2 * HALF], F32)) for i in range(4)]
    ring = [ps[0][:, 0:HALF], ps[0][:, HALF:], ps[1][:, 0:HALF], ps[1][:, HALF:]]
    xt_bank = [ps[2][:, 0:HALF], ps[2][:, HALF:], ps[3][:, 0:HALF], ps[3][:, HALF:]]

    X = sb("X", [P, NT, HID])
    XT_h = sb("XT_h", [P, KC, T], F32R)
    XT_l = sb("XT_l", [P, KC, T], F32R)
    ident = sb("ident", [P, P])
    ident_bf = sb("ident_bf", [P, P], BF16)
    mask_bf = sb("mask_bf", [P, P], BF16)
    rows_bc = sb("rows_bc", [P, 3, HID])
    subln = sb("subln", [P, KC])
    eps_col = sb("eps_col", [P, 1])
    bsel = sb("bsel", [P, 2])
    isum = sb("isum", [P, 32])
    rbias = sb("rbias", [P, EXPERTS])
    first = sb("first", [P, EXPERTS])
    neglam = sb("neglam", [P, 1])
    Wa_raw = sb("Wa_raw", [P, KC, PROJ0])
    Wa_h = sb("Wa_h", [P, KC, PROJ0], F32R)
    Wa_l = sb("Wa_l", [P, KC, PROJ0], F32R)
    ba = sb("ba", [P, 6])
    bva = sb("bva", [P, E0])
    st = sb("st", [P, NT, 6])
    mv = sb("mv", [P, NT, 2])
    sd = sb("sd", [P, NT])
    rstd = sb("rstd", [P, NT])

    with ExitStack() as s:
        mask_raw = sb("mask_raw", [P, P], F32, s)
        lam_in = sb("lam_in", [P, 4, D0], F32, s)
        lam_prod = sb("lam_prod", [P, 2, D0], F32, s)
        lam_sum = sb("lam_sum", [P, 2], F32, s)
        lam_exp = sb("lam_exp", [P, 2], F32, s)
        hada_raw = sb("hada_raw", [P, P], F32, s)
        hada = sb("hada", [P, P], F32R, s)
        w2a = sb("w2a", [P, CH_F0, HID], F32, s)
        w2b = sb("w2b", [P, CH_F0, HID], F32, s)
        w2_h = sb("w2_h", [P, CH_F0, HID], F32R, s)
        w2_l = sb("w2_l", [P, CH_F0, HID], F32R, s)

    with ExitStack() as s:
        O = sb("O", [P, NT, HEADS0, E0], F32, s)
        ssq = sb("ssq", [P, HEADS0 * NT], F32, s)
        orstd = sb("orstd", [P, HEADS0 * NT], F32, s)
        with ExitStack() as s2:
            K_h = sb("K_h", [P, 2, T], F32R, s2)
            K_l = sb("K_l", [P, 2, T], F32R, s2)
            Q_h = sb("Q_h", [P, 2, 2, T], F32R, s2)
            Q_l = sb("Q_l", [P, 2, 2, T], F32R, s2)
            V_h = sb("V_h", [P, NT, E0], F32R, s2)
            V_l = sb("V_l", [P, NT, E0], F32R, s2)
            E1 = [sb(f"E1_{i}", [P, T], F32, s2) for i in range(2)]
            E2 = [sb(f"E2_{i}", [P, T], F32, s2) for i in range(2)]
            PT_h = sb("PT_h", [P, T], F32R, s2)
            PT_l = sb("PT_l", [P, T], F32R, s2)
            sq_junk = ps[3][:, HALF:HALF + E0]
            nmax = sb("nmax", [P, 4, 2], F32, s2)
            lsum = sb("lsum", [P, 4, 2], F32, s2)
            rsum = sb("rsum", [P, 8, 2], F32, s2)
            mixc = sb("mixc", [P, 4], F32, s2)
        with ExitStack() as s2:
            Wo_raw = sb("Wo_raw", [P, 2 * HEADS0, HID], F32, s2)
            Wo_h = sb("Wo_h", [P, 2 * HEADS0, HID], F32R, s2)
            Wo_l = sb("Wo_l", [P, 2 * HEADS0, HID], F32R, s2)
            On = sb("On", [P, HEADS0, E0], F32, s2)
            OT_h = [sb(f"OT_h{i}", [P, 2 * HEADS0, P], F32R, s2) for i in range(2)]
            OT_l = [sb(f"OT_l{i}", [P, 2 * HEADS0, P], F32R, s2) for i in range(2)]

    s = ctx
    Fw_raw = [sb(f"Fw_raw{i}", [P, FFN_COLS], F32, s) for i in range(2)]
    Fw_h = [sb(f"Fw_h{i}", [P, FFN_COLS], F32R, s) for i in range(QUAD)]
    Fw_l = [sb(f"Fw_l{i}", [P, FFN_COLS], F32R, s) for i in range(QUAD)]
    Wb_raw = sb("Wb_raw", [P, KC, 4 * P], F32, s)
    Wb_h = sb("Wb_h", [P, KC, 4 * P], F32R, s)
    Wb_l = sb("Wb_l", [P, KC, 4 * P], F32R, s)
    Wv_raw = sb("Wv_raw", [P, 2, KC, HID], F32, s)
    Wv_h = sb("Wv_h", [P, 2, KC, HID], F32R, s)
    Wv_l = sb("Wv_l", [P, 2, KC, HID], F32R, s)
    with ExitStack() as s:
        silu_g = [sb(f"silu_g{i}", [P, HALF], F32, s) for i in range(2)]
        comb_bc = sb("comb_bc", [P, EXPERTS, NT, P], F32, s)
        Hf = [sb(f"Hf{i}", [P, T], F32, s) for i in range(2)]
        H_h = [sb(f"H_h{i}", [P, T], F32R, s) for i in range(2)]
        H_l = [sb(f"H_l{i}", [P, T], F32R, s) for i in range(2)]
        Rw_raw = sb("Rw_raw", [P, KC, P], F32, s)
        Rw_h = sb("Rw_h", [P, KC, P], F32R, s)
        Rw_l = sb("Rw_l", [P, KC, P], F32R, s)
        LG = sb("LG", [P, T], F32, s)
        sc = sb("sc", [P, NT, EXPERTS], F32, s)
        sel = sb("sel", [P, NT, EXPERTS], F32, s)
        ta = sb("ta", [P, NT, EXPERTS], F32, s)
        tb = sb("tb", [P, NT, EXPERTS], F32, s)
        comb_oh = sb("comb_oh", [P, 2, NT, EXPERTS], F32, s)
        comb, oh = comb_oh[:, 0], comb_oh[:, 1]
        tm = sb("tm", [P, NT], F32, s)
        combT = sb("combT", [NT * EXPERTS, P], F32, s)
        Xn = sb("Xn", [P, NT, HID], F32, s)
    with ExitStack() as s:
        bb = sb("bb", [P, 4], F32, s)
        alibi = sb("alibi", [P, 2, T], F32, s)
        V1 = sb("V1", [P, NT, HID], F32, s)
        Vs = sb("Vs", [P, NT, 4, 32], F32, s)
        st_k = sb("st_k", [P, HALF], F32, s)
        st_q = sb("st_q", [P, HALF], F32, s)
        neg_k = sb("neg_k", [P, HALF], F32R, s)
        neg_q = sb("neg_q", [P, HALF], F32R, s)
        QS = sb("QS", [P, 4, T], F32R, s)
        KS = sb("KS", [P, 2, T], F32R, s)
        PT = sb("PT", [P, PIECES1, HALF], F32, s)
        nmax1 = sb("nmax1", [P, NT], F32, s)
        nmax1_part = sb("nmax1_part", [P, 2, NT // 2], F32, s)
        nmax1_cols = sb("nmax1_cols", [P, NT, P], F32R, s)
        rsum1 = sb("rsum1", [P, NT], F32, s)
        OTs = sb("OTs", [P, T], F32, s)
        O1 = sb("O1", [P, NT, HID], F32, s)
        O1T_h, O1T_l = QS[:, 0:KC], QS[:, KC:2 * KC]

    const_in = sem("const_in")
    w2_in = sem("w2_in")
    x_in = sem("x_in")
    out_done = sem("out_done")
    wa_in = sem("wa_in")
    wo_in = sem("wo_in")
    w2_out = sem("w2_out")
    fw_in = [sem("fw_in0"), sem("fw_in1")]
    wb_in = sem("wb_in")
    wv_in = sem("wv_in")
    rw_in = sem("rw_in")
    combt_out = sem("combt_out")
    comb_in = sem("comb_in")
    pre_dve = sem("pre_dve")
    pre_act = sem("pre_act")
    pre_pe = sem("pre_pe")
    pre_hi = sem("pre_hi")
    w2_ready = sem("w2_ready")
    z_done = sem("z_done")
    ln_st = sem("ln_st")
    ln_ag = sem("ln_ag")
    ln_sd = sem("ln_sd")
    ln_rs = sem("ln_rs")
    ln_done = sem("ln_done")
    xt_ps = sem("xt_ps")
    xt_hi = sem("xt_hi")
    xt_lo = sem("xt_lo")
    xb_done = sem("xb_done")
    wa_scaled = sem("wa_scaled")
    wa_hi = sem("wa_hi")
    wa_lo = sem("wa_lo")
    pj_mm = sem("pj_mm")
    pj_hi = sem("pj_hi")
    pj_dve = sem("pj_dve")
    v_hi = sem("v_hi")
    v_lo = sem("v_lo")
    s_ready = [sem("s_ready0"), sem("s_ready1")]
    nmax_ready = [sem("nmax_ready0"), sem("nmax_ready1")]
    exp_done = [sem("exp_done0"), sem("exp_done1")]
    rsum_ready = sem("rsum_ready")
    mix_ready = sem("mix_ready")
    mix_scaled = sem("mix_scaled")
    p_ready = sem("p_ready")
    pt_ps = sem("pt_ps")
    pt_hi = sem("pt_hi")
    pt_lo = sem("pt_lo")
    pv_done = sem("pv_done")
    o_done = sem("o_done")
    sq_done = sem("sq_done")
    wo_scaled = sem("wo_scaled")
    wo_hi = sem("wo_hi")
    wo_lo = sem("wo_lo")
    or_dve = sem("or_dve")
    or_act = sem("or_act")
    on_done = sem("on_done")
    ot_ps = sem("ot_ps")
    ot_hi = sem("ot_hi")
    ot_lo = sem("ot_lo")
    y_mm = sem("y_mm")
    y_zero = sem("y_zero")
    y_bank = sem("y_bank")
    fw_hi = sem("fw_hi")
    fw_lo = sem("fw_lo")
    gate_mm = sem("gate_mm")
    up_mm = sem("up_mm")
    silu_done = sem("silu_done")
    gu_used = sem("gu_used")
    hm_done = sem("hm_done")
    h_hi = sem("h_hi")
    h_lo = sem("h_lo")
    down_mm = sem("down_mm")
    rw_hi = sem("rw_hi")
    rw_lo = sem("rw_lo")
    lg_mm = sem("lg_mm")
    lg_copy = sem("lg_copy")
    lg_t = sem("lg_t")
    sig_exp = sem("sig_exp")
    rt_dve = sem("rt_dve")
    ct_ps = sem("ct_ps")
    ct_copy = sem("ct_copy")
    qs_zero = sem("qs_zero")
    wv_hi = sem("wv_hi")
    wv_lo = sem("wv_lo")
    v1_mm = sem("v1_mm")
    v1_done = sem("v1_done")
    vs_done = sem("vs_done")
    wb_hi = sem("wb_hi")
    wb_lo = sem("wb_lo")
    bb_in = sem("bb_in")
    u_mm = sem("u_mm")
    uk_full = sem("uk_full")
    uq_full = sem("uq_full")
    uk_neg = sem("uk_neg")
    uq_neg = sem("uq_neg")
    ks_done = sem("ks_done")
    qs_done = sem("qs_done")
    o_zero = sem("o_zero")
    a_ready = sem("a_ready")
    a_used = sem("a_used")
    nm_both = sem("nm_both")
    nm_hi = sem("nm_hi")
    nm_lo = sem("nm_lo")
    nt_ps = sem("nt_ps")
    n_done = sem("n_done")
    t_ready = sem("t_ready")
    t_used = sem("t_used")
    pv1_done = sem("pv1_done")
    ots_done = [sem("ots_done0"), sem("ots_done1")]
    o_ps = sem("o_ps")
    rs1_done = sem("rs1_done")
    o1_done = sem("o1_done")
    o1t_ps = sem("o1t_ps")
    o1t_hi = sem("o1t_hi")
    o1t_lo = sem("o1t_lo")
    y1_mm = sem("y1_mm")

    def pass3(pe, out, a_h, a_l, b_h, b_l, start, stop, **kw):
        nc.tensor.matmul(out, a_h, b_h, start=start, stop=False, **kw)
        nc.tensor.matmul(out, a_h, b_l, start=False, stop=False, **kw)
        return nc.tensor.matmul(out, a_l, b_h, start=False, stop=stop, **kw)

    def tile(i, n=P):
        return slice(i * n, (i + 1) * n)

    def key_span(i):
        w = (i + 1) * P
        return [(a, min(max(w, a + 2 * P), a + HALF)) for a in range(0, w, HALF)]

    def tail0(last):
        u = [("u", i) for i in range(0 if last else UNITS0)]
        return [("t", STEPS0 - 2), *u[0:2], ("v", STEPS0 - 2), *u[2:4], ("t", STEPS0 - 1), *u[4:8],
                ("v", STEPS0 - 1), *u[8:]]

    def slot1(j, last):
        order = """t0 a0 uk0 t1 a1 uq0 t2 a2 zk0 t3 a3 zq0 n1 o0 uk1 t4 a4 t5 a5 uq1 v0 zk1 c0 t6 a6 zq1 n0 t7 a7
                   t8 a8 t9 a9 v1 t10 t11 a10 a11 v2 c1""".split()
        tokens = [(x.rstrip("0123456789"), int(x.lstrip("abcdefghijklmnopqrstuvwxyz"))) for x in order]
        dropped = set()
        if last and j == 3:
            dropped |= {("a", k) for k in range(PIECES1)} | {("n", 0)}
        if j % 2 == 1 or (last and j == 2):
            dropped |= {(k, h) for k in ("uk", "uq", "zk", "zq") for h in range(2)}
        if j == 0:
            dropped |= {("o", 0)}
        return [t for t in tokens if t not in dropped] + ([("end", 0)] if j == 3 else [])

    STACK1 = [("uk", 0), ("uq", 0), ("zk", 0), ("uk", 1), ("zq", 0), ("uq", 1), ("zk", 1), ("zq", 1)]
    MAXIMA1 = [("a", k) for k in range(8)] + [("n", 0)] + [("a", k) for k in range(8, PIECES1)]

    def quads(eng, n, body):
        if n > 2:
            with eng.Fori(0, n - 1) as q:
                body(q, False)
        else:
            body(0, False)
        body(n - 1, True)

    def a_piece(k):
        i, a = (k, 0) if k < 4 else (4 + (k - 4) // 2, (k - 4) % 2 * HALF)
        z = min((i + 1) * P, a + HALF)
        return i, a, z, max(z, a + 2 * P)

    def t_piece(k):
        kb = k % 4 + (4 if k >= 8 else 0)
        half = 0 if k < 4 else HALF
        return kb, max(half, kb * P), half + HALF

    LN_B = 4 * NT
    UNITS_IT = UNITS0 + NT
    R_B = 20
    CONSTS = 9

    block = ctx.enter_context(nc.Block())

    @block.sync
    def _(sp):
        def load_wa(g):
            sp.dma_start(Wa_raw[:], d["wa"][g]).then_inc(wa_in, 16)
            sp.dma_start(ba[:], d["ba"][g]).then_inc(wa_in, 16)
            sp.dma_start(bva[:], d["bva"][g].partition_broadcast(P)).then_inc(wa_in, 16)

        def load_wb(g):
            sp.dma_start(Wb_raw[:], d["wb"][g]).then_inc(wb_in, 16)

        def load_bb(g):
            sp.dma_start(bb[:], d["bb"][g]).then_inc(bb_in, 16)
            sp.dma_start(alibi[:], d["alibi"][g]).then_inc(bb_in, 16)

        def load_chunk(b, c, j, down):
            cc = b * CHUNKS + c
            sp.wait_ge(fw_lo, cc + 1)
            sp.dma_start(Fw_raw[j % 2][:, 0:2 * KC * P], d["fa"][c]).then_inc(fw_in[j % 2], 16)
            sp.dma_start(Fw_raw[j % 2][:, 2 * KC * P:], down).then_inc(fw_in[j % 2], 16)

        def load_x(b):
            sp.dma_start(Xn[:], d["x"][b].rearrange("(t p) n -> p t n", p=P)).then_inc(x_in, 16)

        sp.dma_start(w2a[:], d["w2"]).then_inc(w2_in, 16)
        sp.dma_start(hada_raw[:], d["hada"]).then_inc(w2_in, 16)
        load_x(0)
        for t, src in ((ident, "ident"), (mask_raw, "mask"), (bsel, "bsel"), (isum, "isum"),
                       (subln, "subln")):
            sp.dma_start(t[:], d[src]).then_inc(const_in, 16)
        for t, src in ((rows_bc, "rows"), (lam_in, "lam"), (rbias, "rbias"), (first, "first")):
            sp.dma_start(t[:], d[src].partition_broadcast(P)).then_inc(const_in, 16)
        load_wa(0)
        sp.wait_ge(w2_ready, 4)
        sp.dma_start(d["w2s"].rearrange("c p n -> p c n"), w2b[:]).then_inc(w2_out, 16)
        sp.wait_ge(w2_out, 16)
        with sp.Fori(0, B) as b:
            with sp.Fori(0, GROUPS0) as g:
                it = b * GROUPS0 + g
                sp.wait_ge(wa_lo, it + 1)
                sp.wait_ge(pj_dve, it * UNITS_IT + UNITS_IT)
                load_wa(g + 1)
            sp.wait_ge(sq_done, STEPS0 * GROUPS0 * b + STEPS0 * GROUPS0 + 1)
            for q in range(4):
                sp.dma_start(Wo_raw[:, tile(q, 4), :], d["wo0"][:, tile(q, 4), :]).then_inc(wo_in, 16)
            with sp.Fori(0, CH_F0 // QUAD) as q:
                sp.wait_ge(z_done, LN_B * b + NT)
                for j in range(QUAD):
                    load_chunk(b, q * QUAD + j, j, d["w2s"][q * QUAD + j])
            sp.dma_start(Wv_raw[:], d["wvo"]).then_inc(wv_in, 16)
            load_wb(0)
            sp.wait_ge(z_done, LN_B * b + 2 * NT)
            load_bb(0)
            with sp.Fori(0, GROUPS1 - 1) as g:
                it = b * GROUPS1 + g
                sp.wait_ge(wb_lo, it + 1)
                load_wb(g + 1)
                sp.wait_ge(uk_full, 4 * it + 4)
                sp.wait_ge(uq_full, 4 * it + 4)
                load_bb(g + 1)
            sp.wait_ge(z_done, LN_B * b + 3 * NT)
            sp.dma_start(Rw_raw[:], d["rw"]).then_inc(rw_in, 16)
            load_x(B - 1)
            for c in range(CH_SHARED):
                if c == QUAD:
                    sp.wait_ge(ct_copy, b + 1)
                    sp.dma_start(d["combs"], combT[:]).then_inc(combt_out, 16)
                    sp.wait_ge(combt_out, 16 * b + 16)
                    for e in range(EXPERTS):
                        src = d["combs"].rearrange("(t e) p -> e t p", e=EXPERTS)[e]
                        sp.dma_start(comb_bc[:, e], src.partition_broadcast(P)).then_inc(comb_in, 16)
                load_chunk(b, CH_F0 + c, c, d["fb"][c])
            with sp.Fori(0, CH_ROUTED // QUAD) as q:
                for j in range(QUAD):
                    e = q * QUAD + j
                    load_chunk(b, CH_F0 + CH_SHARED + e, j, d["fb"][CH_SHARED + e])
            sp.wait_ge(ln_done, LN_B * b + LN_B)
            sp.dma_start(d["out"][b].rearrange("(t p) n -> p t n", p=P), X[:]).then_inc(out_done, 16)
        sp.wait_ge(out_done, 16 * B + 1)

    @block.tensor
    def _(pe):
        def transpose_x(b, k):
            for j in range(NT // 2):
                if k == 0:
                    pe.wait_ge(const_in, CONSTS * 16)
                    pe.wait_ge(x_in, 16 * b + 16)
                    pe.wait_ge(gu_used, 2 * CHUNKS * b + 2)
                else:
                    pe.wait_ge(ln_done, LN_B * b + NT * (k - 1) + 2 * j + 2)
                for c in range(KC):
                    for r in range(2):
                        mm = nc.tensor.transpose(xt_bank[j][:, c * 2 * P + r * P:c * 2 * P + (r + 1) * P],
                                                 (X if k else Xn)[:, 2 * j + r, tile(c)], ident[:])
                mm.then_inc(xt_ps, 1)

        def wait_xt(b, k):
            pe.wait_ge(xt_lo, LN_B // 2 * b + 4 * k + 4)

        def project0(it, u):
            if u == 0:
                pe.wait_ge(wa_lo, it + 1)
            if u < UNITS0:
                if u >= 4:
                    pe.wait_ge(pj_dve, UNITS_IT * it + u - 3)
                w, n = tile(u // 2), tile(u % 2, HALF)
                for c in range(KC):
                    mm = pass3(pe, ring[u % 4], Wa_h[:, c, w], Wa_l[:, c, w], XT_h[:, c, n], XT_l[:, c, n],
                               c == 0, c == KC - 1)
            else:
                t, w = u - UNITS0, slice(UNITS0 // 2 * P, PROJ0)
                if t >= 2:
                    pe.wait_ge(pj_dve, UNITS_IT * it + u - 1)
                for c in range(KC):
                    mm = pass3(pe, ring[u % 2 * 2 + 1][:, 0:E0], XT_h[:, c, tile(t)], XT_l[:, c, tile(t)],
                               Wa_h[:, c, w], Wa_l[:, c, w], c == 0, c == KC - 1)
            mm.then_inc(pj_mm, 1)

        def attn0_group(b, g, last):
            it = b * GROUPS0 + g

            def scores(n):
                h, i = n // NT, n % NT
                if n == 0:
                    pe.wait_ge(pj_dve, UNITS_IT * it + UNITS0)
                if n == V_STEPS:
                    pe.wait_ge(pj_dve, UNITS_IT * it + UNITS_IT)
                for m in range(2):
                    if n >= 1:
                        pe.wait_ge(exp_done[m], STEPS0 * it + n)
                    for a, z in key_span(i):
                        mm = pass3(pe, ps[m][:, a:z], Q_h[:, h, m, tile(i)], Q_l[:, h, m, tile(i)],
                                   K_h[:, m, a:z], K_l[:, m, a:z], True, True)
                    mm = nc.tensor.matmul(ps[m][:, tile(i)], ident_bf[:], mask_bf[:],
                                          start=False, stop=True, skip_group_check=True)
                    mm.then_inc(s_ready[m], 1)

            def weigh_values(n):
                i = n % NT
                if n < NT:
                    pe.wait_ge(v_lo, NT * it + n + 1)
                pe.wait_ge(pt_lo, STEPS0 * it + n + 1)
                if n >= 1:
                    pe.wait_ge(o_done, STEPS0 * it + n)
                for kb in range(i + 1):
                    mm = pass3(pe, ps[3][:, 0:E0], PT_h[:, tile(kb)], PT_l[:, tile(kb)], V_h[:, kb, :], V_l[:, kb, :],
                               kb == 0, kb == i)
                mm.then_inc(pv_done, 1)

            def transpose_p(n):
                pe.wait_ge(p_ready, STEPS0 * it + n + 1)
                if n >= 1:
                    pe.wait_ge(pt_lo, STEPS0 * it + n)
                for kb in range(n % NT + 1):
                    mm = nc.tensor.transpose(ps[2][:, tile(kb)], E1[n % 2][:, tile(kb)], ident[:])
                mm.then_inc(pt_ps, 1)

            for s in range(STEPS0):
                if s >= 2:
                    transpose_p(s - 2)
                scores(s)
                if s < V_STEPS:
                    project0(it, UNITS0 + 2 * s)
                    project0(it, UNITS0 + 2 * s + 1)
                if s >= 2:
                    weigh_values(s - 2)
            for kind, n in tail0(last):
                if kind == "u":
                    if n % 2 == 0 and n < 4:
                        pe.wait_ge(exp_done[n // 2], STEPS0 * it + STEPS0)
                    project0(it + 1, n)
                elif kind == "t":
                    transpose_p(n)
                else:
                    weigh_values(n)

        def attn0_out(b):
            for i in range(NT + 1):
                if i < NT:
                    pe.wait_ge(on_done, NT * b + i + 1)
                    for q in range(4):
                        if i >= 1:
                            pe.wait_ge(ot_lo, 4 * NT * b + 4 * (i - 1) + q + 1)
                        for r in range(4):
                            ch = 4 * q + r
                            mm = nc.tensor.transpose(ring[q][:, tile(r)], On[:, ch // 2, tile(ch % 2)], ident[:])
                        mm.then_inc(ot_ps, 1)
                if i >= 1:
                    t = i - 1
                    pe.wait_ge(ot_lo, 4 * NT * b + 4 * t + 4)
                    if t == 0:
                        pe.wait_ge(wo_lo, 4 * b + 4)
                    if t >= 2:
                        pe.wait_ge(z_done, LN_B * b + t - 1)
                    y = ps[3][:, t % 2 * HALF:t % 2 * HALF + HID]
                    for ch in range(2 * HEADS0):
                        mm = pass3(pe, y, OT_h[t % 2][:, ch, :], OT_l[t % 2][:, ch, :], Wo_h[:, ch, :], Wo_l[:, ch, :],
                                   ch == 0, ch == 2 * HEADS0 - 1)
                    mm.then_inc(y_mm, 1)

        def gate_up(b, c, j):
            cc = b * CHUNKS + c
            pe.wait_ge(fw_lo, cc + 3)
            for h in range(2):
                pe.wait_ge(gu_used, 2 * cc + h + 1)
                for k, ready in ((0, gate_mm), (1, up_mm)):
                    for kc in range(KC):
                        w, n = tile(k * KC + kc), tile(h, HALF)
                        mm = pass3(pe, ps[2 + h][:, tile(k, HALF)], Fw_h[j][:, w], Fw_l[j][:, w],
                                   XT_h[:, kc, n], XT_l[:, kc, n], kc == 0, kc == KC - 1)
                    mm.then_inc(ready, 1)

        def down(b, c, j):
            cc = b * CHUNKS + c
            w = slice(2 * KC * P, FFN_COLS)
            for t in range(NT):
                if t % 4 == 0:
                    pe.wait_ge(h_lo, 2 * cc + t // 4 + 5)
                mm = pass3(pe, ring[t // 2][:, tile(t % 2, HID)], H_h[j % 2][:, tile(t)], H_l[j % 2][:, tile(t)],
                           Fw_h[j][:, w], Fw_l[j][:, w], False, True, skip_group_check=True)
                if t in (1, 3, 5):
                    mm.then_inc(y_bank, 1)
            mm.then_inc(down_mm, 1)

        def ffn(b, layer, c0, chunks):
            def body(q, last):
                for j in range(QUAD):
                    c = q * QUAD + (c0 + j)
                    if not (last and j == QUAD - 1):
                        gate_up(b, c + 1, (j + 1) % QUAD)
                    if j == 0:
                        pe.wait_ge(y_zero, 2 * b + layer + 1)
                    down(b, c, j)

            wait_xt(b, 2 * layer + 1)
            gate_up(b, c0, 0)
            if layer == 1:
                pe.wait_ge(rt_dve, R_B * b + R_B)
                nc.tensor.transpose(ps[0][:, 0:P], comb_oh[:].rearrange("p a t e -> p (a t e)"),
                                    ident[:]).then_inc(ct_ps, 1)
            quads(pe, chunks // QUAD, body)

        def attn1_values(b):
            pe.wait_ge(wv_lo, b + 1)
            wait_xt(b, 2)
            for t in range(NT):
                if t >= 4:
                    pe.wait_ge(v1_done, NT * b + t - 3)
                for c in range(KC):
                    mm = pass3(pe, ring[t % 4][:, 0:HID], XT_h[:, c, tile(t)], XT_l[:, c, tile(t)], Wv_h[:, 0, c, :],
                               Wv_l[:, 0, c, :], c == 0, c == KC - 1)
                mm.then_inc(v1_mm, 1)

        def stack1(kind, p, h, it, heads_out):
            if kind == "uk":
                if h == 0:
                    pe.wait_ge(wb_lo, it + 1)
                if not (p == 0 and h == 0):
                    pe.wait_ge(uk_full, 4 * it + 2 * p + h)
                pe.wait_ge(o1_done, heads_out + 1)
            elif h == 1:
                pe.wait_ge(uq_full, 4 * it + 2 * p + 1)
            w, n = tile(p + (2 if kind == "uk" else 0)), tile(h, HALF)
            bank = ps[3][:, HALF:] if kind == "uk" else ps[3][:, 0:HALF]
            for c in range(KC):
                mm = pass3(pe, bank, Wb_h[:, c, w], Wb_l[:, c, w], XT_h[:, c, n], XT_l[:, c, n], c == 0, c == KC - 1)
            mm.then_inc(u_mm, 1)

        def score_piece(H, j, k):
            if k == 0 and j % 2 == 0:
                pe.wait_ge(ks_done, H + 3)
                pe.wait_ge(qs_done, H + 3)
            pe.wait_ge(a_used, PIECES1 * H + k + 1)
            i, a, z, scored = a_piece(k)
            bank = ps[0][:, tile(k % 2, HALF)]
            mm = nc.tensor.matmul(bank[:, 0:scored - a], QS[:, j, tile(i)], KS[:, j // 2, a:scored], start=True, stop=True)
            if z == (i + 1) * P:
                mm = nc.tensor.matmul(bank[:, z - P - a:z - a], ident_bf[:], mask_bf[:], start=False, stop=True,
                                      skip_group_check=True)
            mm.then_inc(a_ready, 1)

        def max_rows(H, h):
            pe.wait_ge(nm_lo, 2 * H + h + 1)
            for i in range(4):
                mm = nc.tensor.transpose(ps[3][:, tile(i)], nmax1_cols[:, 4 * h + i, :].bitcast(F32), ident[:])
            mm.then_inc(nt_ps, 1)

        def attn1_group(b, g, last):
            it = b * GROUPS1 + g

            def score_piece_t(H, j, k):
                if k in (0, 4):
                    pe.wait_ge(n_done, 2 * H + (2 if k else 1))
                pe.wait_ge(t_used, PIECES1 * H + k + 1)
                kb, a, z = t_piece(k)
                bank, base = ps[1][:, tile(k % 2, HALF)], z - HALF
                n = min(a, z - 2 * P)
                mm = nc.tensor.matmul(bank[:, n - base:], KS[:, j // 2, tile(kb)], QS[:, j, n:z], start=True, stop=True)
                if a == kb * P:
                    mm = nc.tensor.matmul(bank[:, a - base:a - base + P], mask_bf[:], ident_bf[:], start=False, stop=True,
                                          skip_group_check=True)
                mm.then_inc(t_ready, 1)

            def weigh_values(H, j, rd):
                pe.wait_ge(t_used, PIECES1 * H + 4 * rd + 4 + 2)
                if rd == 0:
                    pe.wait_ge(vs_done, H + 1)
                if rd < 2:
                    pe.wait_ge(ots_done[rd], H + 1)
                for c in range(4):
                    kb, a, z = t_piece(4 * rd + c)
                    mm = nc.tensor.matmul(ps[2][32 * c:32 * c + 32, a:z], Vs[:, kb, j, :],
                                          PT[:, 4 * rd + c, a - (z - HALF):], start=rd < 2, stop=True,
                                          skip_group_check=rd == 2, tile_position=(0, 32 * c))
                mm.then_inc(pv1_done, 1)

            def output(H, pieces):
                pe.wait_ge(uk_full, pieces)
                for h in range(2):
                    pe.wait_ge(ots_done[h], H + 2)
                for t in range(NT):
                    mm = nc.tensor.matmul(ps[3][:, HALF + t * 32:HALF + t * 32 + 32], OTs[:, tile(t)], isum[:],
                                          start=True, stop=True)
                mm.then_inc(o_ps, 1)

            for j in range(4):
                H = it * 4 + j
                pieces = 4 * it + (2 if j < 1 else 4)
                stacked = 0
                for kind, n in slot1(j, last):
                    if kind == "a":
                        score_piece(H + 1, (j + 1) % 4, n)
                    elif kind == "t":
                        score_piece_t(H, j, n)
                    elif kind in ("uk", "uq"):
                        stack1(kind, 1 if j == 0 else 0, n, it + (0 if j == 0 else 1), H - (1 if j == 2 and n == 0 else 0))
                        stacked += kind == "uk"
                    elif kind == "n":
                        if stacked:
                            pe.wait_ge(uq_full, pieces + 2 - n)
                        pe.wait_ge(n_done, 2 * H + 2 - n)
                        max_rows(H + 1 - n, n)
                    elif kind == "v":
                        weigh_values(H, j, n)
                    elif kind == "o":
                        output(H - 1, pieces + stacked)
                    elif kind == "end":
                        output(H, pieces + (0 if last else 2))

        def attn1_out(b):
            pe.wait_ge(o1_done, HEADS1 * b + HEADS1 + 1)
            for j in range(NT // 2):
                for c in range(KC):
                    for r in range(2):
                        mm = nc.tensor.transpose(xt_bank[j][:, c * 2 * P + r * P:c * 2 * P + (r + 1) * P],
                                                 O1[:, 2 * j + r, tile(c)], ident[:])
                mm.then_inc(o1t_ps, 1)
            for t in range(NT):
                pe.wait_ge(o1t_lo, 4 * b + t // 2 + 1)
                for c in range(KC):
                    mm = pass3(pe, ring[t // 2][:, tile(t % 2, HID)], O1T_h[:, c, tile(t)], O1T_l[:, c, tile(t)],
                               Wv_h[:, 1, c, :], Wv_l[:, 1, c, :], c == 0, c == KC - 1)
                mm.then_inc(y1_mm, 1)

        def router(b):
            pe.wait_ge(rw_lo, b + 1)
            wait_xt(b, 3)
            for h in range(2):
                for c in range(KC):
                    n = tile(h, HALF)
                    mm = pass3(pe, ps[0][:, n], Rw_h[:, c, :], Rw_l[:, c, :], XT_h[:, c, n], XT_l[:, c, n],
                               c == 0, c == KC - 1)
                mm.then_inc(lg_mm, 1)
            for t in range(NT):
                if t % 4 == 0:
                    pe.wait_ge(lg_copy, 2 * b + t // 4 + 1)
                mm = nc.tensor.transpose(ps[1][:, tile(t)], LG[:, tile(t)], ident[:])
            mm.then_inc(lg_t, 1)
        pe.wait_ge(pre_dve, 8)
        for q in range(4):
            n = tile(q, 2)
            nc.tensor.matmul(ring[q], hada[:], w2_h[:, n, :], start=True, stop=False)
            nc.tensor.matmul(ring[q], hada[:], w2_l[:, n, :], start=False, stop=True).then_inc(pre_pe, 1)
        with pe.Fori(0, B) as b:
            transpose_x(b, 0)
            wait_xt(b, 0)
            pe.wait_ge(w2_ready, 4)
            pe.wait_ge(pre_dve, 13)
            for u in range(UNITS0):
                project0(b * GROUPS0, u)
            with pe.Fori(0, GROUPS0 - 1) as g:
                attn0_group(b, g, False)
            attn0_group(b, GROUPS0 - 1, True)
            attn0_out(b)
            transpose_x(b, 1)
            ffn(b, 0, 0, CH_F0)
            transpose_x(b, 2)
            attn1_values(b)
            pe.wait_ge(o_zero, b + 1)
            for kind, n in STACK1:
                if kind in ("uk", "uq"):
                    stack1(kind, 0, n, b * GROUPS1, b * HEADS1)
            for kind, n in MAXIMA1:
                if kind == "a":
                    score_piece(b * HEADS1, 0, n)
                else:
                    pe.wait_ge(uq_full, 4 * GROUPS1 * b + 2)
                    max_rows(b * HEADS1, n)
            with pe.Fori(0, GROUPS1 - 1) as g:
                attn1_group(b, g, False)
            attn1_group(b, GROUPS1 - 1, True)
            attn1_out(b)
            transpose_x(b, 3)
            router(b)
            ffn(b, 1, CH_F0, CH_SHARED + CH_ROUTED)

    @block.scalar
    def _(act):
        def x_parts(b, k):
            for j in range(NT // 2):
                act.wait_ge(xt_ps, LN_B // 2 * b + 4 * k + j + 1)
                nc.scalar.activation(XT_h[:, :, tile(j, 2 * P)], xt_bank[j].rearrange("p (c n) -> p c n", c=KC),
                                     ACT.Copy).then_inc(xt_hi, 1)

        def ln_sqrt(b, k):
            for h in range(2):
                act.wait_ge(ln_ag, LN_B * b + NT * k + 4 * h + 4)
                nc.scalar.activation(sd[:, tile(h, 4)], mv[:, tile(h, 4), 1], ACT.Sqrt, bias=eps_col[:]).then_inc(ln_sd, 1)

        def split_wa(it):
            act.wait_ge(wa_in, 48 * it + 48)
            q = slice(2 * D0, UNITS0 // 2 * D0)
            nc.scalar.mul(ba[:, 2:6], ba[:, 2:6], SCALE0)
            nc.scalar.mul(Wa_raw[:, :, q], Wa_raw[:, :, q], SCALE0).then_inc(wa_scaled, 1)
            act.wait_ge(wa_scaled, it + 1)
            nc.scalar.copy(Wa_h[:], Wa_raw[:]).then_inc(wa_hi, 1)

        def take0(it, u):
            if u < UNITS0:
                act.wait_ge(pj_mm, UNITS_IT * it + u + 1)
                dst = K_h[:, u // 2, tile(u % 2, HALF)] if u < 4 else \
                    Q_h[:, (u - 4) // 4, (u - 4) // 2 % 2, tile(u % 2, HALF)]
                nc.scalar.activation(dst, ring[u % 4], ACT.Identity, bias=ba[:, u // 2:u // 2 + 1]).then_inc(pj_hi, 1)

        def attn0_group(b, g, last):
            it = b * GROUPS0 + g

            def high(n):
                w = (n % NT + 1) * P
                act.wait_ge(pt_ps, STEPS0 * it + n + 1)
                nc.scalar.copy(PT_h[:, 0:w], ps[2][:, 0:w]).then_inc(pt_hi, 1)

            def squares(n):
                act.wait_ge(o_done, STEPS0 * it + n + 1)
                act.wait_ge(sq_done, STEPS0 * it + n + 1)
                nc.scalar.activation(sq_junk, O[:, n % NT, bass.ds(g * 2 + n // NT, 1), :], ACT.Square,
                                     accum_out=ssq[:, bass.ds(g * STEPS0 + n, 1)]).then_inc(sq_done, 1)

            for s in range(STEPS0):
                if s >= 2:
                    high(s - 2)
                w = (s % NT + 1) * P
                for m, e in ((0, E1[s % 2]), (1, E2[s % 2])):
                    act.wait_ge(nmax_ready[m], STEPS0 * it + s + 1)
                    nc.scalar.activation(e[:, 0:w], ps[m][:, 0:w], ACT.Exp, bias=nmax[:, s % 4, m:m + 1],
                                         accum_out=lsum[:, s % 4, m:m + 1]).then_inc(exp_done[m], 1)
                if s < V_STEPS:
                    for t in (2 * s, 2 * s + 1):
                        act.wait_ge(pj_dve, UNITS_IT * it + UNITS0 + t + 1)
                        nc.scalar.copy(V_h[:, t, :], O[:, t, bass.ds(g * 2 + 1, 1), :]).then_inc(v_hi, 1)
                if s >= 3:
                    squares(s - 3)
                if s == NT:
                    split_wa(it + 1)
            squares(STEPS0 - 3)
            for kind, n in tail0(last):
                if kind == "u":
                    take0(it + 1, n)
                    if n == 3:
                        squares(STEPS0 - 2)
                elif kind == "t":
                    high(n)
            if last:
                squares(STEPS0 - 2)
            squares(STEPS0 - 1)

        def attn0_out(b):
            act.wait_ge(or_dve, 2 * b + 1)
            nc.scalar.activation(ssq[:], orstd[:], ACT.Sqrt).then_inc(or_act, 1)
            for q in range(4):
                act.wait_ge(wo_scaled, 8 * b + 2 * q + 2)
                nc.scalar.copy(Wo_h[:, tile(q, 4), :], Wo_raw[:, tile(q, 4), :]).then_inc(wo_hi, 1)
            for i in range(NT):
                for q in range(4):
                    act.wait_ge(ot_ps, 4 * NT * b + 4 * i + q + 1)
                    nc.scalar.copy(OT_h[i % 2][:, tile(q, 4), :],
                                   ring[q].rearrange("p (c n) -> p c n", c=4)).then_inc(ot_hi, 1)

        def ffn_split(b, c, j):
            cc = b * CHUNKS + c
            act.wait_ge(fw_in[j % 2], b * (CHUNKS * 16) + (c + (2 - j % 2)) * 16)
            nc.scalar.copy(Fw_h[j][:], Fw_raw[j % 2][:]).then_inc(fw_hi, 1)

        def ffn(b, c0, chunks, routed_from):
            def body(q, last, routed=False):
                for j in range(QUAD):
                    c = q * QUAD + (c0 + j)
                    cc = b * CHUNKS + c
                    if not (last and j == QUAD - 1):
                        ffn_split(b, c + 1, (j + 1) % QUAD)
                    act.wait_ge(down_mm, cc + 1)
                    for h in range(2):
                        act.wait_ge(gate_mm, 2 * cc + h + 1)
                        act.wait_ge(gu_used, 2 * cc + h + 1)
                        nc.scalar.activation(silu_g[h][:], ps[2 + h][:, 0:HALF], ACT.Silu).then_inc(silu_done, 1)
                        if routed:
                            act.wait_ge(hm_done, 2 * (b * EXPERTS + (c - (CH_F0 + CH_SHARED))) + h + 1)
                        else:
                            act.wait_ge(gu_used, 2 * cc + h + 3)
                        nc.scalar.copy(H_h[j % 2][:, tile(h, HALF)], Hf[j % 2][:, tile(h, HALF)]).then_inc(h_hi, 1)

            ffn_split(b, c0, 0)
            if routed_from is None:
                quads(act, chunks // QUAD, body)
            else:
                with act.Fori(0, (routed_from - c0) // QUAD) as q:
                    body(q, False)
                for q in range((routed_from - c0) // QUAD, chunks // QUAD):
                    body(q, q == chunks // QUAD - 1, True)

        def split_wb(it):
            act.wait_ge(wb_in, 16 * it + 16)
            nc.scalar.copy(Wb_h[:], Wb_raw[:]).then_inc(wb_hi, 1)

        def stack1(kind, p, h, it):
            done = 4 * it + 2 * p + h
            if kind == "uq":
                act.wait_ge(bb_in, 32 * it + 32)
                act.wait_ge(u_mm, 2 * done + 2)
                act.wait_ge(qs_done, done + 1)
                nc.scalar.activation(st_q[:], ps[3][:, 0:HALF], ACT.Identity, bias=bb[:, p:p + 1]).then_inc(uq_full, 1)
                act.wait_ge(uq_full, done + 1)
                nc.scalar.mul(neg_q[:], st_q[:], bsel[:, 0:1]).then_inc(uq_neg, 1)
            elif kind == "zk":
                act.wait_ge(uk_full, done + 1)
                nc.scalar.mul(neg_k[:], st_k[:], bsel[:, 1:2]).then_inc(uk_neg, 1)

        def max_rows(H, j, h):
            rows = slice(j % 2 * SLOT1 + MAX_ROW, j % 2 * SLOT1 + MAX_ROW + 2)
            act.wait_ge(nt_ps, 2 * H + h + 1)
            nc.scalar.copy(QS[rows, j, tile(h, HALF)], ps[3][rows, 0:HALF]).then_inc(n_done, 1)

        def attn1_group(b, g, last):
            it = b * GROUPS1 + g
            for j in range(4):
                H = it * 4 + j
                if j == 1 and not last:
                    act.wait_ge(u_mm, 8 * it + 8)
                    split_wb(it + 1)
                for kind, n in slot1(j, last):
                    if kind == "t":
                        kb, a, z = t_piece(n)
                        if n % 4 == 0:
                            act.wait_ge(pv1_done, 3 * H + n // 4 + 1)
                        act.wait_ge(t_ready, PIECES1 * H + n + 1)
                        nc.scalar.activation(PT[:, n, a - (z - HALF):], ps[1][:, n % 2 * HALF + a - (z - HALF):(n % 2 + 1) * HALF],
                                             ACT.Exp, scale=SCALE1).then_inc(t_used, 1)
                    elif kind == "n":
                        max_rows(H + 1 - n, (j + 1 - n) % 4, n)
                    elif kind in ("uq", "zk"):
                        stack1(kind, 1 if j == 0 else 0, n, it + (0 if j == 0 else 1))
                    elif kind == "c" and n == 0:
                        act.wait_ge(pv1_done, 3 * H + 1 + 3)
                        nc.scalar.copy(OTs[:, 0:HALF], ps[2][:, 0:HALF]).then_inc(ots_done[0], 1)

        def attn1_out(b):
            for j in range(NT // 2):
                act.wait_ge(o1t_ps, 4 * b + j + 1)
                nc.scalar.copy(O1T_h[:, :, tile(j, 2 * P)],
                               xt_bank[j].rearrange("p (c n) -> p c n", c=KC)).then_inc(o1t_hi, 1)

        def router(b):
            act.wait_ge(rw_in, 16 * b + 16)
            nc.scalar.copy(Rw_h[:], Rw_raw[:]).then_inc(rw_hi, 1)
            act.wait_ge(lg_t, b + 1)
            nc.scalar.activation(ta[:], ps[1][:].rearrange("p (t n) -> p t n", t=NT)[:, :, 0:EXPERTS], ACT.Exp,
                                 scale=-1.0).then_inc(sig_exp, 1)

        for q in range(4):
            act.wait_ge(pre_pe, q + 1)
            nc.scalar.mul(w2b[:, tile(q, 2), :], ring[q].rearrange("p (c n) -> p c n", c=2),
                          float((CH_F0 * P) ** -0.5)).then_inc(w2_ready, 1)
        split_wa(0)
        act.wait_ge(pre_dve, 13)
        nc.scalar.activation(lam_exp[:], lam_sum[:], ACT.Exp).then_inc(pre_act, 1)
        with act.Fori(0, B) as b:
            x_parts(b, 0)
            for u in range(UNITS0):
                if u == UNITS0 - 1:
                    act.wait_ge(xb_done, 2 * b + 1)
                take0(b * GROUPS0, u)
            with act.Fori(0, GROUPS0 - 1) as g:
                attn0_group(b, g, False)
            attn0_group(b, GROUPS0 - 1, True)
            attn0_out(b)
            ln_sqrt(b, 0)
            x_parts(b, 1)
            ffn(b, 0, CH_F0, None)
            act.wait_ge(wv_in, 16 * b + 16)
            nc.scalar.copy(Wv_h[:], Wv_raw[:]).then_inc(wv_hi, 1)
            split_wb(b * GROUPS1)
            ln_sqrt(b, 1)
            x_parts(b, 2)
            for kind, n in STACK1:
                stack1(kind, 0, n, b * GROUPS1)
            max_rows(b * HEADS1, 0, 0)
            with act.Fori(0, GROUPS1 - 1) as g:
                attn1_group(b, g, False)
            attn1_group(b, GROUPS1 - 1, True)
            attn1_out(b)
            ln_sqrt(b, 2)
            x_parts(b, 3)
            router(b)
            ffn(b, CH_F0, CH_SHARED + CH_ROUTED, CH_F0 + CH_SHARED)
            ln_sqrt(b, 3)

    @block.vector
    def _(dve):
        def x_parts(b, k):
            for j in range(NT // 2):
                dve.wait_ge(xt_hi, LN_B // 2 * b + 4 * k + j + 1)
                n = tile(j, 2 * P)
                nc.vector.tensor_tensor(XT_l[:, :, n], xt_bank[j].rearrange("p (c n) -> p c n", c=KC),
                                        XT_h[:, :, n].bitcast(F32), ALU.subtract).then_inc(xt_lo, 1)

        def residual(b, k, t, y):
            nc.vector.tensor_tensor(X[:, t, :], y, X[:, t, :], ALU.add).then_inc(z_done, 1)

        def stats(b, k, t):
            dve.wait_ge(z_done, LN_B * b + NT * k + t + 1)
            nc.vector.bn_stats(st[:, t, :], X[:, t, :]).then_inc(ln_st, 1)

        def moments(b, k, h):
            dve.wait_ge(ln_st, LN_B * b + NT * k + 4 * h + 4)
            dve.nop(nofuse=True)
            for t in range(4 * h, 4 * h + 4):
                nc.vector.bn_aggr(mv[:, t, :], st[:, t, :]).then_inc(ln_ag, 1)

        def layernorm(b, k, h):
            n = 8 * b + 2 * k + h + 1
            dve.wait_ge(ln_sd, n)
            nc.vector.reciprocal(rstd[:, tile(h, 4)], sd[:, tile(h, 4)]).then_inc(ln_rs, 1)
            dve.wait_ge(ln_rs, n)
            for t in range(4 * h, 4 * h + 4):
                nc.vector.tensor_scalar(X[:, t, :], X[:, t, :], mv[:, t, 0:1], rstd[:, t:t + 1], ALU.subtract,
                                        ALU.mult).then_inc(ln_done, 1)

        def add_norm(b, k, wait_tile, y):
            for t in range(NT):
                wait_tile(t)
                residual(b, k, t, y(t))
                if t >= 1:
                    stats(b, k, t - 1)
                if t == 4:
                    moments(b, k, 0)
                if t == 5:
                    layernorm(b, k, 0)
            stats(b, k, NT - 1)
            moments(b, k, 1)
            layernorm(b, k, 1)

        def take0(it, u):
            h, l = (K_h, K_l) if u < 4 else (Q_h, Q_l)
            at = (slice(None), u // 2) if u < 4 else (slice(None), (u - 4) // 4, (u - 4) // 2 % 2)
            at += (tile(u % 2, HALF),)
            dve.wait_ge(pj_hi, UNITS0 * it + u + 1)
            nc.vector.scalar_tensor_tensor(out=l[at], in0=ring[u % 4], scalar=ba[:, u // 2:u // 2 + 1],
                                           in1=h[at].bitcast(F32), op0=ALU.add,
                                           op1=ALU.subtract).then_inc(pj_dve, 1)

        def attn0_group(b, g, last):
            it = b * GROUPS0 + g

            def mix(n):
                dve.wait_ge(exp_done[1], STEPS0 * it + n + 1)
                nc.vector.reciprocal(rsum[:, n % 8, :], lsum[:, n % 4, :]).then_inc(rsum_ready, 1)
                dve.wait_ge(rsum_ready, STEPS0 * it + n + 1)
                nc.vector.scalar_tensor_tensor(out=mixc[:, n % 4:n % 4 + 1], in0=rsum[:, n % 8, 1:2],
                                               scalar=lsum[:, n % 4, 0:1], in1=neglam[:], op0=ALU.mult,
                                               op1=ALU.mult).then_inc(mix_ready, 1)

            def low(n):
                w = (n % NT + 1) * P
                dve.wait_ge(pt_hi, STEPS0 * it + n + 1)
                nc.vector.tensor_tensor(PT_l[:, 0:w], ps[2][:, 0:w], PT_h[:, 0:w].bitcast(F32),
                                        ALU.subtract).then_inc(pt_lo, 1)

            def output(n):
                dve.wait_ge(pv_done, STEPS0 * it + n + 1)
                nc.vector.tensor_scalar(O[:, n % NT, bass.ds(g * 2 + n // NT, 1), :],
                                        ps[3][:, 0:E0].unsqueeze(1), rsum[:, n % 8, 0:1], None,
                                        ALU.mult).then_inc(o_done, 1)

            for s in range(STEPS0):
                if s >= 1:
                    mix(s - 1)
                if s >= 2:
                    low(s - 2)
                for m in range(2):
                    dve.wait_ge(s_ready[m], STEPS0 * it + s + 1)
                    nc.vector.tensor_reduce(nmax[:, s % 4, m:m + 1], ps[m][:, 0:(s % NT + 1) * P], AX.X, ALU.max,
                                            negate=True).then_inc(nmax_ready[m], 1)
                if s < V_STEPS:
                    for t in (2 * s, 2 * s + 1):
                        dve.wait_ge(pj_mm, UNITS_IT * it + UNITS0 + t + 1)
                        nc.vector.tensor_tensor(O[:, t, bass.ds(g * 2 + 1, 1), :],
                                                ring[t % 2 * 2 + 1][:, 0:E0].unsqueeze(1), bva[:].unsqueeze(1),
                                                ALU.add).then_inc(pj_dve, 1)
                if s >= 2:
                    output(s - 2)
            mix(STEPS0 - 1)
            for kind, n in tail0(last):
                if kind == "u":
                    take0(it + 1, n)
                elif kind == "t":
                    low(n)
                else:
                    output(n)

        def attn0_out(b):
            dve.wait_ge(sq_done, STEPS0 * GROUPS0 * b + STEPS0 * GROUPS0 + 1)
            nc.vector.tensor_scalar(orstd[:], ssq[:], 1.0 / E0, EPS, ALU.mult, ALU.add).then_inc(or_dve, 1)
            dve.wait_ge(or_act, b + 1)
            nc.vector.reciprocal(orstd[:], ssq[:]).then_inc(or_dve, 1)
            dve.wait_ge(or_dve, 2 * b + 2)

            def normalise(i):
                if i >= 1:
                    dve.wait_ge(ot_ps, 4 * NT * b + 4 * i)
                for h in range(HEADS0):
                    ins = nc.vector.tensor_scalar(On[:, h, :], O[:, i, h, :], orstd[:, h * NT + i:h * NT + i + 1], None,
                                                  ALU.mult)
                ins.then_inc(on_done, 1)

            normalise(0)
            for q in range(4):
                dve.wait_ge(wo_hi, 4 * b + q + 1)
                n = tile(q, 4)
                nc.vector.tensor_tensor(Wo_l[:, n, :], Wo_raw[:, n, :], Wo_h[:, n, :].bitcast(F32),
                                        ALU.subtract).then_inc(wo_lo, 1)
            dve.wait_ge(xb_done, 2 * b + 1)

            def next_tile(t):
                for i in (0, 1) if t == 0 else (t + 1,):
                    if i < NT:
                        for q in range(4):
                            dve.wait_ge(ot_hi, 4 * NT * b + 4 * i + q + 1)
                            n = tile(q, 4)
                            nc.vector.tensor_tensor(OT_l[i % 2][:, n, :], ring[q].rearrange("p (c n) -> p c n", c=4),
                                                    OT_h[i % 2][:, n, :].bitcast(F32), ALU.subtract).then_inc(ot_lo, 1)
                    if i + 1 < NT:
                        normalise(i + 1)
                dve.wait_ge(y_mm, NT * b + t + 1)

            add_norm(b, 0, next_tile, lambda t: ps[3][:, t % 2 * HALF:t % 2 * HALF + HID])

        def ffn(b, layer, c0, chunks, routed):
            if not routed:
                if layer == 1:
                    dve.wait_ge(ct_copy, b + 1)
                for p in ps[0:2]:
                    last = nc.vector.memset(p[:], 0.0)
                last.then_inc(y_zero, 1)
            with dve.Fori(0, chunks // QUAD) as q:
                for j in range(QUAD):
                    c = q * QUAD + (c0 + j)
                    cc = b * CHUNKS + c
                    for h in range(2):
                        n = tile(h, HALF)
                        dve.wait_ge(h_lo, 2 * cc + h + 1)
                        dve.wait_ge(silu_done, 2 * cc + h + 1)
                        dve.wait_ge(up_mm, 2 * cc + h + 1)
                        nc.vector.tensor_tensor(Hf[j % 2][:, n], ps[2 + h][:, HALF:], silu_g[h][:],
                                                ALU.mult).then_inc(gu_used, 1)
                        if routed:
                            dve.wait_ge(gu_used, 2 * cc + h + 3)
                            dve.wait_ge(comb_in, EXPERTS * 16 * b + EXPERTS * 16)
                            nc.vector.tensor_tensor(Hf[j % 2][:, n], Hf[j % 2][:, n],
                                                    comb_bc[:, bass.ds(q * QUAD + j, 1), tile(h, 4)]
                                                    .rearrange("p e t n -> p (e t n)"), ALU.mult).then_inc(hm_done, 1)

        def ffn_out(b, k, c_end):
            def bank(t):
                if t < 6:
                    dve.wait_ge(y_bank, 3 * CHUNKS * b + 3 * c_end - 2 + t // 2)
                else:
                    dve.wait_ge(down_mm, b * CHUNKS + c_end + 2)

            add_norm(b, k, bank, lambda t: ring[t // 2][:, tile(t % 2, HID)])

        def stack1(kind, p, h, it):
            done, n = 4 * it + 2 * p + h, tile(h, HALF)
            if kind == "uk":
                dve.wait_ge(bb_in, 32 * it + 32)
                dve.wait_ge(u_mm, 2 * done + 1)
                dve.wait_ge(ks_done, done + 1)
                nc.vector.scalar_tensor_tensor(out=st_k[:], in0=ps[3][:, HALF:], scalar=bb[:, 2 + p:3 + p],
                                               in1=alibi[:, p, n], op0=ALU.add, op1=ALU.add).then_inc(uk_full, 1)
            elif kind == "zq":
                dve.wait_ge(uq_neg, done + 1)
                for r in range(2):
                    rows = tile(r, SLOT1)
                    ins = nc.vector.tensor_tensor(QS[rows, 2 * p + r, n], st_q[rows, :], neg_q[rows, :].bitcast(F32), ALU.add)
                ins.then_inc(qs_done, 1)

        def row_max(H, k):
            i, a, z, _ = a_piece(k)
            dst = nmax1[:, i:i + 1] if i < 4 else nmax1_part[:, k % 2, i - 4:i - 3]
            dve.wait_ge(a_ready, PIECES1 * H + k + 1)
            nc.vector.tensor_reduce(dst, ps[0][:, k % 2 * HALF:k % 2 * HALF + z - a], AX.X, ALU.max,
                                    negate=True).then_inc(a_used, 1)
            if k not in (3, PIECES1 - 1):
                return
            h = 0 if k == 3 else 1
            tiles = tile(h, 4)
            dve.wait_ge(a_used, PIECES1 * H + k + 3)
            if h == 1:
                nc.vector.tensor_tensor(nmax1[:, tiles], nmax1_part[:, 0], nmax1_part[:, 1], ALU.min).then_inc(nm_both, 1)
                dve.wait_ge(nm_both, H + 1)
            full = nmax1[:, tiles].unsqueeze(2).to_broadcast([P, 4, 2])
            high, low = (nmax1_cols[:, tiles, MAX_ROW + i::SLOT1] for i in range(2))
            nc.vector.tensor_copy(high, full).then_inc(nm_hi, 1)
            dve.wait_ge(nm_hi, 2 * H + h + 1)
            nc.vector.tensor_tensor(low, full, high.bitcast(F32), ALU.subtract).then_inc(nm_lo, 1)

        def attn1_group(b, g, last):
            it = b * GROUPS1 + g

            def output(H, j):
                o = ps[3][:, HALF:HALF + NT * 32].rearrange("p (t e) -> p t e", t=NT)
                dve.wait_ge(o_ps, H + 1)
                nc.vector.reciprocal(rsum1[:], o[:, :, D1]).then_inc(rs1_done, 1)
                dve.wait_ge(rs1_done, H + 1)
                nc.vector.tensor_tensor(O1[:, :, bass.ds(g * 4 * D1 + j * D1, D1)], o[:, :, 0:D1],
                                        rsum1[:].unsqueeze(2).to_broadcast([P, NT, D1]), ALU.mult).then_inc(o1_done, 1)

            for j in range(4):
                H = it * 4 + j
                for kind, n in slot1(j, last):
                    if kind == "a":
                        row_max(H + 1, n)
                    elif kind in ("uk", "zq"):
                        stack1(kind, 1 if j == 0 else 0, n, it + (0 if j == 0 else 1))
                    elif kind == "c" and n == 1:
                        dve.wait_ge(pv1_done, 3 * H + 3 + 3)
                        nc.vector.tensor_copy(OTs[:, HALF:], ps[2][:, HALF:]).then_inc(ots_done[1], 1)
                    elif kind == "o":
                        output(H - 1, j - 1)
                    elif kind == "end":
                        output(H, j)

        def attn1_out(b):
            for j in range(NT // 2):
                dve.wait_ge(o1t_hi, 4 * b + j + 1)
                n = tile(j, 2 * P)
                nc.vector.tensor_tensor(O1T_l[:, :, n], xt_bank[j].rearrange("p (c n) -> p c n", c=KC),
                                        O1T_h[:, :, n].bitcast(F32), ALU.subtract).then_inc(o1t_lo, 1)
            dve.wait_ge(xb_done, 2 * b + 2)
            add_norm(b, 2, lambda t: dve.wait_ge(y1_mm, NT * b + t // 2 * 2 + 2),
                     lambda t: ring[t // 2][:, tile(t % 2, HID)])

        def router(b):
            for h in range(2):
                dve.wait_ge(lg_mm, 2 * b + h + 1)
                nc.vector.tensor_copy(LG[:, tile(h, HALF)], ps[0][:, tile(h, HALF)]).then_inc(lg_copy, 1)
            dve.wait_ge(sig_exp, b + 1)
            done = [0]

            def then(ins):
                done[0] += 1
                ins.then_inc(rt_dve, 1)
                dve.wait_ge(rt_dve, R_B * b + done[0])

            def over_e(a):
                return a[:].unsqueeze(2).to_broadcast([P, NT, EXPERTS])

            def over_t(a):
                return a[:].unsqueeze(1).to_broadcast([P, NT, EXPERTS])

            def pick_first_best(vals, tmp, dst):
                then(nc.vector.tensor_reduce(tm[:], vals, AX.X, ALU.max))
                then(nc.vector.tensor_tensor(tmp, vals, over_e(tm), ALU.is_equal))
                then(nc.vector.tensor_tensor(tmp, tmp, over_t(first), ALU.mult))
                then(nc.vector.tensor_reduce(tm[:], tmp, AX.X, ALU.max))
                then(nc.vector.tensor_tensor(dst, tmp, over_e(tm), ALU.is_equal))

            then(nc.vector.tensor_scalar(ta[:], ta[:], 1.0, None, ALU.add))
            then(nc.vector.reciprocal(sc[:], ta[:]))
            then(nc.vector.tensor_tensor(sel[:], sc[:], over_t(rbias), ALU.add))
            pick_first_best(sel[:], ta[:], oh)
            then(nc.vector.scalar_tensor_tensor(out=sel[:], in0=oh, scalar=-1e30, in1=sel[:], op0=ALU.mult,
                                                op1=ALU.add))
            pick_first_best(sel[:], ta[:], tb[:])
            then(nc.vector.tensor_tensor(oh, oh, tb[:], ALU.add))
            then(nc.vector.tensor_tensor(sc[:], sc[:], oh, ALU.mult))
            then(nc.vector.tensor_reduce(tm[:], sc[:], AX.X, ALU.add))
            then(nc.vector.tensor_scalar(tm[:], tm[:], 1e-9, None, ALU.add))
            then(nc.vector.reciprocal(tm[:], tm[:]))
            then(nc.vector.tensor_tensor(comb, sc[:], over_e(tm), ALU.mult))
            assert done[0] == R_B
            dve.wait_ge(ct_ps, b + 1)
            nc.vector.tensor_copy(combT[:], ps[0][0:NT * EXPERTS, 0:P]).then_inc(ct_copy, 1)

        dve.wait_ge(w2_in, 32)
        src, dst = w2a, w2b
        for n, h in enumerate((1, 2, 4)):
            v, o = (a[:].rearrange("p (g r h) n -> p g r (h n)", r=2, h=h) for a in (src, dst))
            nc.vector.tensor_tensor(o[:, :, 0], v[:, :, 0], v[:, :, 1], ALU.add).then_inc(pre_dve, 1)
            nc.vector.tensor_tensor(o[:, :, 1], v[:, :, 0], v[:, :, 1], ALU.subtract).then_inc(pre_dve, 1)
            dve.wait_ge(pre_dve, 2 + 2 * n)
            src, dst = dst, src
        nc.vector.tensor_copy(hada[:], hada_raw[:]).then_inc(pre_dve, 1)
        nc.vector.tensor_copy(w2_h[:], src[:]).then_inc(pre_hi, 1)
        dve.wait_ge(pre_hi, 1)
        nc.vector.tensor_tensor(w2_l[:], src[:], w2_h[:].bitcast(F32), ALU.subtract).then_inc(pre_dve, 1)
        dve.wait_ge(const_in, CONSTS * 16)
        nc.vector.memset(eps_col[:], EPS).then_inc(pre_dve, 1)
        nc.vector.tensor_copy(ident_bf[:], ident[:]).then_inc(pre_dve, 1)
        nc.vector.tensor_copy(mask_bf[:], mask_raw[:]).then_inc(pre_dve, 1)
        for k in range(2):
            nc.vector.tensor_tensor_reduce(out=lam_prod[:, k, :], in0=lam_in[:, 2 * k, :], in1=lam_in[:, 2 * k + 1, :],
                                           scale=1.0, scalar=0.0, op0=ALU.mult, op1=ALU.add,
                                           accum_out=lam_sum[:, k:k + 1]).then_inc(pre_dve, 1)
        nc.vector.tensor_scalar(subln[:], subln[:], 1.0 - LAMBDA_INIT, None, ALU.mult)
        dve.wait_ge(pre_act, 1)
        nc.vector.scalar_tensor_tensor(out=neglam[:], in0=lam_exp[:, 1:2], scalar=-LAMBDA_INIT, in1=lam_exp[:, 0:1],
                                       op0=ALU.add, op1=ALU.subtract).then_inc(pre_dve, 1)
        dve.wait_ge(pre_dve, 14)
        with dve.Fori(0, B) as b:
            x_parts(b, 0)
            for u in range(UNITS0):
                take0(b * GROUPS0, u)
            dve.wait_ge(w2_out, 16)
            with dve.Fori(0, GROUPS0 - 1) as g:
                attn0_group(b, g, False)
            attn0_group(b, GROUPS0 - 1, True)
            attn0_out(b)
            x_parts(b, 1)
            ffn(b, 0, 0, CH_F0, False)
            ffn_out(b, 1, CH_F0)
            x_parts(b, 2)
            nc.vector.memset(Vs[:], 1.0).then_inc(qs_zero, 1)
            nc.vector.memset(QS[:].bitcast(F32), 0.0).then_inc(qs_zero, 1)
            nc.vector.memset(nmax1_cols[:].bitcast(F32), 0.0).then_inc(qs_zero, 1)
            for t in range(NT):
                dve.wait_ge(v1_mm, NT * b + t + 1)
                nc.vector.tensor_tensor(V1[:, t, :], ring[t % 4][:, 0:HID], rows_bc[:, 2, :], ALU.add).then_inc(v1_done, 1)
            nc.vector.memset(ps[2][:, 0:HALF], 0.0).then_inc(o_zero, 1)
            dve.wait_ge(qs_zero, 3 * b + 3)
            for kind, n in STACK1:
                stack1(kind, 0, n, b * GROUPS1)
            for kind, n in MAXIMA1:
                if kind == "a":
                    row_max(b * HEADS1, n)
            with dve.Fori(0, GROUPS1 - 1) as g:
                attn1_group(b, g, False)
            attn1_group(b, GROUPS1 - 1, True)
            attn1_out(b)
            x_parts(b, 3)
            router(b)
            ffn(b, 1, CH_F0, CH_SHARED, False)
            ffn(b, 1, CH_F0 + CH_SHARED, CH_ROUTED, True)
            ffn_out(b, 3, CHUNKS)

    @block.gpsimd
    def _(pool):
        def low(dst, full, high):
            return nc.gpsimd.tensor_tensor(dst, full, high.bitcast(F32), ALU.subtract)

        def split_wa(it):
            pool.wait_ge(wa_hi, it + 1)
            low(Wa_l[:], Wa_raw[:], Wa_h[:]).then_inc(wa_lo, 1)

        def attn0_group(b, g):
            it = b * GROUPS0 + g
            for n in range(STEPS0):
                if n == 0:
                    pool.wait_ge(xb_done, 2 * b + 1)
                if n < V_STEPS:
                    for t in (2 * n, 2 * n + 1):
                        pool.wait_ge(v_hi, NT * it + t + 1)
                        low(V_l[:, t, :].unsqueeze(1), O[:, t, bass.ds(g * 2 + 1, 1), :],
                            V_h[:, t, :].unsqueeze(1)).then_inc(v_lo, 1)
                w = (n % NT + 1) * P
                e1, e2 = E1[n % 2][:, 0:w], E2[n % 2][:, 0:w]
                pool.wait_ge(mix_ready, STEPS0 * it + n + 1)
                pool.nop(nofuse=True)
                nc.gpsimd.tensor_scalar(e2, e2, mixc[:, n % 4:n % 4 + 1], 1.0, ALU.mult,
                                        ALU.mult).then_inc(mix_scaled, 1)
                pool.wait_ge(mix_scaled, STEPS0 * it + n + 1)
                nc.gpsimd.tensor_tensor(e1, e1, e2, ALU.add).then_inc(p_ready, 1)
                if n == NT:
                    split_wa(it + 1)

        def add_bias(src, row):
            nc.gpsimd.tensor_tensor(X[:], src[:], rows_bc[:, row, :].unsqueeze(1).to_broadcast([P, NT, HID]),
                                    ALU.add).then_inc(xb_done, 1)

        def attn0_out(b):
            pool.wait_ge(wo_in, 64 * b + 64)
            pool.nop(nofuse=True)
            for q in range(4):
                for c in range(KC):
                    w = Wo_raw[:, tile(q, 4), :].rearrange("p (h c) n -> p c h n", c=KC)[:, c]
                    nc.gpsimd.tensor_scalar(w, w, subln[:, c:c + 1], 1.0, ALU.mult, ALU.mult).then_inc(wo_scaled, 1)

        def ffn(b, c0, chunks):
            def split(c, j):
                pool.wait_ge(fw_hi, b * CHUNKS + c + 1)
                low(Fw_l[j][:], Fw_raw[j % 2][:], Fw_h[j][:]).then_inc(fw_lo, 1)

            def body(q, last):
                for j in range(QUAD):
                    c = q * QUAD + (c0 + j)
                    if not (last and j == QUAD - 1):
                        split(c + 1, (j + 1) % QUAD)
                    for h in range(2):
                        n = tile(h, HALF)
                        pool.wait_ge(h_hi, 2 * (b * CHUNKS + c) + h + 1)
                        low(H_l[j % 2][:, n], Hf[j % 2][:, n], H_h[j % 2][:, n]).then_inc(h_lo, 1)

            split(c0, 0)
            quads(pool, chunks // QUAD, body)

        def split_wb(it):
            pool.wait_ge(wb_hi, it + 1)
            low(Wb_l[:], Wb_raw[:], Wb_h[:]).then_inc(wb_lo, 1)

        def stack1(p, h, it):
            pool.wait_ge(uk_neg, 4 * it + 2 * p + h + 1)
            nc.gpsimd.tensor_tensor(KS[:, p, tile(h, HALF)], st_k[:], neg_k[:].bitcast(F32), ALU.add).then_inc(ks_done, 1)

        def head_values(j, col):
            pool.nop(nofuse=True)
            nc.gpsimd.tensor_copy(Vs[:, :, j, 0:D1], V1[:, :, bass.ds(col, D1)]).then_inc(vs_done, 1)

        def attn1_group(b, g):
            it = b * GROUPS1 + g
            for j in range(4):
                if j == 1:
                    split_wb(it + 1)
                for kind, n in slot1(j, False):
                    if kind == "zk":
                        stack1(1 if j == 0 else 0, n, it + (0 if j == 0 else 1))
                pool.wait_ge(pv1_done, 3 * (it * 4 + j) + 3 + 3)
                head_values(j, (g + 1) * 4 * D1 + j * D1)

        pool.sem_inc(fw_lo, 2)
        pool.sem_inc(h_lo, 4)
        pool.sem_inc(gu_used, 2)
        pool.sem_inc(down_mm, 2)
        for free in (a_used, t_used):
            pool.sem_inc(free, 2)
        pool.sem_inc(pv1_done, 3)
        for free in (ks_done, qs_done, *ots_done, o1_done):
            pool.sem_inc(free, 1)
        pool.sem_inc(out_done, 1)
        pool.sem_inc(sq_done, 1)
        split_wa(0)
        with pool.Fori(0, B) as b:
            pool.wait_ge(const_in, CONSTS * 16)
            pool.wait_ge(x_in, 16 * b + 16)
            pool.wait_ge(out_done, 16 * b + 1)
            add_bias(Xn, 0)
            with pool.Fori(0, GROUPS0) as g:
                attn0_group(b, g)
            attn0_out(b)
            ffn(b, 0, CH_F0)
            pool.wait_ge(wv_hi, b + 1)
            low(Wv_l[:], Wv_raw[:], Wv_h[:]).then_inc(wv_lo, 1)
            split_wb(b * GROUPS1)
            for h in range(2):
                stack1(0, h, b * GROUPS1)
            pool.wait_ge(qs_zero, 3 * b + 3)
            pool.wait_ge(v1_done, NT * b + NT)
            for j in range(4):
                head_values(j, j * D1)
            with pool.Fori(0, GROUPS1 - 1) as g:
                attn1_group(b, g)
            for h in range(2):
                stack1(1, h, b * GROUPS1 + (GROUPS1 - 1))
            pool.wait_ge(xt_ps, LN_B // 2 * b + 12)
            add_bias(X, 1)
            pool.wait_ge(rw_in, 16 * b + 16)
            pool.wait_ge(rw_hi, b + 1)
            low(Rw_l[:], Rw_raw[:], Rw_h[:]).then_inc(rw_lo, 1)
            ffn(b, CH_F0, CH_SHARED + CH_ROUTED)


def kernel(**inputs):
    import concourse.bacc as bacc
    from concourse.bass_utils import run_bass_kernel_spmd

    f32 = np.float32
    a = {k: np.asarray(v) for k, v in inputs.items()}

    def rows(w):
        return w.T.reshape(-1, P, w.shape[0]).transpose(1, 0, 2)

    w, bias = a["L0_attn_Wqkv_w"], a["L0_attn_Wqkv_b"]
    nq, nk = 2 * HEADS0 * D0, 2 * GROUPS0 * D0
    wa, ba, bva = [], [], []
    for g in [*range(GROUPS0), 0]:
        k, v = slice(nq + g * E0, nq + (g + 1) * E0), slice(nq + nk + g * E0, nq + nk + (g + 1) * E0)
        q = slice(g * 2 * E0, (g + 1) * 2 * E0)
        wa.append(rows(np.concatenate([w[k], w[q], w[v]])))
        ba.append(np.concatenate([bias[k], bias[q]]).reshape(6, P).T)
        bva.append(bias[v])

    wb, bb = [], []
    low_q, low_k = slice(D1, 2 * D1), slice(SLOT1 - D1, SLOT1)
    max_rows, alibi_rows = slice(MAX_ROW, MAX_ROW + 2), slice(MAX_ROW + 2, MAX_ROW + 4)
    for g in range(GROUPS1):
        cols, bcols = np.zeros((HID, 4 * P), f32), np.zeros((4 * P,), f32)
        for s, (wn, bn) in enumerate((("L1_attn_Wq", "L1_attn_bq"), ("L1_attn_Wk", "L1_attn_bk"))):
            for j in range(4):
                src = slice((4 * g + j) * D1, (4 * g + j + 1) * D1)
                at = s * 2 * P + j * SLOT1
                for r in (0, D1, low_k.start):
                    cols[:, at + r:at + r + D1] = a[wn][:, src]
                    bcols[at + r:at + r + D1] = a[bn][src]
                ones = (alibi_rows, max_rows)[s]
                bcols[at + ones.start:at + ones.stop] = 1.0
        wb.append(cols.reshape(KC, P, 4 * P).transpose(1, 0, 2))
        bb.append(bcols.reshape(4, P).T)
    bsel = np.zeros((P, 2), f32)
    slopes_start = 2.0 ** (-2.0 ** -(np.log2(HEADS1) - 3))
    slopes = np.array([slopes_start * slopes_start ** i for i in range(HEADS1)], f32)
    ramp = -slopes[:, None] * (T - 1 - np.arange(T, dtype=f32))[None, :] / f32(SCALE1)
    alibi = np.zeros((GROUPS1, P, 2, T), f32)
    for j in range(2):
        at = j * SLOT1
        bsel[at + low_q.start:at + low_q.stop, 0] = -1.0
        bsel[at + low_k.start:at + low_k.stop, 1] = -1.0
        bsel[at + alibi_rows.start + 1, 1] = -1.0
        for g in range(GROUPS1):
            for p in range(2):
                alibi[g, at + alibi_rows.start:at + alibi_rows.stop, p, :] = ramp[4 * g + 2 * p + j]

    def chunks(gate, up):
        return [np.concatenate([rows(g).reshape(P, -1), rows(u).reshape(P, -1)], axis=1)
                for g, u in zip(gate.reshape(-1, P, HID), up.reshape(-1, P, HID))]

    w12 = a["L1_ffn_w12"]
    fa = chunks(a["L0_ffn_W1"], a["L0_ffn_W3"]) + chunks(a["L1_ffn_sw1"], a["L1_ffn_sw2"]) \
        + chunks(w12[:, :P].reshape(-1, HID), w12[:, P:].reshape(-1, HID))
    fb = np.concatenate([a["L1_ffn_sw3"].T.reshape(-1, P, HID), a["L1_ffn_w3"].transpose(0, 2, 1)])
    rw = np.zeros((P, KC, P), f32)
    rw[:, :, 0:EXPERTS] = rows(a["L1_ffn_router_w"])
    hada = np.ones((1, 1), f32)
    while hada.shape[0] < P:
        hada = np.block([[hada, hada], [hada, -hada]])

    arrays = {
        "x": a["L0_attn_hidden_states"],
        "wa": np.stack(wa), "ba": np.stack(ba), "bva": np.stack(bva),
        "lam": np.stack([a[f"L0_attn_lambda_{n}"] for n in ("q1", "k1", "q2", "k2")]),
        "subln": a["L0_attn_subln_w"].reshape(KC, P).T,
        "wo0": rows(a["L0_attn_out_w"]),
        "rows": np.stack([a["L0_attn_out_b"], a["L1_attn_bo"], a["L1_attn_bv"]]),
        "w2": rows(a["L0_ffn_W2"]),
        "fa": np.stack(fa), "fb": fb, "rw": rw, "rbias": a["L1_ffn_expert_bias"],
        "wb": np.stack(wb), "bb": np.stack(bb), "bsel": bsel, "alibi": alibi,
        "isum": np.tile(np.eye(32, dtype=f32), (4, 1)),
        "wvo": np.stack([a[n].reshape(KC, P, HID).transpose(1, 0, 2) for n in ("L1_attn_Wv", "L1_attn_Wo")], axis=1),
        "ident": np.eye(P, dtype=f32),
        "mask": np.triu(np.full((P, P), -1e30, f32), 1),
        "hada": hada.astype(f32),
        "first": np.arange(EXPERTS, 0, -1).astype(f32),
    }
    arrays = {f"in_{k}": np.ascontiguousarray(v) for k, v in arrays.items()}
    nc = bacc.Bacc("TRN2", target_bir_lowering=False, num_devices=1)
    d = {k[3:]: nc.dram_tensor(k, v.shape, F32, kind="ExternalInput").ap() for k, v in arrays.items()}
    d["out"] = nc.dram_tensor("out", (B, T, HID), F32, kind="ExternalOutput").ap()
    d["w2s"] = nc.dram_tensor("w2s", (CH_F0, P, HID), F32, kind="Internal").ap()
    d["combs"] = nc.dram_tensor("combs", (NT * EXPERTS, P), F32, kind="Internal").ap()
    build(nc, d)
    r = run_bass_kernel_spmd(nc, [arrays], core_ids=[0])
    return r.results[0]["out"]
```

```python
from contextlib import ExitStack

import numpy as np

import concourse.bass as bass
from concourse import mybir

F32 = mybir.dt.float32
F32R = mybir.dt.float32r
BF16 = mybir.dt.bfloat16
ACT = mybir.ActivationFunctionType
ALU = mybir.AluOpType
AX = mybir.AxisListType

P = 128
B, T, HID = 2, 1024, 256
NT = T // P
KC = HID // P
HALF = 512
EPS = 1e-5

D0 = 128
GROUPS0 = 4
HEADS0 = 8
E0 = 2 * D0
LAMBDA_INIT = float(0.8 - 0.6 * np.exp(-0.3 * 1))
SCALE0 = float(D0 ** -0.5)
PROJ0 = 2 * D0 + 2 * 2 * D0 + E0
UNITS0 = 12
SPLIT_STEPS = (8, 9, 10, 11)
STEPS0 = 2 * NT

HEADS1, D1 = 16, 16
GROUPS1 = 4
SLOT1 = 64
PIECES1 = 12
MAX_ROW = 32
SCALE1 = float(D1 ** -0.5)

CH_F0, CH_SHARED, CH_ROUTED = 8, 8, 8
EXPERTS = 8
CHUNKS = CH_F0 + CH_SHARED + CH_ROUTED
QUAD = 4
FFN_COLS = 2 * KC * P + HID


def build(nc, d):
    with ExitStack() as ctx:
        program(nc, d, ctx)


def program(nc, d, ctx):
    def sem(name):
        return ctx.enter_context(nc.semaphore(name))

    def sb(name, shape, dt=F32, scope=ctx):
        return scope.enter_context(nc.sbuf_tensor(name, shape, dt))

    ps = [ctx.enter_context(nc.psum_tensor(f"ps{i}", [P, 2 * HALF], F32)) for i in range(4)]
    ring = [ps[0][:, 0:HALF], ps[0][:, HALF:], ps[1][:, 0:HALF], ps[1][:, HALF:]]
    xt_bank = [ps[2][:, 0:HALF], ps[2][:, HALF:], ps[3][:, 0:HALF], ps[3][:, HALF:]]

    X = sb("X", [P, NT, HID])
    XT_h = sb("XT_h", [P, KC, T], F32R)
    XT_l = sb("XT_l", [P, KC, T], F32R)
    ident = sb("ident", [P, P])
    ident_bf = sb("ident_bf", [P, P], BF16)
    mask_bf = sb("mask_bf", [P, P], BF16)
    rows_bc = sb("rows_bc", [P, 3, HID])
    subln = sb("subln", [P, KC])
    eps_col = sb("eps_col", [P, 1])
    bsel = sb("bsel", [P, 2])
    rbias = sb("rbias", [P, EXPERTS])
    first = sb("first", [P, EXPERTS])
    neglam = sb("neglam", [P, 1])
    Wa_raw = sb("Wa_raw", [P, KC, PROJ0])
    Wa_h = sb("Wa_h", [P, KC, PROJ0], F32R)
    Wa_l = sb("Wa_l", [P, KC, PROJ0], F32R)
    ba = sb("ba", [P, 6])
    bva = sb("bva", [P, E0])
    st = sb("st", [P, NT, 6])
    mv = sb("mv", [P, NT, 2])
    sd = sb("sd", [P, NT])
    rstd = sb("rstd", [P, NT])

    with ExitStack() as s:
        mask_raw = sb("mask_raw", [P, P], F32, s)
        lam_in = sb("lam_in", [P, 4, D0], F32, s)
        lam_prod = sb("lam_prod", [P, 2, D0], F32, s)
        lam_sum = sb("lam_sum", [P, 2], F32, s)
        lam_exp = sb("lam_exp", [P, 2], F32, s)
        hada_raw = sb("hada_raw", [P, P], F32, s)
        hada = sb("hada", [P, P], F32R, s)
        w2a = sb("w2a", [P, CH_F0, HID], F32, s)
        w2b = sb("w2b", [P, CH_F0, HID], F32, s)
        w2_h = sb("w2_h", [P, CH_F0, HID], F32R, s)
        w2_l = sb("w2_l", [P, CH_F0, HID], F32R, s)

    with ExitStack() as s:
        O = sb("O", [P, NT, 4, E0], F32, s)
        ssq = sb("ssq", [P, 2 * STEPS0], F32, s)
        orms = sb("orms", [P, 2, STEPS0], F32, s)
        orstd = sb("orstd", [P, STEPS0], F32, s)
        K_h = sb("K_h", [P, 2, T], F32R, s)
        K_l = sb("K_l", [P, 2, T], F32R, s)
        Q_h = sb("Q_h", [P, 2, 2, T], F32R, s)
        Q_l = sb("Q_l", [P, 2, 2, T], F32R, s)
        V_h = sb("V_h", [P, NT, E0], F32R, s)
        V_l = sb("V_l", [P, NT, E0], F32R, s)
        E1 = [sb(f"E1_{i}", [P, T], F32, s) for i in range(2)]
        E2 = [sb(f"E2_{i}", [P, T], F32, s) for i in range(2)]
        PT_h = [sb(f"PT_h{i}", [P, T], F32R, s) for i in range(2)]
        PT_l = [sb(f"PT_l{i}", [P, T], F32R, s) for i in range(2)]
        nmax = sb("nmax", [P, 4, 2], F32, s)
        lsum = sb("lsum", [P, 4, 2], F32, s)
        rsum = sb("rsum", [P, 8, 2], F32, s)
        mixc = sb("mixc", [P, 4], F32, s)
        sq_junk = sb("sq_junk", [P, E0], F32, s)
        Wo_raw = sb("Wo_raw", [P, 4, HID], F32, s)
        Wo_h = sb("Wo_h", [P, 4, HID], F32R, s)
        Wo_l = sb("Wo_l", [P, 4, HID], F32R, s)
        On = [sb(f"On{i}", [P, 2, E0], F32, s) for i in range(2)]
        OT_h = [sb(f"OT_h{i}", [P, 4, P], F32R, s) for i in range(2)]
        OT_l = [sb(f"OT_l{i}", [P, 4, P], F32R, s) for i in range(2)]

    s = ctx
    Vs = sb("Vs", [P, NT, 4, 32], F32, s)
    QS = sb("QS", [P, 4, T], F32R, s)
    nmax1_cols = sb("nmax1_cols", [P, NT, P], F32R, s)
    Wv_raw = sb("Wv_raw", [P, 2, KC, HID], F32, s)
    Wv_h = sb("Wv_h", [P, 2, KC, HID], F32R, s)
    Wv_l = sb("Wv_l", [P, 2, KC, HID], F32R, s)
    Rw_raw = sb("Rw_raw", [P, KC, P], F32, s)
    Rw_h = sb("Rw_h", [P, KC, P], F32R, s)
    Rw_l = sb("Rw_l", [P, KC, P], F32R, s)
    Fw_raw = [sb(f"Fw_raw{i}", [P, FFN_COLS], F32, s) for i in range(2)]
    Fw_h = [sb(f"Fw_h{i}", [P, FFN_COLS], F32R, s) for i in range(QUAD)]
    Fw_l = [sb(f"Fw_l{i}", [P, FFN_COLS], F32R, s) for i in range(QUAD)]
    Wb_raw = sb("Wb_raw", [P, KC, 4 * P], F32, s)
    Wb_h = sb("Wb_h", [P, KC, 4 * P], F32R, s)
    Wb_l = sb("Wb_l", [P, KC, 4 * P], F32R, s)
    with ExitStack() as s:
        silu_g = [sb(f"silu_g{i}", [P, HALF], F32, s) for i in range(2)]
        comb_bc = sb("comb_bc", [P, EXPERTS, NT, P], F32, s)
        Hf = [sb(f"Hf{i}", [P, T], F32, s) for i in range(2)]
        H_h = [sb(f"H_h{i}", [P, T], F32R, s) for i in range(2)]
        H_l = [sb(f"H_l{i}", [P, T], F32R, s) for i in range(2)]
        LG = Hf[0]
        sc = sb("sc", [P, NT, EXPERTS], F32, s)
        sel = sb("sel", [P, NT, EXPERTS], F32, s)
        ta = sb("ta", [P, NT, EXPERTS], F32, s)
        tb = sb("tb", [P, NT, EXPERTS], F32, s)
        comb_oh = sb("comb_oh", [P, 2, NT, EXPERTS], F32, s)
        comb, oh = comb_oh[:, 0], comb_oh[:, 1]
        tm = sb("tm", [P, NT], F32, s)
        combT = sb("combT", [NT * EXPERTS, P], F32, s)
        Xn = sb("Xn", [P, NT, HID], F32, s)
    with ExitStack() as s:
        bb = sb("bb", [P, 4], F32, s)
        alibi = sb("alibi", [P, 2, T], F32, s)
        V1 = sb("V1", [P, NT, HID], F32, s)
        st_k = sb("st_k", [P, HALF], F32, s)
        st_q = sb("st_q", [P, HALF], F32, s)
        neg_k = sb("neg_k", [P, HALF], F32R, s)
        neg_q = sb("neg_q", [P, HALF], F32R, s)
        KS = sb("KS", [P, 2, T], F32R, s)
        PT = sb("PT", [P, PIECES1, HALF], F32, s)
        nmax1 = sb("nmax1", [P, NT], F32, s)
        nmax1_part = sb("nmax1_part", [P, 2, NT // 2], F32, s)
        osum = sb("osum", [P, NT, D1 + 1], F32, s)
        rsum1 = sb("rsum1", [P, NT], F32, s)
        OTs = sb("OTs", [P, T], F32, s)
        O1 = sb("O1", [P, NT, HID], F32, s)
        O1T_h, O1T_l = QS[:, 0:KC], QS[:, KC:2 * KC]

    const_in = sem("const_in")
    w2_in = sem("w2_in")
    x_in = sem("x_in")
    out_done = sem("out_done")
    wa_in = sem("wa_in")
    ba_in = sem("ba_in")
    wo_in = sem("wo_in")
    w2_out = sem("w2_out")
    fw_in = [sem("fw_in0"), sem("fw_in1")]
    wb_in = sem("wb_in")
    wv_in = sem("wv_in")
    rw_in = sem("rw_in")
    combt_out = sem("combt_out")
    comb_in = sem("comb_in")
    pre_dve = sem("pre_dve")
    pre_act = sem("pre_act")
    pre_pe = sem("pre_pe")
    pre_hi = sem("pre_hi")
    w2_ready = sem("w2_ready")
    z_done = sem("z_done")
    ln_st = sem("ln_st")
    ln_ag = sem("ln_ag")
    ln_sd = sem("ln_sd")
    ln_rs = sem("ln_rs")
    ln_done = sem("ln_done")
    xt_ps = sem("xt_ps")
    xt_hi = sem("xt_hi")
    xt_lo = sem("xt_lo")
    xb_done = sem("xb_done")
    wa_scaled = sem("wa_scaled")
    ba_scaled = sem("ba_scaled")
    wa_hi = sem("wa_hi")
    wa_lo = sem("wa_lo")
    pj_mm = sem("pj_mm")
    pj_hi = sem("pj_hi")
    pj_dve = sem("pj_dve")
    v_hi = sem("v_hi")
    v_lo = sem("v_lo")
    s_ready = [sem("s_ready0"), sem("s_ready1")]
    nmax_ready = [sem("nmax_ready0"), sem("nmax_ready1")]
    exp_done = [sem("exp_done0"), sem("exp_done1")]
    rsum_ready = sem("rsum_ready")
    mix_ready = sem("mix_ready")
    mix_scaled = sem("mix_scaled")
    p_ready = sem("p_ready")
    pt_ps = sem("pt_ps")
    pt_hi = sem("pt_hi")
    pt_lo = sem("pt_lo")
    pv_done = sem("pv_done")
    o_done = sem("o_done")
    sq_done = sem("sq_done")
    wo_scaled = sem("wo_scaled")
    wo_hi = sem("wo_hi")
    wo_lo = sem("wo_lo")
    or_var = sem("or_var")
    or_act = sem("or_act")
    or_done = sem("or_done")
    on_done = sem("on_done")
    ot_ps = sem("ot_ps")
    ot_hi = sem("ot_hi")
    ot_lo = sem("ot_lo")
    y_mm = sem("y_mm")
    y_added = sem("y_added")
    y_zero = sem("y_zero")
    y_bank = sem("y_bank")
    fw_hi = sem("fw_hi")
    fw_lo = sem("fw_lo")
    gate_mm = sem("gate_mm")
    up_mm = sem("up_mm")
    silu_done = sem("silu_done")
    gu_used = sem("gu_used")
    hm_done = sem("hm_done")
    h_hi = sem("h_hi")
    h_lo = sem("h_lo")
    down_mm = sem("down_mm")
    rw_hi = sem("rw_hi")
    rw_lo = sem("rw_lo")
    lg_mm = sem("lg_mm")
    lg_copy = sem("lg_copy")
    lg_t = sem("lg_t")
    sig_exp = sem("sig_exp")
    rt_dve = sem("rt_dve")
    ct_ps = sem("ct_ps")
    ct_copy = sem("ct_copy")
    qs_zero = sem("qs_zero")
    wv_hi = sem("wv_hi")
    wv_lo = sem("wv_lo")
    v1_mm = sem("v1_mm")
    v1_done = sem("v1_done")
    vs_done = sem("vs_done")
    wb_hi = sem("wb_hi")
    wb_lo = sem("wb_lo")
    bb_in = sem("bb_in")
    u_mm = sem("u_mm")
    uk_full = sem("uk_full")
    uq_full = sem("uq_full")
    uk_neg = sem("uk_neg")
    uq_neg = sem("uq_neg")
    ks_done = sem("ks_done")
    qs_done = sem("qs_done")
    o_zero = sem("o_zero")
    a_ready = sem("a_ready")
    a_used = sem("a_used")
    nm_both = sem("nm_both")
    nm_hi = sem("nm_hi")
    nm_lo = sem("nm_lo")
    nt_ps = sem("nt_ps")
    n_done = sem("n_done")
    t_ready = sem("t_ready")
    t_used = sem("t_used")
    pv1_done = sem("pv1_done")
    ots_done = [sem("ots_done0"), sem("ots_done1")]
    o_ps = sem("o_ps")
    o_used = sem("o_used")
    rs1_done = sem("rs1_done")
    o1_done = sem("o1_done")
    o1t_ps = sem("o1t_ps")
    o1t_hi = sem("o1t_hi")
    o1t_lo = sem("o1t_lo")
    y1_mm = sem("y1_mm")

    def pass3(pe, out, a_h, a_l, b_h, b_l, start, stop, **kw):
        nc.tensor.matmul(out, a_h, b_h, start=start, stop=False, **kw)
        nc.tensor.matmul(out, a_h, b_l, start=False, stop=False, **kw)
        return nc.tensor.matmul(out, a_l, b_h, start=False, stop=stop, **kw)

    def tile(i, n=P):
        return slice(i * n, (i + 1) * n)

    def key_span(i):
        w = (i + 1) * P
        return [(a, min(max(w, a + 2 * P), a + HALF)) for a in range(0, w, HALF)]

    def v_tiles(s):
        return (2 * s, 2 * s + 1) if s < 2 else (s + 2,) if s + 2 < NT else ()

    def out_bank(t, alone):
        return ps[2 if alone and t % 2 else 3][:, HALF:]

    def root_cols(a, half):
        return a.rearrange("p (h t) -> p h t", h=2)[:, :, tile(half, NT // 2)]

    def v_bank(t):
        return ps[3 - t % 2][:, HALF:HALF + E0]

    def tail0(last):
        u = [("u", i) for i in range(UNITS0)]
        if last:
            return [("t", STEPS0 - 2), ("v", STEPS0 - 3), ("t", STEPS0 - 1), ("v", STEPS0 - 2), ("r", 0), ("o", 0),
                    ("v", STEPS0 - 1)]
        return [("t", STEPS0 - 2), *u[0:2], ("v", STEPS0 - 3), *u[2:4], ("t", STEPS0 - 1), ("v", STEPS0 - 2), ("r", 0),
                *u[4:9], ("v", STEPS0 - 1), *u[9:10], ("r", 1), *u[10:]]

    def out0(s, late):
        t = 2 * (s - NT) + 1
        if s == NT - 1:
            return [] if late else [("t", 0)]
        if not NT <= s < NT + NT // 2:
            return []
        return [("t", i) for i in (t + late,) if i < NT] + [("y", t - 1 + late)]

    def slot1(j, last):
        order = """t0 t1 a0 uk0 uq0 a1 o0 t2 a2 a3 n1 t3 o1 a4 zk0 zq0 uk1 a5 t4 t5 uq1 v0 t6 a6 a7 t7 n0 zq1 t8 zk1 a8
                   a9 t9 v1 t10 a10 t11 a11 v2 c0 c1""".split()
        tokens = [(x.rstrip("0123456789"), int(x.lstrip("abcdefghijklmnopqrstuvwxyz"))) for x in order]
        dropped = set()
        if last and j == 3:
            dropped |= {("a", k) for k in range(PIECES1)} | {("n", 0)}
        if j % 2 == 1 or (last and j == 2):
            dropped |= {(k, h) for k in ("uk", "uq", "zk", "zq") for h in range(2)}
        if j == 0:
            dropped |= {("o", h) for h in range(2)}
        return [t for t in tokens if t not in dropped] + ([("end", 0)] if j == 3 else [])

    FIRST1 = [(x.rstrip("0123456789"), int(x.lstrip("abcdefghijklmnopqrstuvwxyzV"))) for x in
              """V0 uk0 uq0 zk0 zq0 V1 uk1 uq1 V2 zk1 V3 zq1 V4 V5 a0 a1 a2 a3 V6 a4 a5 a6 a7 V7 a8 a9 n0
                 a10 a11""".split()]

    def quads(eng, n, body):
        if n > 2:
            with eng.Fori(0, n - 1) as q:
                body(q, False)
        else:
            body(0, False)
        body(n - 1, True)

    def a_piece(k):
        i, a = (k, 0) if k < 4 else (4 + (k - 4) // 2, (k - 4) % 2 * HALF)
        z = min((i + 1) * P, a + HALF)
        return i, a, z, max(z, a + 2 * P)

    def t_piece(k):
        kb = k % 4 + (4 if k >= 8 else 0)
        half = 0 if k < 4 else HALF
        return kb, max(half, kb * P), half + HALF

    LN_B = 4 * NT
    UNITS_IT = UNITS0 + NT
    R_B = 20
    STORES = 4
    CONSTS = 8

    block = ctx.enter_context(nc.Block())

    @block.sync
    def _(sp):
        def load_wa(g):
            sp.dma_start(Wa_raw[:], d["wa"][g]).then_inc(wa_in, 16)

        def load_ba(g):
            sp.dma_start(ba[:], d["ba"][g]).then_inc(ba_in, 16)
            sp.dma_start(bva[:], d["bva"][g].partition_broadcast(P)).then_inc(ba_in, 16)

        def load_wb(g):
            sp.dma_start(Wb_raw[:], d["wb"][g]).then_inc(wb_in, 16)

        def load_bb(g):
            sp.dma_start(bb[:], d["bb"][g]).then_inc(bb_in, 16)
            sp.dma_start(alibi[:], d["alibi"][g]).then_inc(bb_in, 16)

        def load_chunk(b, c, j, down):
            cc = b * CHUNKS + c
            sp.wait_ge(fw_lo, cc + 1)
            sp.dma_start(Fw_raw[j % 2][:, 0:2 * KC * P], d["fa"][c]).then_inc(fw_in[j % 2], 16)
            sp.dma_start(Fw_raw[j % 2][:, 2 * KC * P:], down).then_inc(fw_in[j % 2], 16)

        def load_x(b):
            sp.dma_start(Xn[:], d["x"][b].rearrange("(t p) n -> p t n", p=P)).then_inc(x_in, 16)

        sp.dma_start(w2a[:], d["w2"]).then_inc(w2_in, 16)
        sp.dma_start(hada_raw[:], d["hada"]).then_inc(w2_in, 16)
        load_x(0)
        for t, src in ((ident, "ident"), (mask_raw, "mask"), (bsel, "bsel"), (subln, "subln")):
            sp.dma_start(t[:], d[src]).then_inc(const_in, 16)
        for t, src in ((rows_bc, "rows"), (lam_in, "lam"), (rbias, "rbias"), (first, "first")):
            sp.dma_start(t[:], d[src].partition_broadcast(P)).then_inc(const_in, 16)
        load_wa(0)
        load_ba(0)
        sp.wait_ge(w2_ready, 4)
        sp.dma_start(d["w2s"].rearrange("c p n -> p c n"), w2b[:]).then_inc(w2_out, 16)
        sp.wait_ge(w2_out, 16)
        with sp.Fori(0, B) as b:
            with sp.Fori(0, GROUPS0) as g:
                it = b * GROUPS0 + g
                sp.wait_ge(wa_lo, 4 * it + 4)
                load_wa(g + 1)
                sp.wait_ge(pj_dve, it * UNITS_IT + UNITS_IT)
                sp.nop(nofuse=True)
                sp.wait_ge(wo_lo, it + 1)
                sp.dma_start(Wo_raw[:], d["wo0"][g]).then_inc(wo_in, 16)
                load_ba(g + 1)
            with sp.Fori(0, CH_F0 // QUAD) as q:
                sp.wait_ge(pv_done, GROUPS0 * STEPS0 * (b + 1))
                for j in range(QUAD):
                    load_chunk(b, q * QUAD + j, j, d["w2s"][q * QUAD + j])
            sp.dma_start(Wv_raw[:], d["wvo"]).then_inc(wv_in, 16)
            sp.dma_start(Rw_raw[:], d["rw"]).then_inc(rw_in, 16)
            load_wb(0)
            sp.wait_ge(z_done, LN_B * b + 2 * NT)
            load_bb(0)
            with sp.Fori(0, GROUPS1 - 1) as g:
                it = b * GROUPS1 + g
                sp.wait_ge(wb_lo, it + 1)
                load_wb(g + 1)
                sp.wait_ge(uk_full, 4 * it + 4)
                sp.wait_ge(uq_full, 4 * it + 4)
                load_bb(g + 1)
            for c in range(2):
                load_chunk(b, CH_F0 + c, c, d["fb"][c])
            sp.wait_ge(z_done, LN_B * b + 3 * NT)
            load_x(B - 1)
            for c in range(2, CH_SHARED):
                if c == QUAD:
                    sp.wait_ge(ct_copy, b + 1)
                    sp.dma_start(d["combs"], combT[:]).then_inc(combt_out, 16)
                    sp.wait_ge(combt_out, 16 * b + 16)
                    for e in range(EXPERTS):
                        src = d["combs"].rearrange("(t e) p -> e t p", e=EXPERTS)[e]
                        sp.dma_start(comb_bc[:, e], src.partition_broadcast(P)).then_inc(comb_in, 16)
                load_chunk(b, CH_F0 + c, c, d["fb"][c])
            with sp.Fori(0, CH_ROUTED // QUAD) as q:
                for j in range(QUAD):
                    e = q * QUAD + j
                    load_chunk(b, CH_F0 + CH_SHARED + e, j, d["fb"][CH_SHARED + e])
            for q in range(STORES):
                sp.wait_ge(ln_done, LN_B * b + LN_B - NT + (q + 1) * (NT // STORES))
                t = slice(q * (NT // STORES), (q + 1) * (NT // STORES))
                sp.dma_start(d["out"][b].rearrange("(t p) n -> p t n", p=P)[:, t], X[:, t]).then_inc(out_done, 16)
        sp.wait_ge(out_done, 16 * STORES * B + 1)

    @block.tensor
    def _(pe):
        def transpose_x(b, k, h):
            for j in (2 * h, 2 * h + 1):
                if k == 0:
                    pe.wait_ge(const_in, CONSTS * 16)
                    pe.wait_ge(x_in, 16 * b + 16)
                    pe.wait_ge(gu_used, 2 * CHUNKS * b + 2)
                else:
                    pe.wait_ge(ln_done, LN_B * b + NT * (k - 1) + 2 * j + 2)
                for c in range(KC):
                    for r in range(2):
                        mm = nc.tensor.transpose(xt_bank[j][:, c * 2 * P + r * P:c * 2 * P + (r + 1) * P],
                                                 (X if k else Xn)[:, 2 * j + r, tile(c)], ident[:])
                mm.then_inc(xt_ps, 1)

        def wait_xt(b, k, h=1):
            pe.wait_ge(xt_lo, LN_B // 2 * b + 4 * k + 2 * h + 2)

        def project0(it, u):
            if u == 0:
                pe.wait_ge(wa_lo, 4 * it + 4)
            if u < UNITS0:
                if u >= 4:
                    pe.wait_ge(pj_dve, UNITS_IT * it + u - 3)
                w, n = tile(u // 2), tile(u % 2, HALF)
                for c in range(KC):
                    mm = pass3(pe, ring[u % 4], Wa_h[:, c, w], Wa_l[:, c, w], XT_h[:, c, n], XT_l[:, c, n],
                               c == 0, c == KC - 1)
            else:
                t, w = u - UNITS0, slice(UNITS0 // 2 * P, PROJ0)
                if t >= 2:
                    pe.wait_ge(pj_dve, UNITS_IT * it + u - 1)
                for c in range(KC):
                    mm = pass3(pe, v_bank(t), XT_h[:, c, tile(t)], XT_l[:, c, tile(t)],
                               Wa_h[:, c, w], Wa_l[:, c, w], c == 0, c == KC - 1)
            mm.then_inc(pj_mm, 1)

        def out_transpose(it, t, alone=False):
            pe.wait_ge(on_done, NT * it + t + 1)
            if t >= (2 if alone else 1):
                pe.wait_ge(ot_lo, NT * it + t - (1 if alone else 0))
            for c in range(4):
                mm = nc.tensor.transpose(out_bank(t, alone)[:, tile(c)], On[t % 2][:, c // 2, tile(c % 2)],
                                         ident[:])
            mm.then_inc(ot_ps, 1)

        def out_product(it, t):
            if t == 0:
                pe.wait_ge(wo_lo, it + 2)
            pe.wait_ge(ot_lo, NT * it + t + 1)
            for c in range(4):
                mm = pass3(pe, ring[t % 2 * 2 + 1][:, 0:HID], OT_h[t % 2][:, c, :], OT_l[t % 2][:, c, :], Wo_h[:, c, :],
                           Wo_l[:, c, :], c == 0, c == 3)
            mm.then_inc(y_mm, 1)

        def attn0_group(b, g, out, last):
            it = b * GROUPS0 + g

            def project_out(s, late):
                for kind, t in out0(s, late) if out else ():
                    if kind == "t":
                        out_transpose(it - 1, t)
                    else:
                        if t >= 2:
                            pe.wait_ge(y_added, 3 * NT * b + NT * (g - 1) + t - 1)
                        out_product(it - 1, t)

            def scores(n):
                h, i = n // NT, n % NT
                if out and n == NT + NT // 2:
                    pe.wait_ge(y_added, 3 * NT * b + NT * g)
                if n == 0:
                    pe.wait_ge(pj_dve, UNITS_IT * it + UNITS0)
                for m in range(2):
                    if n >= 1:
                        pe.wait_ge(exp_done[m], STEPS0 * it + n)
                    for a, z in key_span(i):
                        mm = pass3(pe, ps[m][:, a:z], Q_h[:, h, m, tile(i)], Q_l[:, h, m, tile(i)],
                                   K_h[:, m, a:z], K_l[:, m, a:z], True, True)
                    mm = nc.tensor.matmul(ps[m][:, tile(i)], ident_bf[:], mask_bf[:],
                                          start=False, stop=True, skip_group_check=True)
                    mm.then_inc(s_ready[m], 1)

            def weigh_values(n):
                i = n % NT
                if n < NT:
                    pe.wait_ge(v_lo, NT * it + n + 1)
                pe.wait_ge(pt_lo, STEPS0 * it + n + 1)
                if n >= 1:
                    pe.wait_ge(o_done, STEPS0 * it + n)
                for kb in range(i + 1):
                    mm = pass3(pe, ps[3][:, 0:E0], PT_h[n % 2][:, tile(kb)], PT_l[n % 2][:, tile(kb)], V_h[:, kb, :], V_l[:, kb, :],
                               kb == 0, kb == i)
                mm.then_inc(pv_done, 1)

            def transpose_p(n):
                pe.wait_ge(p_ready, STEPS0 * it + n + 1)
                if n >= 1:
                    pe.wait_ge(pt_lo, STEPS0 * it + n)
                if n == NT // 2:
                    pe.wait_ge(pj_dve, UNITS_IT * it + UNITS_IT)
                for kb in range(n % NT + 1):
                    mm = nc.tensor.transpose(ps[2][:, tile(kb)], E1[n % 2][:, tile(kb)], ident[:])
                mm.then_inc(pt_ps, 1)

            for s in range(STEPS0):
                if s >= 2:
                    transpose_p(s - 2)
                if s == 0:
                    for t in v_tiles(s):
                        project0(it, UNITS0 + t)
                if s != NT:
                    scores(s)
                for t in v_tiles(s) if s else ():
                    project0(it, UNITS0 + t)
                project_out(s, 0)
                if s >= 3:
                    weigh_values(s - 3)
                if s == NT:
                    scores(s)
                project_out(s, 1)
            for kind, n in tail0(last):
                if kind == "u":
                    if n % 2 == 0 and n < 4:
                        pe.wait_ge(exp_done[n // 2], STEPS0 * it + STEPS0)
                    project0(it + 1, n)
                elif kind == "t":
                    transpose_p(n)
                elif kind == "o":
                    out_transpose(it, n, True)
                elif kind == "v":
                    weigh_values(n)

        def attn0_out(b):
            it = b * GROUPS0 + GROUPS0 - 1
            for t in range(NT):
                if t + 1 < NT:
                    out_transpose(it, t + 1, True)
                if t >= 2:
                    pe.wait_ge(z_done, LN_B * b + t - 1)
                out_product(it, t)

        def gate_up(b, c, j, layer=None):
            cc = b * CHUNKS + c
            pe.wait_ge(fw_lo, cc + 3)
            for h in range(2):
                if layer == 0:
                    transpose_x(b, 1, h)
                    wait_xt(b, 1, h)
                pe.wait_ge(gu_used, 2 * cc + h + 1)
                for k, ready in ((0, gate_mm), (1, up_mm)):
                    for kc in range(KC):
                        w, n = tile(k * KC + kc), tile(h, HALF)
                        mm = pass3(pe, ps[2 + h][:, tile(k, HALF)], Fw_h[j][:, w], Fw_l[j][:, w],
                                   XT_h[:, kc, n], XT_l[:, kc, n], kc == 0, kc == KC - 1)
                    mm.then_inc(ready, 1)

        def down(b, c, j):
            cc = b * CHUNKS + c
            w = slice(2 * KC * P, FFN_COLS)
            for t in range(NT):
                if t % 4 == 0:
                    pe.wait_ge(h_lo, 2 * cc + t // 4 + 5)
                mm = pass3(pe, ring[t // 2][:, tile(t % 2, HID)], H_h[j % 2][:, tile(t)], H_l[j % 2][:, tile(t)],
                           Fw_h[j][:, w], Fw_l[j][:, w], False, True, skip_group_check=True)
                if t in (1, 3, 5):
                    mm.then_inc(y_bank, 1)
            mm.then_inc(down_mm, 1)

        def ffn(b, layer, c0, chunks):
            def body(q, last):
                for j in range(QUAD):
                    c = q * QUAD + (c0 + j)
                    if not (last and j == QUAD - 1):
                        gate_up(b, c + 1, (j + 1) % QUAD)
                    if j == 0:
                        pe.wait_ge(y_zero, 3 * b + 2 * layer + 1)
                    down(b, c, j)

            gate_up(b, c0, 0, layer)
            if layer == 1:
                router_weights(b)
            quads(pe, chunks // QUAD, body)

        def values1(b, t):
            if t == 0:
                pe.wait_ge(wv_lo, b + 1)
                wait_xt(b, 2, 0)
            if t >= 2:
                pe.wait_ge(v1_done, NT * b + t - 1)
            for c in range(KC):
                mm = pass3(pe, ring[2 + t % 2][:, 0:HID], XT_h[:, c, tile(t)], XT_l[:, c, tile(t)], Wv_h[:, 0, c, :],
                           Wv_l[:, 0, c, :], c == 0, c == KC - 1)
            mm.then_inc(v1_mm, 1)

        def stack1(kind, p, h, it, heads_out):
            if kind == "uk":
                if h == 0:
                    pe.wait_ge(wb_lo, it + 1)
                if not (p == 0 and h == 0):
                    pe.wait_ge(uk_full, 4 * it + 2 * p + h)
                pe.wait_ge(o_used, 2 * heads_out + 1)
            elif h == 1:
                pe.wait_ge(uq_full, 4 * it + 2 * p + 1)
            w, n = tile(p + (2 if kind == "uk" else 0)), tile(h, HALF)
            bank = ps[3][:, HALF:] if kind == "uk" else ps[3][:, 0:HALF]
            for c in range(KC):
                mm = pass3(pe, bank, Wb_h[:, c, w], Wb_l[:, c, w], XT_h[:, c, n], XT_l[:, c, n], c == 0, c == KC - 1)
            mm.then_inc(u_mm, 1)

        def score_piece(H, j, k):
            if k == 0 and j % 2 == 0:
                pe.wait_ge(ks_done, H + 3)
                pe.wait_ge(qs_done, H + 3)
            pe.wait_ge(a_used, PIECES1 * H + k + 1)
            i, a, z, scored = a_piece(k)
            bank = ps[0][:, tile(k % 2, HALF)]
            mm = nc.tensor.matmul(bank[:, 0:scored - a], QS[:, j, tile(i)], KS[:, j // 2, a:scored], start=True, stop=True)
            if z == (i + 1) * P:
                mm = nc.tensor.matmul(bank[:, z - P - a:z - a], ident_bf[:], mask_bf[:], start=False, stop=True,
                                      skip_group_check=True)
            mm.then_inc(a_ready, 1)

        def max_rows(H, h):
            pe.wait_ge(nm_lo, 2 * H + h + 1)
            for i in range(4):
                mm = nc.tensor.transpose(ps[3][:, tile(i)], nmax1_cols[:, 4 * h + i, :].bitcast(F32), ident[:])
            mm.then_inc(nt_ps, 1)

        def attn1_group(b, g, last):
            it = b * GROUPS1 + g

            def score_piece_t(H, j, k):
                if k in (0, 4):
                    pe.wait_ge(n_done, 2 * H + (2 if k else 1))
                pe.wait_ge(t_used, PIECES1 * H + k + 1)
                kb, a, z = t_piece(k)
                bank, base = ps[1][:, tile(k % 2, HALF)], z - HALF
                n = min(a, z - 2 * P)
                mm = nc.tensor.matmul(bank[:, n - base:], KS[:, j // 2, tile(kb)], QS[:, j, n:z], start=True, stop=True)
                if a == kb * P:
                    mm = nc.tensor.matmul(bank[:, a - base:a - base + P], mask_bf[:], ident_bf[:], start=False, stop=True,
                                          skip_group_check=True)
                mm.then_inc(t_ready, 1)

            def weigh_values(H, j, rd):
                pe.wait_ge(t_used, PIECES1 * H + 4 * rd + 4 + 2)
                if rd == 0:
                    pe.wait_ge(vs_done, H + 1)
                if rd < 2:
                    pe.wait_ge(ots_done[rd], H + 1)
                for c in range(4):
                    kb, a, z = t_piece(4 * rd + c)
                    mm = nc.tensor.matmul(ps[2][32 * c:32 * c + 32, a:z], Vs[:, kb, j, :],
                                          PT[:, 4 * rd + c, a - (z - HALF):], start=rd < 2, stop=True,
                                          skip_group_check=rd == 2, tile_position=(0, 32 * c))
                mm.then_inc(pv1_done, 1)

            def output(H, h, pieces):
                if h == 0:
                    pe.wait_ge(uk_full, pieces)
                pe.wait_ge(o_used, 2 * H + h + 1)
                pe.wait_ge(ots_done[h], H + 2)
                for t in range(4):
                    mm = nc.tensor.transpose(ps[3][:, HALF + t * P:HALF + (t + 1) * P], OTs[:, tile(4 * h + t)], ident[:])
                mm.then_inc(o_ps, 1)

            for j in range(4):
                H = it * 4 + j
                pieces = 4 * it + (2 if j < 1 else 4)
                stacked = 0
                for kind, n in slot1(j, last):
                    if kind == "a":
                        score_piece(H + 1, (j + 1) % 4, n)
                    elif kind == "t":
                        score_piece_t(H, j, n)
                    elif kind in ("uk", "uq"):
                        stack1(kind, 1 if j == 0 else 0, n, it + (0 if j == 0 else 1), H - (1 if j == 2 and n == 0 else 0))
                        stacked += kind == "uk"
                    elif kind == "n":
                        if stacked:
                            pe.wait_ge(uq_full, pieces + 2 - n)
                        pe.wait_ge(n_done, 2 * H + 2 - n)
                        max_rows(H + 1 - n, n)
                    elif kind == "v":
                        weigh_values(H, j, n)
                    elif kind == "o":
                        output(H - 1, n, pieces + stacked)
                    elif kind == "end":
                        for h in range(2):
                            output(H, h, pieces + (0 if last else 2))

        def attn1_out(b):
            pe.wait_ge(o1_done, HEADS1 * b + HEADS1 + 1)
            for j in range(NT // 2):
                for c in range(KC):
                    for r in range(2):
                        mm = nc.tensor.transpose(xt_bank[j][:, c * 2 * P + r * P:c * 2 * P + (r + 1) * P],
                                                 O1[:, 2 * j + r, tile(c)], ident[:])
                mm.then_inc(o1t_ps, 1)
            for t in range(NT):
                pe.wait_ge(o1t_lo, 4 * b + t // 2 + 1)
                for c in range(KC):
                    mm = pass3(pe, ring[t // 2][:, tile(t % 2, HID)], O1T_h[:, c, tile(t)], O1T_l[:, c, tile(t)],
                               Wv_h[:, 1, c, :], Wv_l[:, 1, c, :], c == 0, c == KC - 1)
                mm.then_inc(y1_mm, 1)

        def router(b):
            pe.wait_ge(rw_lo, b + 1)
            for h in range(2):
                transpose_x(b, 3, h)
                wait_xt(b, 3, h)
                for c in range(KC):
                    n = tile(h, HALF)
                    mm = pass3(pe, ps[0][:, n], Rw_h[:, c, :], Rw_l[:, c, :], XT_h[:, c, n], XT_l[:, c, n],
                               c == 0, c == KC - 1)
                mm.then_inc(lg_mm, 1)
            for t in range(NT):
                if t % 4 == 0:
                    pe.wait_ge(lg_copy, 2 * b + t // 4 + 1)
                mm = nc.tensor.transpose(ps[1][:, tile(t)], LG[:, tile(t)], ident[:])
            mm.then_inc(lg_t, 1)

        def router_weights(b):
            pe.wait_ge(rt_dve, R_B * b + R_B)
            nc.tensor.transpose(ps[0][:, 0:P], comb_oh[:].rearrange("p a t e -> p (a t e)"), ident[:]).then_inc(ct_ps, 1)
        for h in range(2):
            transpose_x(0, 0, h)
        pe.wait_ge(pre_dve, 8)
        for q in range(4):
            n = tile(q, 2)
            pe.wait_ge(xt_lo, q + 1)
            nc.tensor.matmul(xt_bank[q], hada[:], w2_h[:, n, :], start=True, stop=False)
            nc.tensor.matmul(xt_bank[q], hada[:], w2_l[:, n, :], start=False, stop=True).then_inc(pre_pe, 1)
        with pe.Fori(0, B) as b:
            wait_xt(b, 0)
            for u in range(UNITS0):
                project0(b * GROUPS0, u)
            pe.wait_ge(w2_ready, 4)
            pe.wait_ge(pre_dve, 13)
            attn0_group(b, 0, False, False)
            with pe.Fori(1, GROUPS0 - 1) as g:
                attn0_group(b, g, True, False)
            attn0_group(b, GROUPS0 - 1, True, True)
            attn0_out(b)
            ffn(b, 0, 0, CH_F0)
            transpose_x(b, 2, 0)
            for kind, n in FIRST1:
                if kind == "uk" and n == 0:
                    transpose_x(b, 2, 1)
                    wait_xt(b, 2)
                if kind in ("uk", "uq"):
                    stack1(kind, 0, n, b * GROUPS1, b * HEADS1)
                elif kind == "V":
                    values1(b, n)
                elif kind == "a":
                    if n == PIECES1 - 1:
                        pe.wait_ge(o_zero, b + 1)
                        pe.wait_ge(v1_done, NT * b + NT)
                    score_piece(b * HEADS1, 0, n)
                elif kind == "n":
                    pe.wait_ge(uq_full, 4 * GROUPS1 * b + 2)
                    max_rows(b * HEADS1, n)
            with pe.Fori(0, GROUPS1 - 1) as g:
                attn1_group(b, g, False)
            attn1_group(b, GROUPS1 - 1, True)
            attn1_out(b)
            router(b)
            ffn(b, 1, CH_F0, CH_SHARED + CH_ROUTED)
            for h in range(2):
                transpose_x(b + 1, 0, h)

    @block.scalar
    def _(act):
        def x_parts(b, k, h):
            for j in (2 * h, 2 * h + 1):
                act.wait_ge(xt_ps, LN_B // 2 * b + 4 * k + j + 1)
                nc.scalar.copy(XT_h[:, :, tile(j, 2 * P)], xt_bank[j].rearrange("p (c n) -> p c n", c=KC)).then_inc(xt_hi, 1)

        def ln_sqrt(b, k, h):
            act.wait_ge(ln_ag, LN_B * b + NT * k + 4 * h + 4)
            nc.scalar.activation(sd[:, tile(h, 4)], mv[:, tile(h, 4), 1], ACT.Sqrt, bias=eps_col[:]).then_inc(ln_sd, 1)

        def split_wa(it, i):
            if i == 0:
                act.wait_ge(wa_in, 16 * it + 16)
                q = slice(2 * D0, UNITS0 // 2 * D0)
                nc.scalar.mul(Wa_raw[:, :, q], Wa_raw[:, :, q], SCALE0).then_inc(wa_scaled, 1)
                act.wait_ge(wa_scaled, it + 1)
            part = (slice(None), i // 2, tile(i % 2, PROJ0 // 2))
            nc.scalar.copy(Wa_h[part], Wa_raw[part]).then_inc(wa_hi, 1)

        def scale_ba(it):
            act.wait_ge(ba_in, 32 * it + 32)
            nc.scalar.mul(ba[:, 2:6], ba[:, 2:6], SCALE0).then_inc(ba_scaled, 1)
            act.wait_ge(ba_scaled, it + 1)

        def take0(it, u):
            if u < UNITS0:
                act.wait_ge(pj_mm, UNITS_IT * it + u + 1)
                dst = K_h[:, u // 2, tile(u % 2, HALF)] if u < 4 else \
                    Q_h[:, (u - 4) // 4, (u - 4) // 2 % 2, tile(u % 2, HALF)]
                nc.scalar.activation(dst, ring[u % 4], ACT.Identity, bias=ba[:, u // 2:u // 2 + 1]).then_inc(pj_hi, 1)

        def out_root(it, half):
            act.wait_ge(or_var, 2 * it + half + 1)
            nc.scalar.activation(root_cols(orms[:, 1], half), root_cols(orms[:, 0], half), ACT.Sqrt).then_inc(or_act, 1)

        def out_high(it, t, alone=False):
            if t >= 2:
                act.wait_ge(y_mm, NT * it + t - 1)
            act.wait_ge(ot_ps, NT * it + t + 1)
            nc.scalar.copy(OT_h[t % 2][:], out_bank(t, alone).rearrange("p (c n) -> p c n", c=4)).then_inc(ot_hi, 1)

        def attn0_group(b, g, out, last):
            it = b * GROUPS0 + g

            def project_out(s, late):
                for kind, t in out0(s, late) if out else ():
                    if kind == "t":
                        out_high(it - 1, t)

            def high(n):
                w = (n % NT + 1) * P
                act.wait_ge(pt_ps, STEPS0 * it + n + 1)
                if n >= 2:
                    act.wait_ge(pv_done, STEPS0 * it + n - 1)
                nc.scalar.copy(PT_h[n % 2][:, 0:w], ps[2][:, 0:w]).then_inc(pt_hi, 1)

            def squares(n):
                act.wait_ge(o_done, STEPS0 * it + n + 1)
                act.wait_ge(sq_done, STEPS0 * it + n + 1)
                nc.scalar.activation(sq_junk[:].unsqueeze(1), O[:, n % NT, bass.ds(g % 2 * 2 + n // NT, 1), :], ACT.Square,
                                     accum_out=ssq[:, bass.ds(g % 2 * STEPS0 + n, 1)]).then_inc(sq_done, 1)

            for s in range(STEPS0):
                if s >= 2:
                    high(s - 2)
                w = (s % NT + 1) * P
                if s == NT:
                    project_out(s, 0)
                for m, e in ((0, E1[s % 2]), (1, E2[s % 2])):
                    if m == 1 and s != NT:
                        project_out(s, 0)
                    act.wait_ge(nmax_ready[m], STEPS0 * it + s + 1)
                    nc.scalar.activation(e[:, 0:w], ps[m][:, 0:w], ACT.Exp, bias=nmax[:, s % 4, m:m + 1],
                                         accum_out=lsum[:, s % 4, m:m + 1]).then_inc(exp_done[m], 1)
                for t in v_tiles(s):
                    act.wait_ge(pj_dve, UNITS_IT * it + UNITS0 + t + 1)
                    nc.scalar.copy(V_h[:, t, :], O[:, t, bass.ds(g % 2 * 2 + 1, 1), :]).then_inc(v_hi, 1)
                if s >= 4:
                    squares(s - 4)
                project_out(s, 1)
                if s in SPLIT_STEPS:
                    split_wa(it + 1, SPLIT_STEPS.index(s))
                if s == STEPS0 - 1:
                    scale_ba(it + 1)
            for kind, n in tail0(last):
                if kind == "u":
                    take0(it + 1, n)
                elif kind == "t":
                    high(n)
                elif kind == "o":
                    out_high(it, n, True)
                elif kind == "r":
                    if n == 1:
                        squares(STEPS0 - 1)
                    out_root(it, n)
                elif kind == "v":
                    if n == STEPS0 - 2:
                        if out:
                            act.wait_ge(y_mm, NT * it)
                        act.wait_ge(wo_scaled, KC * it + KC)
                        nc.scalar.copy(Wo_h[:], Wo_raw[:]).then_inc(wo_hi, 1)
                    squares(n - 1)
            if last:
                squares(STEPS0 - 1)

        def attn0_out(b):
            it = b * GROUPS0 + GROUPS0 - 1
            for t in range(1, NT):
                out_high(it, t, True)
                if t == 1:
                    out_root(it, 1)
                if t == NT // 2:
                    ffn_split(b, 0, 0)

        def ffn_split(b, c, j):
            cc = b * CHUNKS + c
            act.wait_ge(fw_in[j % 2], b * (CHUNKS * 16) + (c + (2 - j % 2)) * 16)
            nc.scalar.copy(Fw_h[j][:], Fw_raw[j % 2][:]).then_inc(fw_hi, 1)

        def ffn(b, c0, chunks, routed_from):
            def body(q, last, routed=False):
                for j in range(QUAD):
                    c = q * QUAD + (c0 + j)
                    cc = b * CHUNKS + c
                    if not (last and j == QUAD - 1):
                        ffn_split(b, c + 1, (j + 1) % QUAD)
                    act.wait_ge(down_mm, cc + 1)
                    for h in range(2):
                        act.wait_ge(gate_mm, 2 * cc + h + 1)
                        act.wait_ge(gu_used, 2 * cc + h + 1)
                        nc.scalar.activation(silu_g[h][:], ps[2 + h][:, 0:HALF], ACT.Silu).then_inc(silu_done, 1)
                        if routed:
                            act.wait_ge(hm_done, 2 * (b * EXPERTS + (c - (CH_F0 + CH_SHARED))) + h + 1)
                        else:
                            act.wait_ge(gu_used, 2 * cc + h + 3)
                        nc.scalar.copy(H_h[j % 2][:, tile(h, HALF)], Hf[j % 2][:, tile(h, HALF)]).then_inc(h_hi, 1)

            if routed_from is None:
                quads(act, chunks // QUAD, body)
            else:
                with act.Fori(0, (routed_from - c0) // QUAD) as q:
                    body(q, False)
                for q in range((routed_from - c0) // QUAD, chunks // QUAD):
                    body(q, q == chunks // QUAD - 1, True)

        def split_wb(it):
            act.wait_ge(wb_in, 16 * it + 16)
            nc.scalar.copy(Wb_h[:], Wb_raw[:]).then_inc(wb_hi, 1)

        def stack1(kind, p, h, it):
            done = 4 * it + 2 * p + h
            if kind == "uq":
                act.wait_ge(bb_in, 32 * it + 32)
                act.wait_ge(u_mm, 2 * done + 2)
                act.wait_ge(qs_done, done + 1)
                nc.scalar.activation(st_q[:], ps[3][:, 0:HALF], ACT.Identity, bias=bb[:, p:p + 1]).then_inc(uq_full, 1)
                act.wait_ge(uq_full, done + 1)
                nc.scalar.mul(neg_q[:], st_q[:], bsel[:, 0:1]).then_inc(uq_neg, 1)
            elif kind == "zk":
                act.wait_ge(uk_full, done + 1)
                nc.scalar.mul(neg_k[:], st_k[:], bsel[:, 1:2]).then_inc(uk_neg, 1)

        def max_rows(H, j, h):
            rows = slice(j % 2 * SLOT1 + MAX_ROW, j % 2 * SLOT1 + MAX_ROW + 2)
            act.wait_ge(nt_ps, 2 * H + h + 1)
            nc.scalar.copy(QS[rows, j, tile(h, HALF)], ps[3][rows, 0:HALF]).then_inc(n_done, 1)

        def attn1_group(b, g, last):
            it = b * GROUPS1 + g
            for j in range(4):
                H = it * 4 + j
                if j == 1 and not last:
                    act.wait_ge(u_mm, 8 * it + 8)
                    split_wb(it + 1)
                for kind, n in slot1(j, last):
                    if kind == "t":
                        kb, a, z = t_piece(n)
                        if n % 4 == 0:
                            act.wait_ge(pv1_done, 3 * H + n // 4 + 1)
                        act.wait_ge(t_ready, PIECES1 * H + n + 1)
                        nc.scalar.activation(PT[:, n, a - (z - HALF):], ps[1][:, n % 2 * HALF + a - (z - HALF):(n % 2 + 1) * HALF],
                                             ACT.Exp, scale=SCALE1).then_inc(t_used, 1)
                    elif kind == "n":
                        max_rows(H + 1 - n, (j + 1 - n) % 4, n)
                    elif kind in ("uq", "zk"):
                        stack1(kind, 1 if j == 0 else 0, n, it + (0 if j == 0 else 1))
                    elif kind == "c" and n == 0:
                        act.wait_ge(pv1_done, 3 * H + 1 + 3)
                        nc.scalar.copy(OTs[:, 0:HALF], ps[2][:, 0:HALF]).then_inc(ots_done[0], 1)

        def attn1_out(b):
            for j in range(NT // 2):
                act.wait_ge(o1t_ps, 4 * b + j + 1)
                nc.scalar.copy(O1T_h[:, :, tile(j, 2 * P)],
                               xt_bank[j].rearrange("p (c n) -> p c n", c=KC)).then_inc(o1t_hi, 1)

        def router(b):
            act.wait_ge(lg_t, b + 1)
            nc.scalar.activation(ta[:], ps[1][:].rearrange("p (t n) -> p t n", t=NT)[:, :, 0:EXPERTS], ACT.Exp,
                                 scale=-1.0).then_inc(sig_exp, 1)

        for h in range(2):
            x_parts(0, 0, h)
        for i in range(4):
            split_wa(0, i)
        scale_ba(0)
        for q in range(4):
            act.wait_ge(pre_pe, q + 1)
            nc.scalar.mul(w2b[:, tile(q, 2), :], xt_bank[q].rearrange("p (c n) -> p c n", c=2),
                          float((CH_F0 * P) ** -0.5)).then_inc(w2_ready, 1)
        act.wait_ge(pre_dve, 13)
        nc.scalar.activation(lam_exp[:], lam_sum[:], ACT.Exp).then_inc(pre_act, 1)
        with act.Fori(0, B) as b:
            for u in range(UNITS0):
                take0(b * GROUPS0, u)
            attn0_group(b, 0, False, False)
            with act.Fori(1, GROUPS0 - 1) as g:
                attn0_group(b, g, True, False)
            attn0_group(b, GROUPS0 - 1, True, True)
            attn0_out(b)
            for h in range(2):
                ln_sqrt(b, 0, h)
                x_parts(b, 1, h)
            ffn(b, 0, CH_F0, None)
            act.wait_ge(wv_in, 16 * b + 16)
            nc.scalar.copy(Wv_h[:], Wv_raw[:]).then_inc(wv_hi, 1)
            split_wb(b * GROUPS1)
            for h in range(2):
                ln_sqrt(b, 1, h)
                x_parts(b, 2, h)
            for kind, n in FIRST1:
                if kind in ("uq", "zk"):
                    stack1(kind, 0, n, b * GROUPS1)
                elif kind == "n":
                    max_rows(b * HEADS1, 0, n)
            with act.Fori(0, GROUPS1 - 1) as g:
                attn1_group(b, g, False)
            attn1_group(b, GROUPS1 - 1, True)
            act.wait_ge(rw_in, 16 * b + 16)
            nc.scalar.copy(Rw_h[:], Rw_raw[:]).then_inc(rw_hi, 1)
            attn1_out(b)
            ffn_split(b, CH_F0, 0)
            for h in range(2):
                ln_sqrt(b, 2, h)
                x_parts(b, 3, h)
            router(b)
            ffn(b, CH_F0, CH_SHARED + CH_ROUTED, CH_F0 + CH_SHARED)
            for h in range(2):
                ln_sqrt(b, 3, h)
            for h in range(2):
                x_parts(b + 1, 0, h)

    @block.vector
    def _(dve):
        def x_parts(b, k, h):
            for j in (2 * h, 2 * h + 1):
                dve.wait_ge(xt_hi, LN_B // 2 * b + 4 * k + j + 1)
                n = tile(j, 2 * P)
                nc.vector.tensor_tensor(XT_l[:, :, n], xt_bank[j].rearrange("p (c n) -> p c n", c=KC),
                                        XT_h[:, :, n].bitcast(F32), ALU.subtract).then_inc(xt_lo, 1)

        def residual(b, k, t, y):
            nc.vector.tensor_tensor(X[:, t, :], y, X[:, t, :], ALU.add).then_inc(z_done, 1)

        def stats(b, k, t):
            dve.wait_ge(z_done, LN_B * b + NT * k + t + 1)
            nc.vector.bn_stats(st[:, t, :], X[:, t, :]).then_inc(ln_st, 1)

        def moments(b, k, h):
            dve.wait_ge(ln_st, LN_B * b + NT * k + 4 * h + 4)
            dve.nop(nofuse=True)
            for t in range(4 * h, 4 * h + 4):
                nc.vector.bn_aggr(mv[:, t, :], st[:, t, :]).then_inc(ln_ag, 1)

        def layernorm(b, k, h):
            n = 8 * b + 2 * k + h + 1
            dve.wait_ge(ln_sd, n)
            nc.vector.reciprocal(rstd[:, tile(h, 4)], sd[:, tile(h, 4)]).then_inc(ln_rs, 1)
            dve.wait_ge(ln_rs, n)
            for t in range(4 * h, 4 * h + 4):
                nc.vector.tensor_scalar(X[:, t, :], X[:, t, :], mv[:, t, 0:1], rstd[:, t:t + 1], ALU.subtract,
                                        ALU.mult).then_inc(ln_done, 1)

        def add_norm(b, k, wait_tile, y):
            for t in range(NT):
                wait_tile(t)
                residual(b, k, t, y(t))
                if t >= 1:
                    stats(b, k, t - 1)
                if t == 4:
                    moments(b, k, 0)
                if t == 5:
                    layernorm(b, k, 0)
            stats(b, k, NT - 1)
            moments(b, k, 1)
            if k < 3:
                x_parts(b, k + 1, 0)
            layernorm(b, k, 1)

        def take0(it, u):
            h, l = (K_h, K_l) if u < 4 else (Q_h, Q_l)
            at = (slice(None), u // 2) if u < 4 else (slice(None), (u - 4) // 4, (u - 4) // 2 % 2)
            at += (tile(u % 2, HALF),)
            dve.wait_ge(pj_hi, UNITS0 * it + u + 1)
            nc.vector.scalar_tensor_tensor(out=l[at], in0=ring[u % 4], scalar=ba[:, u // 2:u // 2 + 1],
                                           in1=h[at].bitcast(F32), op0=ALU.add,
                                           op1=ALU.subtract).then_inc(pj_dve, 1)

        def out_mean(it, g, half):
            dve.wait_ge(sq_done, STEPS0 * it + (STEPS0 if half else STEPS0 - NT // 2) + 1)
            nc.vector.tensor_scalar(root_cols(orms[:, 0], half), root_cols(ssq[:, bass.ds(g % 2 * STEPS0, STEPS0)], half),
                                    1.0 / E0, EPS, ALU.mult, ALU.add).then_inc(or_var, 1)

        def out_rstd(it, half):
            dve.wait_ge(or_act, 2 * it + half + 1)
            nc.vector.reciprocal(root_cols(orstd[:], half), root_cols(orms[:, 1], half)).then_inc(or_done, 1)
            dve.wait_ge(or_done, 2 * it + half + 1)

        def out_normalise(it, g, t):
            if t >= 2:
                dve.wait_ge(ot_ps, NT * it + t - 1)
            for h in range(2):
                ins = nc.vector.tensor_scalar(On[t % 2][:, h:h + 1, :], O[:, t, bass.ds(g % 2 * 2 + h, 1), :],
                                              orstd[:, h * NT + t:h * NT + t + 1], None, ALU.mult)
            ins.then_inc(on_done, 1)

        def out_low(it, t, alone=False):
            dve.wait_ge(ot_hi, NT * it + t + 1)
            nc.vector.tensor_tensor(OT_l[t % 2][:], out_bank(t, alone).rearrange("p (c n) -> p c n", c=4),
                                    OT_h[t % 2][:].bitcast(F32), ALU.subtract).then_inc(ot_lo, 1)

        def attn0_group(b, g, out, last):
            it = b * GROUPS0 + g

            def project_out(s, late):
                for kind, t in out0(s, late) if out else ():
                    if kind == "t":
                        out_low(it - 1, t)
                        if 1 <= t < NT - 1:
                            out_normalise(it - 1, g + 1, t + 1)
                    else:
                        dve.wait_ge(y_mm, NT * (it - 1) + t + 1)
                        nc.vector.tensor_tensor(X[:, t, :], ring[t % 2 * 2 + 1][:, 0:HID], X[:, t, :],
                                                ALU.add).then_inc(y_added, 1)

            def mix(n):
                dve.wait_ge(exp_done[1], STEPS0 * it + n + 1)
                nc.vector.reciprocal(rsum[:, n % 8, :], lsum[:, n % 4, :]).then_inc(rsum_ready, 1)
                dve.wait_ge(rsum_ready, STEPS0 * it + n + 1)
                nc.vector.scalar_tensor_tensor(out=mixc[:, n % 4:n % 4 + 1], in0=rsum[:, n % 8, 1:2],
                                               scalar=lsum[:, n % 4, 0:1], in1=neglam[:], op0=ALU.mult,
                                               op1=ALU.mult).then_inc(mix_ready, 1)

            def low(n):
                w = (n % NT + 1) * P
                dve.wait_ge(pt_hi, STEPS0 * it + n + 1)
                nc.vector.tensor_tensor(PT_l[n % 2][:, 0:w], ps[2][:, 0:w], PT_h[n % 2][:, 0:w].bitcast(F32),
                                        ALU.subtract).then_inc(pt_lo, 1)

            def output(n):
                dve.wait_ge(pv_done, STEPS0 * it + n + 1)
                nc.vector.tensor_scalar(O[:, n % NT, bass.ds(g % 2 * 2 + n // NT, 1), :],
                                        ps[3][:, 0:E0].unsqueeze(1), rsum[:, n % 8, 0:1], None,
                                        ALU.mult).then_inc(o_done, 1)

            for s in range(STEPS0):
                if s >= 1:
                    mix(s - 1)
                if out and s in (2, 3):
                    if s == 2:
                        dve.wait_ge(xb_done, 2 * b + 1)
                    out_normalise(it - 1, g + 1, s - 2)
                if s >= 2:
                    low(s - 2)
                if s == NT:
                    project_out(s, 0)
                    output(s - 3)
                for m in range(2):
                    dve.wait_ge(s_ready[m], STEPS0 * it + s + 1)
                    nc.vector.tensor_reduce(nmax[:, s % 4, m:m + 1], ps[m][:, 0:(s % NT + 1) * P], AX.X, ALU.max,
                                            negate=True).then_inc(nmax_ready[m], 1)
                for t in v_tiles(s):
                    dve.wait_ge(pj_mm, UNITS_IT * it + UNITS0 + t + 1)
                    nc.vector.tensor_tensor(O[:, t, bass.ds(g % 2 * 2 + 1, 1), :], v_bank(t).unsqueeze(1),
                                            bva[:].unsqueeze(1), ALU.add).then_inc(pj_dve, 1)
                if s != NT:
                    project_out(s, 0)
                    if s >= 3:
                        output(s - 3)
                project_out(s, 1)
            mix(STEPS0 - 1)
            for kind, n in tail0(last):
                if kind == "u":
                    take0(it + 1, n)
                elif kind == "t":
                    low(n)
                elif kind == "o":
                    out_low(it, n, True)
                elif kind == "r":
                    out_mean(it, g, n)
                    out_rstd(it, n)
                elif kind == "v":
                    output(n)

        def attn0_out(b):
            it, g = b * GROUPS0 + GROUPS0 - 1, GROUPS0 - 1

            def next_tile(t):
                if t + 1 < NT:
                    out_low(it, t + 1, True)
                if t == 0:
                    out_mean(it, g, 1)
                if t == 1:
                    out_rstd(it, 1)
                dve.wait_ge(y_mm, NT * it + t + 1)

            add_norm(b, 0, next_tile, lambda t: ring[t % 2 * 2 + 1][:, 0:HID])

        def ffn(b, layer, c0, chunks, routed):
            if not routed:
                if layer == 0:
                    nc.vector.memset(ps[0][:, 0:HALF], 0.0)
                nc.vector.memset(ps[0][:, HALF:], 0.0)
                nc.vector.memset(ps[1][:], 0.0).then_inc(y_zero, 1)
                if layer == 1:
                    dve.wait_ge(ct_ps, b + 1)
                    nc.vector.tensor_copy(combT[:], ps[0][0:NT * EXPERTS, 0:P]).then_inc(ct_copy, 1)
                    dve.wait_ge(ct_copy, b + 1)
                    nc.vector.memset(ps[0][:, 0:HALF], 0.0).then_inc(y_zero, 1)
            with dve.Fori(0, chunks // QUAD) as q:
                for j in range(QUAD):
                    c = q * QUAD + (c0 + j)
                    cc = b * CHUNKS + c
                    for h in range(2):
                        n = tile(h, HALF)
                        dve.wait_ge(h_lo, 2 * cc + h + 1)
                        dve.wait_ge(silu_done, 2 * cc + h + 1)
                        dve.wait_ge(up_mm, 2 * cc + h + 1)
                        nc.vector.tensor_tensor(Hf[j % 2][:, n], ps[2 + h][:, HALF:], silu_g[h][:],
                                                ALU.mult).then_inc(gu_used, 1)
                        if routed:
                            dve.wait_ge(gu_used, 2 * cc + h + 3)
                            dve.wait_ge(comb_in, EXPERTS * 16 * b + EXPERTS * 16)
                            nc.vector.tensor_tensor(Hf[j % 2][:, n], Hf[j % 2][:, n],
                                                    comb_bc[:, bass.ds(q * QUAD + j, 1), tile(h, 4)]
                                                    .rearrange("p e t n -> p (e t n)"), ALU.mult).then_inc(hm_done, 1)

        def ffn_out(b, k, c_end):
            def bank(t):
                if t < 6:
                    dve.wait_ge(y_bank, 3 * CHUNKS * b + 3 * c_end - 2 + t // 2)
                else:
                    dve.wait_ge(down_mm, b * CHUNKS + c_end + 2)

            add_norm(b, k, bank, lambda t: ring[t // 2][:, tile(t % 2, HID)])

        def stack1(kind, p, h, it):
            done, n = 4 * it + 2 * p + h, tile(h, HALF)
            if kind == "uk":
                dve.wait_ge(bb_in, 32 * it + 32)
                dve.wait_ge(u_mm, 2 * done + 1)
                dve.wait_ge(ks_done, done + 1)
                nc.vector.scalar_tensor_tensor(out=st_k[:], in0=ps[3][:, HALF:], scalar=bb[:, 2 + p:3 + p],
                                               in1=alibi[:, p, n], op0=ALU.add, op1=ALU.add).then_inc(uk_full, 1)
            elif kind == "zq":
                dve.wait_ge(uq_neg, done + 1)
                for r in range(2):
                    rows = tile(r, SLOT1)
                    ins = nc.vector.tensor_tensor(QS[rows, 2 * p + r, n], st_q[rows, :], neg_q[rows, :].bitcast(F32), ALU.add)
                ins.then_inc(qs_done, 1)

        def row_max(H, k):
            i, a, z, _ = a_piece(k)
            dst = nmax1[:, i:i + 1] if i < 4 else nmax1_part[:, k % 2, i - 4:i - 3]
            dve.wait_ge(a_ready, PIECES1 * H + k + 1)
            nc.vector.tensor_reduce(dst, ps[0][:, k % 2 * HALF:k % 2 * HALF + z - a], AX.X, ALU.max,
                                    negate=True).then_inc(a_used, 1)
            if k not in (3, PIECES1 - 1):
                return
            h = 0 if k == 3 else 1
            tiles = tile(h, 4)
            dve.wait_ge(a_used, PIECES1 * H + k + 3)
            if h == 1:
                nc.vector.tensor_tensor(nmax1[:, tiles], nmax1_part[:, 0], nmax1_part[:, 1], ALU.min).then_inc(nm_both, 1)
                dve.wait_ge(nm_both, H + 1)
            full = nmax1[:, tiles].unsqueeze(2).to_broadcast([P, 4, 2])
            high, low = (nmax1_cols[:, tiles, MAX_ROW + i::SLOT1] for i in range(2))
            nc.vector.tensor_copy(high, full).then_inc(nm_hi, 1)
            dve.wait_ge(nm_hi, 2 * H + h + 1)
            nc.vector.tensor_tensor(low, full, high.bitcast(F32), ALU.subtract).then_inc(nm_lo, 1)

        def attn1_group(b, g, last):
            it = b * GROUPS1 + g

            def output(H, j, h):
                dve.wait_ge(o_ps, 2 * H + h + 1)
                if h == 0:
                    dve.wait_ge(o1_done, H + 1)
                nc.vector.tensor_reduce(osum[:, tile(h, 4), 0:D1 + 1],
                                        ps[3][:, HALF:].rearrange("p (t c e) -> p t e c", t=4, c=4)[:, :, 0:D1 + 1, :],
                                        AX.X, ALU.add).then_inc(o_used, 1)
                if h == 1:
                    dve.wait_ge(o_used, 2 * H + 3)
                    nc.vector.reciprocal(rsum1[:], osum[:, :, D1]).then_inc(rs1_done, 1)
                    dve.wait_ge(rs1_done, H + 1)
                    nc.vector.tensor_tensor(O1[:, :, bass.ds(g * 4 * D1 + j * D1, D1)], osum[:, :, 0:D1],
                                            rsum1[:].unsqueeze(2).to_broadcast([P, NT, D1]), ALU.mult).then_inc(o1_done, 1)

            for j in range(4):
                H = it * 4 + j
                for kind, n in slot1(j, last):
                    if kind == "a":
                        row_max(H + 1, n)
                    elif kind in ("uk", "zq"):
                        stack1(kind, 1 if j == 0 else 0, n, it + (0 if j == 0 else 1))
                    elif kind == "c" and n == 1:
                        dve.wait_ge(pv1_done, 3 * H + 3 + 3)
                        nc.vector.tensor_copy(OTs[:, HALF:], ps[2][:, HALF:]).then_inc(ots_done[1], 1)
                    elif kind == "o":
                        output(H - 1, j - 1, n)
                    elif kind == "end":
                        for h in range(2):
                            output(H, j, h)

        def attn1_out(b):
            for j in range(NT // 2):
                dve.wait_ge(o1t_hi, 4 * b + j + 1)
                n = tile(j, 2 * P)
                nc.vector.tensor_tensor(O1T_l[:, :, n], xt_bank[j].rearrange("p (c n) -> p c n", c=KC),
                                        O1T_h[:, :, n].bitcast(F32), ALU.subtract).then_inc(o1t_lo, 1)
            dve.wait_ge(xb_done, 2 * b + 2)
            add_norm(b, 2, lambda t: dve.wait_ge(y1_mm, NT * b + t // 2 * 2 + 2),
                     lambda t: ring[t // 2][:, tile(t % 2, HID)])

        def router(b):
            for h in range(2):
                dve.wait_ge(lg_mm, 2 * b + h + 1)
                nc.vector.tensor_copy(LG[:, tile(h, HALF)], ps[0][:, tile(h, HALF)]).then_inc(lg_copy, 1)
            dve.wait_ge(sig_exp, b + 1)
            done = [0]

            def then(ins):
                done[0] += 1
                ins.then_inc(rt_dve, 1)
                dve.wait_ge(rt_dve, R_B * b + done[0])

            def over_e(a):
                return a[:].unsqueeze(2).to_broadcast([P, NT, EXPERTS])

            def over_t(a):
                return a[:].unsqueeze(1).to_broadcast([P, NT, EXPERTS])

            def pick_first_best(vals, tmp, dst):
                then(nc.vector.tensor_reduce(tm[:], vals, AX.X, ALU.max))
                then(nc.vector.tensor_tensor(tmp, vals, over_e(tm), ALU.is_equal))
                then(nc.vector.tensor_tensor(tmp, tmp, over_t(first), ALU.mult))
                then(nc.vector.tensor_reduce(tm[:], tmp, AX.X, ALU.max))
                then(nc.vector.tensor_tensor(dst, tmp, over_e(tm), ALU.is_equal))

            then(nc.vector.tensor_scalar(ta[:], ta[:], 1.0, None, ALU.add))
            then(nc.vector.reciprocal(sc[:], ta[:]))
            then(nc.vector.tensor_tensor(sel[:], sc[:], over_t(rbias), ALU.add))
            pick_first_best(sel[:], ta[:], oh)
            then(nc.vector.scalar_tensor_tensor(out=sel[:], in0=oh, scalar=-1e30, in1=sel[:], op0=ALU.mult,
                                                op1=ALU.add))
            pick_first_best(sel[:], ta[:], tb[:])
            then(nc.vector.tensor_tensor(oh, oh, tb[:], ALU.add))
            then(nc.vector.tensor_tensor(sc[:], sc[:], oh, ALU.mult))
            then(nc.vector.tensor_reduce(tm[:], sc[:], AX.X, ALU.add))
            then(nc.vector.tensor_scalar(tm[:], tm[:], 1e-9, None, ALU.add))
            then(nc.vector.reciprocal(tm[:], tm[:]))
            then(nc.vector.tensor_tensor(comb, sc[:], over_e(tm), ALU.mult))
            assert done[0] == R_B

        dve.wait_ge(w2_in, 32)
        src, dst = w2a, w2b
        for n, h in enumerate((1, 2, 4)):
            v, o = (a[:].rearrange("p (g r h) n -> p g r (h n)", r=2, h=h) for a in (src, dst))
            nc.vector.tensor_tensor(o[:, :, 0], v[:, :, 0], v[:, :, 1], ALU.add).then_inc(pre_dve, 1)
            nc.vector.tensor_tensor(o[:, :, 1], v[:, :, 0], v[:, :, 1], ALU.subtract).then_inc(pre_dve, 1)
            dve.wait_ge(pre_dve, 2 + 2 * n)
            src, dst = dst, src
            if n == 2:
                for h2 in range(2):
                    x_parts(0, 0, h2)
        nc.vector.tensor_copy(hada[:], hada_raw[:]).then_inc(pre_dve, 1)
        nc.vector.tensor_copy(w2_h[:], src[:]).then_inc(pre_hi, 1)
        dve.wait_ge(pre_hi, 1)
        nc.vector.tensor_tensor(w2_l[:], src[:], w2_h[:].bitcast(F32), ALU.subtract).then_inc(pre_dve, 1)
        dve.wait_ge(const_in, CONSTS * 16)
        nc.vector.memset(eps_col[:], EPS).then_inc(pre_dve, 1)
        nc.vector.tensor_copy(ident_bf[:], ident[:]).then_inc(pre_dve, 1)
        nc.vector.tensor_copy(mask_bf[:], mask_raw[:]).then_inc(pre_dve, 1)
        for k in range(2):
            nc.vector.tensor_tensor_reduce(out=lam_prod[:, k, :], in0=lam_in[:, 2 * k, :], in1=lam_in[:, 2 * k + 1, :],
                                           scale=1.0, scalar=0.0, op0=ALU.mult, op1=ALU.add,
                                           accum_out=lam_sum[:, k:k + 1]).then_inc(pre_dve, 1)
        nc.vector.tensor_scalar(subln[:], subln[:], 1.0 - LAMBDA_INIT, None, ALU.mult)
        dve.wait_ge(pre_act, 1)
        nc.vector.scalar_tensor_tensor(out=neglam[:], in0=lam_exp[:, 1:2], scalar=-LAMBDA_INIT, in1=lam_exp[:, 0:1],
                                       op0=ALU.add, op1=ALU.subtract).then_inc(pre_dve, 1)
        dve.wait_ge(pre_dve, 14)
        with dve.Fori(0, B) as b:
            for u in range(UNITS0):
                take0(b * GROUPS0, u)
            dve.wait_ge(w2_out, 16)
            attn0_group(b, 0, False, False)
            with dve.Fori(1, GROUPS0 - 1) as g:
                attn0_group(b, g, True, False)
            attn0_group(b, GROUPS0 - 1, True, True)
            attn0_out(b)
            x_parts(b, 1, 1)
            ffn(b, 0, 0, CH_F0, False)
            ffn_out(b, 1, CH_F0)
            x_parts(b, 2, 1)
            dve.wait_ge(qs_zero, 6 * b + 6)
            for kind, n in FIRST1:
                if kind in ("uk", "zq"):
                    stack1(kind, 0, n, b * GROUPS1)
                elif kind == "V":
                    dve.wait_ge(v1_mm, NT * b + n + 1)
                    nc.vector.tensor_tensor(V1[:, n, :], ring[2 + n % 2][:, 0:HID], rows_bc[:, 2, :],
                                            ALU.add).then_inc(v1_done, 1)
                    if n == 0:
                        nc.vector.memset(ps[2][:, 0:HALF], 0.0).then_inc(o_zero, 1)
                elif kind == "a":
                    row_max(b * HEADS1, n)
            with dve.Fori(0, GROUPS1 - 1) as g:
                attn1_group(b, g, False)
            attn1_group(b, GROUPS1 - 1, True)
            attn1_out(b)
            x_parts(b, 3, 1)
            router(b)
            ffn(b, 1, CH_F0, CH_SHARED, False)
            ffn(b, 1, CH_F0 + CH_SHARED, CH_ROUTED, True)
            ffn_out(b, 3, CHUNKS)
            for h in range(2):
                x_parts(b + 1, 0, h)

    @block.gpsimd
    def _(pool):
        def low(dst, full, high):
            return nc.gpsimd.tensor_tensor(dst, full, high.bitcast(F32), ALU.subtract)

        def split_wa(it, i):
            pool.wait_ge(wa_hi, 4 * it + i + 1)
            part = (slice(None), i // 2, tile(i % 2, PROJ0 // 2))
            low(Wa_l[part], Wa_raw[part], Wa_h[part]).then_inc(wa_lo, 1)

        def attn0_group(b, g, last):
            it = b * GROUPS0 + g
            for n in range(STEPS0):
                w = (n % NT + 1) * P
                e1, e2 = E1[n % 2][:, 0:w], E2[n % 2][:, 0:w]
                pool.wait_ge(mix_ready, STEPS0 * it + n + 1)
                pool.nop(nofuse=True)
                nc.gpsimd.tensor_scalar(e2, e2, mixc[:, n % 4:n % 4 + 1], 1.0, ALU.mult,
                                        ALU.mult).then_inc(mix_scaled, 1)
                pool.wait_ge(mix_scaled, STEPS0 * it + n + 1)
                nc.gpsimd.tensor_tensor(e1, e1, e2, ALU.add).then_inc(p_ready, 1)
                for t in v_tiles(n):
                    pool.wait_ge(v_hi, NT * it + t + 1)
                    low(V_l[:, t, :].unsqueeze(1), O[:, t, bass.ds(g % 2 * 2 + 1, 1), :],
                        V_h[:, t, :].unsqueeze(1)).then_inc(v_lo, 1)
                if n in SPLIT_STEPS:
                    split_wa(it + 1, SPLIT_STEPS.index(n))
            pool.wait_ge(wo_in, 16 * it + 16)
            pool.nop(nofuse=True)
            for c in range(KC):
                w = Wo_raw[:].rearrange("p (h c) n -> p c h n", c=KC)[:, c]
                nc.gpsimd.tensor_scalar(w, w, subln[:, c:c + 1], 1.0, ALU.mult, ALU.mult).then_inc(wo_scaled, 1)
            if last:
                for t in range(2):
                    out_normalise(b, t)
            pool.wait_ge(wo_hi, it + 1)
            low(Wo_l[:], Wo_raw[:], Wo_h[:]).then_inc(wo_lo, 1)

        def ffn_split(b, c, j):
            pool.wait_ge(fw_hi, b * CHUNKS + c + 1)
            low(Fw_l[j][:], Fw_raw[j % 2][:], Fw_h[j][:]).then_inc(fw_lo, 1)

        def out_normalise(b, t):
            it, g = b * GROUPS0 + GROUPS0 - 1, GROUPS0 - 1
            if t % (NT // 2) == 0:
                pool.wait_ge(or_done, 2 * it + t // (NT // 2) + 1)
                pool.nop(nofuse=True)
            if t >= 2:
                pool.wait_ge(ot_ps, NT * it + t - 1)
                pool.nop(nofuse=True)
            for h in range(2):
                ins = nc.gpsimd.tensor_scalar(On[t % 2][:, h, :], O[:, t, g % 2 * 2 + h, :],
                                              orstd[:, h * NT + t:h * NT + t + 1], 1.0, ALU.mult, ALU.mult)
            ins.then_inc(on_done, 1)

        def attn0_out(b):
            for t in range(2, NT):
                out_normalise(b, t)
            ffn_split(b, 0, 0)

        def add_bias(src, row):
            nc.gpsimd.tensor_tensor(X[:], src[:], rows_bc[:, row, :].unsqueeze(1).to_broadcast([P, NT, HID]),
                                    ALU.add).then_inc(xb_done, 1)

        def ffn(b, c0, chunks):
            def body(q, last):
                for j in range(QUAD):
                    c = q * QUAD + (c0 + j)
                    if not (last and j == QUAD - 1):
                        ffn_split(b, c + 1, (j + 1) % QUAD)
                    for h in range(2):
                        n = tile(h, HALF)
                        pool.wait_ge(h_hi, 2 * (b * CHUNKS + c) + h + 1)
                        low(H_l[j % 2][:, n], Hf[j % 2][:, n], H_h[j % 2][:, n]).then_inc(h_lo, 1)
                    if c0 == 0 and c < len(fills):
                        nc.gpsimd.memset(*fills[c]).then_inc(qs_zero, 1)

            fills = [(QS[:, j].bitcast(F32), 0.0) for j in range(4)] + [(nmax1_cols[:].bitcast(F32), 0.0), (Vs[:], 1.0)]
            quads(pool, chunks // QUAD, body)

        def split_wb(it):
            pool.wait_ge(wb_hi, it + 1)
            low(Wb_l[:], Wb_raw[:], Wb_h[:]).then_inc(wb_lo, 1)

        def stack1(p, h, it):
            pool.wait_ge(uk_neg, 4 * it + 2 * p + h + 1)
            nc.gpsimd.tensor_tensor(KS[:, p, tile(h, HALF)], st_k[:], neg_k[:].bitcast(F32), ALU.add).then_inc(ks_done, 1)

        def head_values(j, col):
            pool.nop(nofuse=True)
            nc.gpsimd.tensor_copy(Vs[:, :, j, 0:D1], V1[:, :, bass.ds(col, D1)]).then_inc(vs_done, 1)

        def attn1_group(b, g):
            it = b * GROUPS1 + g
            for j in range(4):
                if j == 1:
                    split_wb(it + 1)
                for kind, n in slot1(j, False):
                    if kind == "zk":
                        stack1(1 if j == 0 else 0, n, it + (0 if j == 0 else 1))
                pool.wait_ge(pv1_done, 3 * (it * 4 + j) + 3 + 3)
                head_values(j, (g + 1) * 4 * D1 + j * D1)

        pool.sem_inc(fw_lo, 2)
        pool.sem_inc(h_lo, 4)
        pool.sem_inc(gu_used, 2)
        pool.sem_inc(down_mm, 2)
        for free in (a_used, t_used):
            pool.sem_inc(free, 2)
        pool.sem_inc(pv1_done, 3)
        for free in (ks_done, qs_done, *ots_done, o1_done, o_used):
            pool.sem_inc(free, 1)
        pool.sem_inc(out_done, 1)
        for free in (sq_done, wo_lo):
            pool.sem_inc(free, 1)
        for i in range(4):
            split_wa(0, i)
        with pool.Fori(0, B) as b:
            pool.wait_ge(const_in, CONSTS * 16)
            pool.wait_ge(x_in, 16 * b + 16)
            pool.wait_ge(out_done, 16 * STORES * b + 1)
            add_bias(Xn, 0)
            with pool.Fori(0, GROUPS0 - 1) as g:
                attn0_group(b, g, False)
            attn0_group(b, GROUPS0 - 1, True)
            attn0_out(b)
            ffn(b, 0, CH_F0)
            pool.wait_ge(wv_hi, b + 1)
            low(Wv_l[:], Wv_raw[:], Wv_h[:]).then_inc(wv_lo, 1)
            split_wb(b * GROUPS1)
            for h in range(2):
                stack1(0, h, b * GROUPS1)
            pool.wait_ge(qs_zero, 6 * b + 6)
            pool.wait_ge(v1_done, NT * b + NT)
            for j in range(4):
                head_values(j, j * D1)
            with pool.Fori(0, GROUPS1 - 1) as g:
                attn1_group(b, g)
            for h in range(2):
                stack1(1, h, b * GROUPS1 + (GROUPS1 - 1))
            pool.wait_ge(xt_ps, LN_B // 2 * b + 12)
            add_bias(X, 1)
            ffn_split(b, CH_F0, 0)
            pool.wait_ge(rw_in, 16 * b + 16)
            pool.wait_ge(rw_hi, b + 1)
            low(Rw_l[:], Rw_raw[:], Rw_h[:]).then_inc(rw_lo, 1)
            ffn(b, CH_F0, CH_SHARED + CH_ROUTED)


def kernel(**inputs):
    import concourse.bacc as bacc
    from concourse.bass_utils import run_bass_kernel_spmd

    f32 = np.float32
    a = {k: np.asarray(v) for k, v in inputs.items()}

    def rows(w):
        return w.T.reshape(-1, P, w.shape[0]).transpose(1, 0, 2)

    w, bias = a["L0_attn_Wqkv_w"], a["L0_attn_Wqkv_b"]
    nq, nk = 2 * HEADS0 * D0, 2 * GROUPS0 * D0
    wa, ba, bva = [], [], []
    for g in [*range(GROUPS0), 0]:
        k, v = slice(nq + g * E0, nq + (g + 1) * E0), slice(nq + nk + g * E0, nq + nk + (g + 1) * E0)
        q = slice(g * 2 * E0, (g + 1) * 2 * E0)
        wa.append(rows(np.concatenate([w[k], w[q], w[v]])))
        ba.append(np.concatenate([bias[k], bias[q]]).reshape(6, P).T)
        bva.append(bias[v])

    wb, bb = [], []
    low_q, low_k = slice(D1, 2 * D1), slice(SLOT1 - D1, SLOT1)
    max_rows, alibi_rows = slice(MAX_ROW, MAX_ROW + 2), slice(MAX_ROW + 2, MAX_ROW + 4)
    for g in range(GROUPS1):
        cols, bcols = np.zeros((HID, 4 * P), f32), np.zeros((4 * P,), f32)
        for s, (wn, bn) in enumerate((("L1_attn_Wq", "L1_attn_bq"), ("L1_attn_Wk", "L1_attn_bk"))):
            for j in range(4):
                src = slice((4 * g + j) * D1, (4 * g + j + 1) * D1)
                at = s * 2 * P + j * SLOT1
                for r in (0, D1, low_k.start):
                    cols[:, at + r:at + r + D1] = a[wn][:, src]
                    bcols[at + r:at + r + D1] = a[bn][src]
                ones = (alibi_rows, max_rows)[s]
                bcols[at + ones.start:at + ones.stop] = 1.0
        wb.append(cols.reshape(KC, P, 4 * P).transpose(1, 0, 2))
        bb.append(bcols.reshape(4, P).T)
    bsel = np.zeros((P, 2), f32)
    slopes_start = 2.0 ** (-2.0 ** -(np.log2(HEADS1) - 3))
    slopes = np.array([slopes_start * slopes_start ** i for i in range(HEADS1)], f32)
    ramp = -slopes[:, None] * (T - 1 - np.arange(T, dtype=f32))[None, :] / f32(SCALE1)
    alibi = np.zeros((GROUPS1, P, 2, T), f32)
    for j in range(2):
        at = j * SLOT1
        bsel[at + low_q.start:at + low_q.stop, 0] = -1.0
        bsel[at + low_k.start:at + low_k.stop, 1] = -1.0
        bsel[at + alibi_rows.start + 1, 1] = -1.0
        for g in range(GROUPS1):
            for p in range(2):
                alibi[g, at + alibi_rows.start:at + alibi_rows.stop, p, :] = ramp[4 * g + 2 * p + j]

    def chunks(gate, up):
        return [np.concatenate([rows(g).reshape(P, -1), rows(u).reshape(P, -1)], axis=1)
                for g, u in zip(gate.reshape(-1, P, HID), up.reshape(-1, P, HID))]

    w12 = a["L1_ffn_w12"]
    fa = chunks(a["L0_ffn_W1"], a["L0_ffn_W3"]) + chunks(a["L1_ffn_sw1"], a["L1_ffn_sw2"]) \
        + chunks(w12[:, :P].reshape(-1, HID), w12[:, P:].reshape(-1, HID))
    fb = np.concatenate([a["L1_ffn_sw3"].T.reshape(-1, P, HID), a["L1_ffn_w3"].transpose(0, 2, 1)])
    rw = np.zeros((P, KC, P), f32)
    rw[:, :, 0:EXPERTS] = rows(a["L1_ffn_router_w"])
    hada = np.ones((1, 1), f32)
    while hada.shape[0] < P:
        hada = np.block([[hada, hada], [hada, -hada]])

    arrays = {
        "x": a["L0_attn_hidden_states"],
        "wa": np.stack(wa), "ba": np.stack(ba), "bva": np.stack(bva),
        "lam": np.stack([a[f"L0_attn_lambda_{n}"] for n in ("q1", "k1", "q2", "k2")]),
        "subln": a["L0_attn_subln_w"].reshape(KC, P).T,
        "wo0": rows(a["L0_attn_out_w"]).reshape(P, GROUPS0, 4, HID).transpose(1, 0, 2, 3),
        "rows": np.stack([a["L0_attn_out_b"], a["L1_attn_bo"], a["L1_attn_bv"]]),
        "w2": rows(a["L0_ffn_W2"]),
        "fa": np.stack(fa), "fb": fb, "rw": rw, "rbias": a["L1_ffn_expert_bias"],
        "wb": np.stack(wb), "bb": np.stack(bb), "bsel": bsel, "alibi": alibi,
        "wvo": np.stack([a[n].reshape(KC, P, HID).transpose(1, 0, 2) for n in ("L1_attn_Wv", "L1_attn_Wo")], axis=1),
        "ident": np.eye(P, dtype=f32),
        "mask": np.triu(np.full((P, P), -1e30, f32), 1),
        "hada": hada.astype(f32),
        "first": np.arange(EXPERTS, 0, -1).astype(f32),
    }
    arrays = {f"in_{k}": np.ascontiguousarray(v) for k, v in arrays.items()}
    nc = bacc.Bacc("TRN2", target_bir_lowering=False, num_devices=1)
    d = {k[3:]: nc.dram_tensor(k, v.shape, F32, kind="ExternalInput").ap() for k, v in arrays.items()}
    d["out"] = nc.dram_tensor("out", (B, T, HID), F32, kind="ExternalOutput").ap()
    d["w2s"] = nc.dram_tensor("w2s", (CH_F0, P, HID), F32, kind="Internal").ap()
    d["combs"] = nc.dram_tensor("combs", (NT * EXPERTS, P), F32, kind="Internal").ap()
    build(nc, d)
    r = run_bass_kernel_spmd(nc, [arrays], core_ids=[0])
    return r.results[0]["out"]
```
